# Optimizing a Trainium2 kernel written in Bass

```python
import numpy as np
import jax
import jax.numpy as jnp

def _softmax(x, axis=-1):
    return jax.nn.softmax(x, axis=axis)
def _gelu(x):
    return jax.nn.gelu(x, approximate=True)
def _silu(x):
    return jax.nn.silu(x)
def _sigmoid(x):
    return jax.nn.sigmoid(x)
def _layernorm(x, axis=-1, eps=1e-5):
    m = jnp.mean(x, axis=axis, keepdims=True)
    v = jnp.var(x, axis=axis, keepdims=True)
    return (x - m) / jnp.sqrt(v + eps)
def _scatter_add(tgt, idx, src, axis=0):
    return tgt.at[idx].add(src)
def _segment_sum(src, seg, n):
    return jax.ops.segment_sum(src, seg, n)

kernel_name = 'mk_conv_seq_d4_conv_nhwc128_f08b39'

def setup_inputs(seed: int = 0):
    np.random.seed(seed)
    _w = jnp.asarray
    def _rec_inputs():
        import jax
        import jax.numpy as jnp
        _gk = jax.random.key(seed)
        x = -0.0005207 + 1.001 * jax.random.normal(jax.random.fold_in(_gk, 1), (4, 64, 64, 128), jnp.float32)
        return x
    x = _rec_inputs()
    def _L0_conv_setup():
        import jax, jax.numpy as jnp
        import numpy as np
        NUM_HEAD = 8

        def conv_same(x, w, b):
            return jax.lax.conv_general_dilated(x, w, window_strides=(1, 1), padding='SAME', dimension_numbers=('NHWC', 'HWIO', 'NHWC')) + b

        def _gated_resnet(x, W1, b1, W2, b2, Wq, bq, Wk, bk, Wv, bv, W3, b3):
            B, H, W, C = x.shape
            c1 = conv_same(jax.nn.elu(x), W1, b1)
            c2 = conv_same(c1, W2, b2)
            a, b = jnp.split(c2, 2, axis=-1)
            c3 = a * jax.nn.sigmoid(b)
            N = H * W
            f = c3.reshape(B, N, C)
            q = f @ Wq + bq
            k = f @ Wk + bk
            v = f @ Wv + bv
            scale = jnp.float32(np.sqrt(C // 8))
            dot = jnp.einsum('bnd,bmd->bnm', q, k) / scale
            mask = jnp.tril(jnp.ones((N, N), jnp.float32), -1)
            dot = dot - (1.0 - mask) * 10000000000.0
            dot = dot - jnp.max(dot, axis=-1, keepdims=True)
            e = jnp.exp(dot) * mask
            probs = e / (jnp.sum(e, axis=-1, keepdims=True) + 1e-10)
            atten = jnp.einsum('bnm,bmd->bnd', probs, v)
            multihead = jnp.tile(atten, (1, 1, NUM_HEAD)).reshape(B, H, W, -1)
            mh = multihead @ W3 + b3
            c3 = c3 + mh.reshape(B, H, W, C)
            return x + c3
        key = jax.random.key(seed)
        ks = jax.random.split(key, 8)
        B, H, W, C = (4, 64, 64, 128)
        DQK, DV = (4, 16)
        s = 0.02
        return {'x': jax.random.normal(ks[0], (B, H, W, C), dtype=jnp.float32), 'W1': jax.random.normal(ks[1], (3, 3, C, C), dtype=jnp.float32) * s, 'b1': jnp.zeros((C,), jnp.float32), 'W2': jax.random.normal(ks[2], (3, 3, C, 2 * C), dtype=jnp.float32) * s, 'b2': jnp.zeros((2 * C,), jnp.float32), 'Wq': jax.random.normal(ks[3], (C, DQK), dtype=jnp.float32) * s, 'bq': jnp.zeros((DQK,), jnp.float32), 'Wk': jax.random.normal(ks[4], (C, DQK), dtype=jnp.float32) * s, 'bk': jnp.zeros((DQK,), jnp.float32), 'Wv': jax.random.normal(ks[5], (C, DV), dtype=jnp.float32) * s, 'bv': jnp.zeros((DV,), jnp.float32), 'W3': jax.random.normal(ks[6], (NUM_HEAD * DV, C), dtype=jnp.float32) * s, 'b3': jnp.zeros((C,), jnp.float32)}
    _L0_conv_all = _L0_conv_setup()
    _L0_conv_in = {k: v for k, v in _L0_conv_all.items() if k in ('W1', 'b1', 'W2', 'b2', 'Wq', 'bq', 'Wk', 'bk', 'Wv', 'bv', 'W3', 'b3', )}
    del _L0_conv_all

    def _L1_conv_setup():
        import jax, jax.numpy as jnp
        import numpy as np
        R = 2
        key = jax.random.key(seed)
        k1, k2 = jax.random.split(key)
        x = jax.random.normal(k1, (4, 32, 128, 128), dtype=jnp.float32)
        gamma = jax.random.normal(k2, (1,), dtype=jnp.float32)
        return {'x': x, 'gamma': gamma}
    _L1_conv_all = _L1_conv_setup()
    _L1_conv_in = {k: v for k, v in _L1_conv_all.items() if k in ('gamma', )}
    del _L1_conv_all

    def _L2_conv_setup():
        import jax, jax.numpy as jnp
        import numpy as np
        LN_EPS = 1e-05

        def _layer_norm(x, scale, bias):
            mu = jnp.mean(x, axis=-1, keepdims=True)
            var = jnp.mean(jnp.square(x - mu), axis=-1, keepdims=True)
            return (x - mu) * jax.lax.rsqrt(var + LN_EPS) * scale + bias
        key = jax.random.key(seed)
        ks = jax.random.split(key, 8)
        B, N, C, H = (1, 384, 128, 128)
        s_in = 1.0 / np.sqrt(C)
        s_h = 1.0 / np.sqrt(H)
        return {'pair': jax.random.normal(ks[0], (B, N, N, C), jnp.float32), 'W_left': jax.random.normal(ks[1], (C, H), jnp.float32) * s_in, 'b_left': jnp.zeros((H,), jnp.float32), 'W_right': jax.random.normal(ks[2], (C, H), jnp.float32) * s_in, 'b_right': jnp.zeros((H,), jnp.float32), 'W_gate': jax.random.normal(ks[3], (C, H), jnp.float32) * s_in, 'b_gate': jnp.zeros((H,), jnp.float32), 'W_eq': jax.random.normal(ks[4], (C, H), jnp.float32) * s_in, 'b_eq': jnp.zeros((H,), jnp.float32), 'W_out': jax.random.normal(ks[5], (H, C), jnp.float32) * s_h, 'b_out': jnp.zeros((C,), jnp.float32), 'ln_scale': jnp.ones((C,), jnp.float32), 'ln_bias': jnp.zeros((C,), jnp.float32)}
    _L2_conv_all = _L2_conv_setup()
    _L2_conv_in = {k: v for k, v in _L2_conv_all.items() if k in ('W_left', 'b_left', 'W_right', 'b_right', 'W_gate', 'b_gate', 'W_eq', 'b_eq', 'W_out', 'b_out', 'ln_scale', 'ln_bias', )}
    del _L2_conv_all

    def _L3_conv_setup():
        import jax, jax.numpy as jnp
        import numpy as np
        R = 2
        key = jax.random.key(seed)
        k1, k2 = jax.random.split(key)
        x = jax.random.normal(k1, (4, 32, 128, 128), dtype=jnp.float32)
        gamma = jax.random.normal(k2, (1,), dtype=jnp.float32)
        return {'x': x, 'gamma': gamma}
    _L3_conv_all = _L3_conv_setup()
    _L3_conv_in = {k: v for k, v in _L3_conv_all.items() if k in ('gamma', )}
    del _L3_conv_all

    return {
        "x": x,
        "L0_conv_W1": _L0_conv_in["W1"],
        "L0_conv_b1": _L0_conv_in["b1"],
        "L0_conv_W2": _L0_conv_in["W2"],
        "L0_conv_b2": _L0_conv_in["b2"],
        "L0_conv_Wq": _L0_conv_in["Wq"],
        "L0_conv_bq": _L0_conv_in["bq"],
        "L0_conv_Wk": _L0_conv_in["Wk"],
        "L0_conv_bk": _L0_conv_in["bk"],
        "L0_conv_Wv": _L0_conv_in["Wv"],
        "L0_conv_bv": _L0_conv_in["bv"],
        "L0_conv_W3": _L0_conv_in["W3"],
        "L0_conv_b3": _L0_conv_in["b3"],
        "L1_conv_gamma": _L1_conv_in["gamma"],
        "L2_conv_W_left": _L2_conv_in["W_left"],
        "L2_conv_b_left": _L2_conv_in["b_left"],
        "L2_conv_W_right": _L2_conv_in["W_right"],
        "L2_conv_b_right": _L2_conv_in["b_right"],
        "L2_conv_W_gate": _L2_conv_in["W_gate"],
        "L2_conv_b_gate": _L2_conv_in["b_gate"],
        "L2_conv_W_eq": _L2_conv_in["W_eq"],
        "L2_conv_b_eq": _L2_conv_in["b_eq"],
        "L2_conv_W_out": _L2_conv_in["W_out"],
        "L2_conv_b_out": _L2_conv_in["b_out"],
        "L2_conv_ln_scale": _L2_conv_in["ln_scale"],
        "L2_conv_ln_bias": _L2_conv_in["ln_bias"],
        "L3_conv_gamma": _L3_conv_in["gamma"],
    }

def reference(x, L0_conv_W1, L0_conv_b1, L0_conv_W2, L0_conv_b2, L0_conv_Wq, L0_conv_bq, L0_conv_Wk, L0_conv_bk, L0_conv_Wv, L0_conv_bv, L0_conv_W3, L0_conv_b3, L1_conv_gamma, L2_conv_W_left, L2_conv_b_left, L2_conv_W_right, L2_conv_b_right, L2_conv_W_gate, L2_conv_b_gate, L2_conv_W_eq, L2_conv_b_eq, L2_conv_W_out, L2_conv_b_out, L2_conv_ln_scale, L2_conv_ln_bias, L3_conv_gamma):
    import jax
    import jax.numpy as jnp
    def _L0_conv_ref(x, W1, b1, W2, b2, Wq, bq, Wk, bk, Wv, bv, W3, b3):
        import jax, jax.numpy as jnp
        import numpy as np
        NUM_HEAD = 8

        def conv_same(x, w, b):
            return jax.lax.conv_general_dilated(x, w, window_strides=(1, 1), padding='SAME', dimension_numbers=('NHWC', 'HWIO', 'NHWC')) + b

        def _gated_resnet(x, W1, b1, W2, b2, Wq, bq, Wk, bk, Wv, bv, W3, b3):
            B, H, W, C = x.shape
            c1 = conv_same(jax.nn.elu(x), W1, b1)
            c2 = conv_same(c1, W2, b2)
            a, b = jnp.split(c2, 2, axis=-1)
            c3 = a * jax.nn.sigmoid(b)
            N = H * W
            f = c3.reshape(B, N, C)
            q = f @ Wq + bq
            k = f @ Wk + bk
            v = f @ Wv + bv
            scale = jnp.float32(np.sqrt(C // 8))
            dot = jnp.einsum('bnd,bmd->bnm', q, k) / scale
            mask = jnp.tril(jnp.ones((N, N), jnp.float32), -1)
            dot = dot - (1.0 - mask) * 10000000000.0
            dot = dot - jnp.max(dot, axis=-1, keepdims=True)
            e = jnp.exp(dot) * mask
            probs = e / (jnp.sum(e, axis=-1, keepdims=True) + 1e-10)
            atten = jnp.einsum('bnm,bmd->bnd', probs, v)
            multihead = jnp.tile(atten, (1, 1, NUM_HEAD)).reshape(B, H, W, -1)
            mh = multihead @ W3 + b3
            c3 = c3 + mh.reshape(B, H, W, C)
            return x + c3
        return _gated_resnet(x, W1, b1, W2, b2, Wq, bq, Wk, bk, Wv, bv, W3, b3)

    def _L1_conv_ref(x, gamma):
        import jax, jax.numpy as jnp
        import numpy as np
        R = 2
        B, C, H, W = x.shape
        h, w = (H // R, W // R)
        xs = x.reshape(B, C, h, R, w, R).transpose(0, 1, 3, 5, 2, 4).reshape(B, C * R * R, h, w)
        hw = h * w
        q = xs.reshape(B, C * R * R, hw)
        energy = jnp.einsum('bci,bcj->bij', q, q)
        d = jnp.sqrt(jnp.diagonal(energy, axis1=1, axis2=2))
        energy = energy / (d[:, :, None] * d[:, None, :])
        attn = jax.nn.softmax(energy, axis=-1)
        out = jnp.einsum('bcj,bij->bci', q, attn).reshape(B, C * R * R, h, w)
        out = gamma * out + xs
        out = out.reshape(B, C, R, R, h, w).transpose(0, 1, 4, 2, 5, 3).reshape(B, C, H, W)
        return out

    def _L2_conv_ref(pair, W_left, b_left, W_right, b_right, W_gate, b_gate, W_eq, b_eq, W_out, b_out, ln_scale, ln_bias):
        import jax, jax.numpy as jnp
        import numpy as np
        LN_EPS = 1e-05

        def _layer_norm(x, scale, bias):
            mu = jnp.mean(x, axis=-1, keepdims=True)
            var = jnp.mean(jnp.square(x - mu), axis=-1, keepdims=True)
            return (x - mu) * jax.lax.rsqrt(var + LN_EPS) * scale + bias
        left = pair @ W_left + b_left
        right = pair @ W_right + b_right
        gate = jax.nn.sigmoid(pair @ W_gate + b_gate)
        left = left + (pair @ W_eq + b_eq)
        right_sum = jnp.sum(right, axis=2, keepdims=True)
        out = left * right_sum
        out = out * gate
        out = out @ W_out + b_out
        return _layer_norm(out + pair, ln_scale, ln_bias)

    def _L3_conv_ref(x, gamma):
        import jax, jax.numpy as jnp
        import numpy as np
        R = 2
        B, C, H, W = x.shape
        h, w = (H // R, W // R)
        xs = x.reshape(B, C, h, R, w, R).transpose(0, 1, 3, 5, 2, 4).reshape(B, C * R * R, h, w)
        hw = h * w
        q = xs.reshape(B, C * R * R, hw)
        energy = jnp.einsum('bci,bcj->bij', q, q)
        d = jnp.sqrt(jnp.diagonal(energy, axis1=1, axis2=2))
        energy = energy / (d[:, :, None] * d[:, None, :])
        attn = jax.nn.softmax(energy, axis=-1)
        out = jnp.einsum('bcj,bij->bci', q, attn).reshape(B, C * R * R, h, w)
        out = gamma * out + xs
        out = out.reshape(B, C, R, R, h, w).transpose(0, 1, 4, 2, 5, 3).reshape(B, C, H, W)
        return out

    def _gn(v, G=32, eps=1e-5):
        B_, H_, W_, C_ = v.shape
        g = v.reshape(B_, H_, W_, G, C_ // G)
        m = jnp.mean(g, axis=(1, 2, 4), keepdims=True)
        s = jnp.var(g, axis=(1, 2, 4), keepdims=True)
        return ((g - m) / jnp.sqrt(s + eps)).reshape(v.shape)

    def _ln_c(v, eps=1e-6):
        m = jnp.mean(v, axis=-1, keepdims=True)
        s = jnp.var(v, axis=-1, keepdims=True)
        return (v - m) / jnp.sqrt(s + eps)

    def _ln_t(v, eps=1e-5):
        m = jnp.mean(v, axis=-1, keepdims=True)
        s = jnp.var(v, axis=-1, keepdims=True)
        return (v - m) / jnp.sqrt(s + eps)

    def _to_tokens(v):
        B_, H_, W_, C_ = v.shape
        return v.reshape(B_, H_ * W_, C_)
    def _from_tokens(t, like):
        return t.reshape(like.shape)

    x = _L0_conv_ref(x, L0_conv_W1, L0_conv_b1, L0_conv_W2, L0_conv_b2, L0_conv_Wq, L0_conv_bq, L0_conv_Wk, L0_conv_bk, L0_conv_Wv, L0_conv_bv, L0_conv_W3, L0_conv_b3)
    x = _L1_conv_ref(x, L1_conv_gamma)
    x = _L2_conv_ref(x, L2_conv_W_left, L2_conv_b_left, L2_conv_W_right, L2_conv_b_right, L2_conv_W_gate, L2_conv_b_gate, L2_conv_W_eq, L2_conv_b_eq, L2_conv_W_out, L2_conv_b_out, L2_conv_ln_scale, L2_conv_ln_bias)
    x = _L3_conv_ref(x, L3_conv_gamma)
    return x


_drawn_inputs = setup_inputs


def setup_inputs(seed=0):
    import zlib

    import numpy as np

    out = dict(_drawn_inputs(seed))
    spreads = {'L0_conv_b1': (0.0, 0.1),
     'L0_conv_b2': (0.0, 0.1),
     'L0_conv_bq': (0.0, 2.0),
     'L0_conv_bk': (0.0, 2.0),
     'L0_conv_bv': (0.0, 0.1),
     'L0_conv_b3': (0.0, 0.1),
     'L2_conv_b_left': (0.0, 0.1),
     'L2_conv_b_right': (0.0, 0.1),
     'L2_conv_b_gate': (0.0, 0.1),
     'L2_conv_b_eq': (0.0, 0.1),
     'L2_conv_b_out': (0.0, 0.8),
     'L2_conv_ln_scale': (1.0, 0.2),
     'L2_conv_ln_bias': (0.0, 0.1)}
    factors = {'L0_conv_Wq': 64.0, 'L0_conv_Wk': 64.0, 'L0_conv_Wv': 3.206}
    for name, (base, spread) in spreads.items():
        noise = np.random.default_rng([zlib.crc32(name.encode()), seed]).standard_normal(out[name].shape)
        drawn = base * np.exp(spread * noise) if base else spread * noise
        out[name] = jnp.asarray(drawn.astype(out[name].dtype))
    for name, factor in factors.items():
        out[name] = (out[name] * factor).astype(out[name].dtype)
    return out
```

```python
import numpy as np
import concourse.bass as bass
from concourse import mybir
from contextlib import ExitStack

F32 = mybir.dt.float32
F32R = mybir.dt.float32r
BF16 = mybir.dt.bfloat16
ALU = mybir.AluOpType
ACT = mybir.ActivationFunctionType
AX = mybir.AxisListType

B, H, W, C = 4, 64, 64, 128
N = H * W
P = 128
DQK, DV, HEADS = 4, 16, 8
CHUNK = 512
CHUNKS = N // CHUNK
ROWS = CHUNK // W
TILES = CHUNK // P
TAPS = 9
STEPS = 3 * TAPS
HP, WP = H + 2, W + 2
NEG = -1e10
EPS_L = 1e-5
R = 2
GROUPS = 8
H2G = 4
NPOS = N // 2
KT = NPOS // P
IHALF = NPOS // 2
G32 = 32


def share(n, u, steps, first=0):
    if u < first:
        return range(0)
    return range(n * (u - first) // (steps - first), n * (u - first + 1) // (steps - first))


def valid(c):
    return 0 <= c < CHUNKS


def score_base(s):
    return sum((4 * t if valid(t - 1) else 0) + (1 if valid(t) else 0) for t in range(s))


def exp_base(c):
    return 2 * c * (c + 1)


def pv_base(c):
    return c * (c + 1) // 2


def build_program(nc, x, W1, b1, W2, b2, Wq, bq, Wk, bk, Wv, bv, W3, b3, gamma1,
                  Wleft, bleft, Wright, bright, Wgate, bgate, Weq, beq, Wout, bout, ln_scale, ln_bias, gamma3, out):
    ctx = ExitStack()
    with ctx:
        def sb(name, shape, dt=F32):
            return ctx.enter_context(nc.sbuf_tensor(name, shape, dt))

        def sem(name):
            return ctx.enter_context(nc.semaphore(name))

        w1h, w1l = sb("w1h", [P, TAPS, C], F32R), sb("w1l", [P, TAPS, C], F32R)
        w2h, w2l = sb("w2h", [P, TAPS, 2 * C], F32R), sb("w2l", [P, TAPS, 2 * C], F32R)
        sqh, sql = sb("sqh", [P, 6, C], F32R), sb("sql", [P, 6, C], F32R)
        Q_, K_, M_, L_, G_, O_ = range(6)
        wv32 = sb("wv32", [P, G32])
        wright = sb("wright", [P, C])
        ident, ones = sb("ident", [P, P]), sb("ones", [P, P])
        identb = sb("identb", [P, P], BF16)
        sel_den = sb("sel_den", [P, P], F32R)
        sel_den32 = sb("sel_den32", [P, P])
        sel_max = sb("sel_max", [P, P])
        mask_q = sb("mask_q", [P, P], BF16)
        mask_k = sb("mask_k", [P, CHUNK + 3 * P], BF16)
        half = sb("half", [P, KT])
        NB = 13
        bias = sb("bias", [P, NB])
        B1, B2A, B2B, B3, QB, KB, BL, BG, BR, BO, G1, G3, BE = range(NB)
        bv_rep = sb("bv_rep", [P, TILES, DV])
        ln_s, ln_b = sb("ln_s", [P, C]), sb("ln_b", [P, C])

        xin = sb("xin", [P, 4, TILES, C])
        ebuf = sb("ebuf", [P, 2, CHUNK])
        th, ah, c3 = sb("th", [P, CHUNK]), sb("ah", [P, CHUNK]), sb("c3", [P, CHUNK])
        c3h, c3l = sb("c3h", [P, CHUNK], F32R), sb("c3l", [P, CHUNK], F32R)
        qop = sb("qop", [P, 3, CHUNK], F32R)
        atth, attl = sb("atth", [P, CHUNK], F32R), sb("attl", [P, CHUNK], F32R)
        rden = sb("rden", [P, CHUNK])
        zbuf = sb("zbuf", [P, CHUNK])
        mpart = sb("mpart", [P, TILES, CHUNKS])
        mneg = sb("mneg", [P, 2, TILES])
        mdiag = sb("mdiag", [P, TILES, P])
        vaug = sb("vaug", [P, CHUNKS * TILES, G32])
        IMG = HP * WP
        planes = sb("planes", [P, 4 * IMG + 8], F32R)
        kop = sb("kop", [P, N], F32R)
        xeh, xel, c1h, c1l = [planes[:, i * IMG:(i + 1) * IMG].rearrange("p (r c) -> p r c", c=WP) for i in range(4)]
        XH, XL, TH, TL = [planes[:, i * N:(i + 1) * N] for i in range(4)]
        res = sb("res", [P, N])
        prob = sb("prob", [P, 8, CHUNK])
        d2, rd, gz = sb("d2", [P, KT]), sb("rd", [P, KT]), sb("gz", [P, KT])
        zsum = sb("zsum", [P, 2, KT])
        square = c3[:, 0:2 * P]
        rpart = ebuf[:, 0, :].rearrange("p (g c) -> p g c", c=H)
        rsum = sb("rsum", [P, H]); rs2 = sb("rs2", [P, H, 2])
        st = sb("st", [P, 2, H2G, 6]); mv = sb("mv", [P, 2, H2G, 2]); rstd = sb("rstd", [P, 2, H2G])
        psum = ctx.enter_context(nc.psum_tensor("psum", [P, 8, CHUNK], F32))
        XT = prob[:, :, :].rearrange("p a n -> p (a n)")
        XTv = XT.rearrange("p (n r) -> p r n", r=R)
        XNH, XNL = [planes[:, i * N:(i + 1) * N].rearrange("p (r n) -> p r n", r=R) for i in range(2)]
        TH, TL = [planes[:, i * N:(i + 1) * N] for i in (2, 3)]
        QTh, QTl = [t.rearrange("p (k i) -> p k i", i=2 * P) for t in (TH, TL)]
        Ph = kop[:, 0:2 * IHALF].rearrange("p (a n) -> p a n", a=2)
        Pl = kop[:, 2 * IHALF:4 * IHALF].rearrange("p (a n) -> p a n", a=2)
        stash = res[:, 0:NPOS].rearrange("p (q n) -> p q n", n=CHUNK)
        pexp = res[:, NPOS:2 * NPOS].rearrange("p (a n) -> p a n", a=2)
        rdiag = res[:, 0:NPOS].rearrange("p (k n) -> p k n", n=P)
        zdiag = res[:, NPOS:2 * NPOS].rearrange("p (k n) -> p k n", n=P)
        scaled = res[:, NPOS:2 * NPOS].rearrange("p (q n) -> p q n", n=CHUNK)
        Gh = kop[:, 0:2 * CHUNK].rearrange("p (a n) -> p a n", a=2)
        Gl = kop[:, 2 * CHUNK:4 * CHUNK].rearrange("p (a n) -> p a n", a=2)
        sg, ug, gg, oT = [res[:, i * 2 * CHUNK:(i + 1) * 2 * CHUNK].rearrange("p (a n) -> p a n", a=2) for i in range(4)]

        bA, bB, bC, bS, bT, bP = 0, 1, 2, 3, 5, 7
        t_bank = {0: bA, 1: bB, 2: bC}
        c1_bank = {0: bB, 1: bC}

        w_loaded, w_stage1, w_stage2 = sem("w_loaded"), sem("w_stage1"), sem("w_stage2")
        pool_set, dve_set, act_set = sem("pool_set"), sem("dve_set"), sem("act_set")
        arrived, go = sem("arrived"), sem("go")
        passed = sem("passed")
        names = """pads x_transposed elu_min elu_exp res_ready elu_read xeh_ready xe_ready c1_mm c1h_ready c1_ready
            gate_mm value_mm th_ready ah_ready c3_ready c3h_ready c3l_ready res_added qk_mm qh_ready kh_ready q_ready k_ready
            s_filled s_drained v_ready max_ready diag_ready mrep_mm mrow_h mrow_ready t_filled exp_done pv_done att_h att_l
            den_mm mh_mm den_added den_inv z_ready y_ready m_step
            a_mm xt_act xt_dve qt_mm qth_ready sq_ready qtl_ready rd_ready rdiag_ready rdrow_mm xn_ready xnh_ready xnl_ready
            e_mm p_ready ph_ready pl_ready ap_mm stash_act stash_dve gz_step zdiag_ready zrow_mm zrow_copied scaled_ready x_pool x_dve
            p_mm pth_ready ptl_ready p_sum rs_mm rs_ready lr_mm gt_mm sg_ready u_ready g_ready gh_ready gl_ready o_mm ot_ready ot_mm z2_ready
            st_ready eps_ready rstd_ready centred_ready ln_ready mfin""".split()
        S = {n: sem(n) for n in names}
        x_loaded = [sem(f"x_loaded{i}") for i in range(4)]
        out_sent = sem("out_sent")
        loop_sems = list(S.values()) + x_loaded + [out_sent]

        block = ctx.enter_context(nc.Block())

        @block.sync
        def _(sp):
            n = 0
            def load(dst, src):
                nonlocal n
                sp.dma_start(dst, src).then_inc(w_loaded, 16)
                n += 16
            stage1 = res[:, 0:TAPS * C]
            stage2 = prob[:, :, :].rearrange("p a n -> p (a n)")[:, 0:TAPS * 2 * C]
            sp.wait_ge(pool_set, POOL_CLEARED)
            load(stage1.rearrange("p (t o) -> p t o", o=C), W1.rearrange("a b i o -> i (a b) o"))
            load(stage2.rearrange("p (t o) -> p t o", o=2 * C), W2.rearrange("a b i o -> i (a b) o"))
            sq = res[:, TAPS * C:TAPS * C + 7 * C].rearrange("p (s o) -> p s o", o=C)
            for g in range(4):
                load(sq[:, 0, g * G32 + 1:g * G32 + 1 + DQK], Wq)
                load(sq[:, 1, g * G32 + 1:g * G32 + 1 + DQK], Wk)
                load(bias[g * G32 + 1:g * G32 + 1 + DQK, QB:QB + 1], bq.rearrange("(d o) -> d o", o=1))
                load(bias[g * G32 + 1:g * G32 + 1 + DQK, KB:KB + 1], bk.rearrange("(d o) -> d o", o=1))
                load(planes_w3(res)[g * G32:g * G32 + DV], W3.rearrange("(h d) o -> d h o", d=DV))
            load(sq[:, 3, :], Wleft)
            load(sq[:, 4, :], Wgate)
            load(sq[:, 5, :], Wout)
            load(sq[:, 6, :], Weq)
            load(wv32[:, 0:DV], Wv)
            load(wright[:], Wright)
            for col, v in ((B1, b1), (B3, b3), (BL, bleft), (BG, bgate), (BR, bright), (BO, bout), (BE, beq)):
                load(bias[:, col:col + 1], v.rearrange("(c o) -> c o", o=1))
            load(bias[:, B2A:B2A + 1], b2[0:C].rearrange("(c o) -> c o", o=1))
            load(bias[:, B2B:B2B + 1], b2[C:2 * C].rearrange("(c o) -> c o", o=1))
            load(bias[:, G1:G1 + 1], bcast(gamma1, P, 1))
            load(bias[:, G3:G3 + 1], bcast(gamma3, P, 1))
            for t in range(TILES):
                load(bv_rep[:, t, :], bcast(bv, P, DV))
            load(ln_s[:], bcast(ln_scale, P, C))
            load(ln_b[:], bcast(ln_bias, P, C))
            assert n == W_LOADS, n
            with sp.Fori(0, B) as b:
                xb = x[b].rearrange("r w c -> (r w) c").rearrange("(k t p) c -> k p t c", t=TILES, p=P)
                for c in range(CHUNKS):
                    if c >= 4:
                        sp.wait_ge(S["x_transposed"], c - 3)
                    sp.dma_start(xin[:, c % 4], xb[c]).then_inc(x_loaded[c % 4], 16)
                ob = out[b].rearrange("c (g h r) k -> g r c h k", r=R, h=8)
                for g in range(4):
                    sp.wait_ge(S["x_pool"], 4 + g + 1)
                    sp.wait_ge(S["x_dve"], 4 + g + 1)
                    for r1 in range(R):
                        src = XT[r1:P:R, g * 8 * C:(g + 1) * 8 * C].rearrange("p (h k) -> p h k", k=C)
                        sp.dma_start(ob[g, r1], src).then_inc(out_sent, 16)
                sp.wait_ge(out_sent, 4 * R * 16)
                sp.sem_inc(arrived, 1)
                sp.wait_ge(go, b + 1)
                sp.sem_inc(passed, 1)

        @block.tensor
        def _(pe):
            mm, tr = nc.tensor.matmul, nc.tensor.transpose

            def three(o, wh, wl, xh, xl, start, stop):
                mm(o, wh, xh, start=start, stop=False)
                mm(o, wh, xl, start=False, stop=False)
                return mm(o, wl, xh, start=False, stop=stop)

            def transpose_x(c):
                pe.wait_ge(x_loaded[c % 4], 16 * (c // 4 + 1))
                bank = t_bank.get(c, bA)
                if c == 3:
                    pe.wait_ge(S["elu_read"], 1)
                    pe.wait_ge(S["res_ready"], 1)
                elif c == 4:
                    pe.wait_ge(S["elu_read"], 4)
                elif c > 4:
                    pe.wait_ge(S["c1_ready"], c - 2)
                for t in range(TILES):
                    last = tr(psum[:, bank, t * P:(t + 1) * P], xin[:, c % 4, t, :], ident[:])
                last.then_inc(S["x_transposed"], 1)

            def conv1_tap(c, tap):
                bank = c1_bank.get(c, bA)
                if tap == 0:
                    pe.wait_ge(S["xe_ready"], min(c + 2, CHUNKS))
                    if c >= 2:
                        pe.wait_ge(S["elu_read"], min(c + 3, CHUNKS))
                        if c >= 3:
                            pe.wait_ge(S["c1_ready"], c)
                dy, dx = divmod(tap, 3)
                r0 = c * ROWS + dy
                last = three(psum[:, bank, :], w1h[:, tap, :], w1l[:, tap, :],
                             xeh[:, r0:r0 + ROWS, dx:dx + W], xel[:, r0:r0 + ROWS, dx:dx + W], tap == 0, tap == TAPS - 1)
                if tap == TAPS - 1:
                    last.then_inc(S["c1_mm"], 1)

            def conv2_tap(c, tap, gate):
                bank = bB if gate else bC
                if tap == 0 and gate:
                    pe.wait_ge(S["c1_ready"], min(c + 2, CHUNKS))
                    if c >= 1:
                        pe.wait_ge(S["q_ready"], c)
                if tap == 0 and not gate and c >= 1:
                    pe.wait_ge(S["k_ready"], c)
                dy, dx = divmod(tap, 3)
                r0 = c * ROWS + dy
                o = C if gate else 0
                last = three(psum[:, bank, :], w2h[:, tap, o:o + C], w2l[:, tap, o:o + C],
                             c1h[:, r0:r0 + ROWS, dx:dx + W], c1l[:, r0:r0 + ROWS, dx:dx + W], tap == 0, tap == TAPS - 1)
                if tap == TAPS - 1:
                    last.then_inc(S["gate_mm" if gate else "value_mm"], 1)

            def project(c):
                pe.wait_ge(S["c3h_ready"], c + 1)
                pe.wait_ge(S["c3l_ready"], c + 1)
                three(psum[:, bB, :], sqh[:, Q_, :], sql[:, Q_, :], c3h[:], c3l[:], True, True)
                three(psum[:, bC, :], sqh[:, K_, :], sql[:, K_, :], c3h[:], c3l[:], True, True).then_inc(S["qk_mm"], 1)

            def project_values(c):
                i = score_base(c) + (4 * c if valid(c - 1) else 0)
                if i >= 2:
                    pe.wait_ge(S["s_drained"], i - 1)
                for t in range(TILES):
                    last = mm(psum[:, bS + i % 2, t * G32:(t + 1) * G32], c3[:, t * P:(t + 1) * P], wv32[:], start=True, stop=True)
                last.then_inc(S["s_filled"], 1)

            def score_tile(c, i):
                t, kc = divmod(i, c + 1)
                n = score_base(c + 1) + i
                if i == 0:
                    pe.wait_ge(S["q_ready"], c + 1)
                    pe.wait_ge(S["k_ready"], c + 1)
                if n >= 2:
                    pe.wait_ge(S["s_drained"], n - 1)
                bank = bS + n % 2
                diag = kc == c
                width = (t + 1) * P if diag else CHUNK
                if diag:
                    mm(psum[:, bank, t * P:width], identb[:], mask_q[:], start=True, stop=False, skip_group_check=True)
                mm(psum[:, bank, 0:width], qop[:, c % 3, t * P:(t + 1) * P], kop[:, kc * CHUNK:kc * CHUNK + width],
                   start=not diag, stop=True, skip_group_check=diag).then_inc(S["s_filled"], 1)

            def max_rows(c):
                pe.wait_ge(S["diag_ready"], c + 1)
                if c >= 1:
                    pe.wait_ge(S["den_added"], c)
                mm(psum[:, bT, :], sel_max[:], mdiag[:, :, :], start=True, stop=True).then_inc(S["mrep_mm"], 1)

            def exp_tile(c, j):
                e = exp_base(c) + j
                if j == 0:
                    pe.wait_ge(S["mrow_ready"], c + 1)
                elif j == 1:
                    if c >= 1:
                        pe.wait_ge(S["z_ready"], c)
                else:
                    pe.wait_ge(S["exp_done"], e - 1)
                bank = bT + j % 2
                diag = j >= TILES * c
                last = mm(psum[:, bank, :], kop[:, j * P:(j + 1) * P], qop[:, c % 3, :], start=True, stop=not diag)
                if diag:
                    r = j - TILES * c
                    o = (TILES - 1 - r) * P
                    last = mm(psum[:, bank, :], identb[:], mask_k[:, o:o + CHUNK], start=False, stop=True)
                last.then_inc(S["t_filled"], 1)

            def attend(c, g):
                if g == 0:
                    pe.wait_ge(S["v_ready"], c + 1)
                    if c >= 1:
                        pe.wait_ge(S["att_l"], c)
                pe.wait_ge(S["exp_done"], exp_base(c) + 4 * g + 4)
                for q in range(4):
                    j = 4 * g + q
                    last = mm(psum[q * G32:(q + 1) * G32, bP, :], vaug[:, j, :], prob[:, (exp_base(c) + j) % 8, :],
                              start=g == 0, stop=g == c, tile_position=(0, q * G32))
                last.then_inc(S["pv_done"], 1)

            def attention_out(c):
                pe.wait_ge(S["att_l"], c + 1)
                pe.wait_ge(S["exp_done"], exp_base(c + 1))
                mm(psum[:, bT, :], sel_den[:], atth[:], start=True, stop=False)
                mm(psum[:, bT, :], sel_den[:], attl[:], start=False, stop=True).then_inc(S["den_mm"], 1)
                three(psum[:, bT + 1, :], sqh[:, M_, :], sql[:, M_, :], atth[:], attl[:], True, True).then_inc(S["mh_mm"], 1)

            def spatial_layer(y):
                for kk in range(8):
                    if y == 0:
                        pe.wait_ge(S["xt_dve" if kk % 2 else "xt_act"], kk // 2 + 1)
                    else:
                        pe.wait_ge(S["ln_ready"], kk + 1)
                        if kk == 0:
                            pe.wait_ge(S["z2_ready"], GROUPS)
                    if kk >= 4:
                        pe.wait_ge(S["qtl_ready"], 8 * y + kk - 3)
                    for k in range(2):
                        for r2 in range(R):
                            last = tr(psum[:, 4 + kk % 4, (2 * k + r2) * P:(2 * k + r2 + 1) * P],
                                      XTv[:, r2, (2 * kk + k) * P:(2 * kk + k + 1) * P], ident[:])
                    last.then_inc(S["qt_mm"], 1)
                pe.wait_ge(S["rdiag_ready"], y + 1)
                for q in range(4):
                    mm(psum[:, q, :], ones[:], rdiag[:, 4 * q:4 * q + 4, :], start=True, stop=True).then_inc(S["rdrow_mm"], 1)
                pe.wait_ge(S["xnl_ready"], 8 * (y + 1))
                for ih in range(2):
                    for j in range(KT + 2):
                        if j < KT:
                            energy(y, ih, j)
                        if j >= 2:
                            apply(y, ih, j - 2)
                pe.wait_ge(S["zdiag_ready"], y + 1)
                for q in range(4):
                    mm(psum[:, q, :], ones[:], zdiag[:, 4 * q:4 * q + 4, :], start=True, stop=True).then_inc(S["zrow_mm"], 1)

            def energy(y, ih, j):
                n = 2 * KT * y + KT * ih + j
                if n >= 2:
                    pe.wait_ge(S["p_ready"], n - 1)
                for q in range(2):
                    i0 = ih * IHALF + q * CHUNK
                    for r in range(R):
                        last = three(psum[:, 2 * (j % 2) + q, :], XNH[:, r, j * P:(j + 1) * P], XNL[:, r, j * P:(j + 1) * P],
                                     XNH[:, r, i0:i0 + CHUNK], XNL[:, r, i0:i0 + CHUNK], r == 0, r == 1)
                last.then_inc(S["e_mm"], 1)

            def apply(y, ih, j):
                n = 2 * KT * y + KT * ih + j
                pe.wait_ge(S["ph_ready"], n + 1)
                pe.wait_ge(S["pl_ready"], n + 1)
                if j == 0 and ih == 1:
                    pe.wait_ge(S["stash_act"], 2 * y + 2)
                    pe.wait_ge(S["stash_dve"], 2 * y + 2)
                for r2 in range(R):
                    for q in range(2):
                        i0 = q * CHUNK
                        last = three(psum[:, 4 + 2 * r2 + q, :], QTh[:, j, r2 * P:(r2 + 1) * P], QTl[:, j, r2 * P:(r2 + 1) * P],
                                     Ph[:, j % 2, i0:i0 + CHUNK], Pl[:, j % 2, i0:i0 + CHUNK], j == 0, j == KT - 1)
                last.then_inc(S["ap_mm"], 1)

            pe.wait_ge(act_set, ACT_SET)
            pe.wait_ge(dve_set, DVE_SET)
            pe.wait_ge(pool_set, POOL_SET)
            with pe.Fori(0, B) as b:
                for c in range(4):
                    transpose_x(c)
                for c in range(2):
                    for tap in range(TAPS):
                        conv1_tap(c, tap)
                for s in range(CHUNKS + 3):
                    cm, ce, cy = s - 1, s - 2, s - 3
                    for u in range(STEPS):
                        if u == 0:
                            if s + 4 < CHUNKS:
                                transpose_x(s + 4)
                            if valid(cy):
                                attention_out(cy)
                        if s < CHUNKS:
                            if u < 2 * TAPS:
                                conv2_tap(s, u % TAPS, u < TAPS)
                            elif s + 2 < CHUNKS:
                                conv1_tap(s + 2, u - 2 * TAPS)
                        if u == 2 and valid(ce):
                            max_rows(ce)
                        if valid(cm):
                            for i in share(4 * s, u, STEPS):
                                score_tile(cm, i)
                        if valid(ce):
                            for j in share(4 * (ce + 1), u, STEPS, 3):
                                if j >= 6 and j % 4 == 2:
                                    attend(ce, (j - 6) // 4)
                                exp_tile(ce, j)
                        if u == 24 and s < CHUNKS:
                            project(s)
                    if s < CHUNKS:
                        project_values(s)
                    if valid(ce):
                        attend(ce, ce)
                for g in range(GROUPS):
                    if g == 0:
                        pe.wait_ge(S["y_ready"], CHUNKS)
                    if g >= 4:
                        pe.wait_ge(S["xt_dve" if g % 2 else "xt_act"], (g - 4) // 2 + 1)
                    for h in range(H2G):
                        src = res[:, (H2G * g + h) * P:(H2G * g + h + 1) * P]
                        last = tr(psum[:, g % 4, h * P:(h + 1) * P], src, ident[:])
                    last.then_inc(S["a_mm"], 1)
                spatial_layer(0)
                for g in range(GROUPS):
                    pe.wait_ge(S["x_pool"], g // 2 + 1)
                    pe.wait_ge(S["x_dve"], max(g // 2, min(g, 3)) + 1)
                    if g >= 4:
                        pe.wait_ge(S["p_sum"], g - 3)
                    for h in range(H2G):
                        last = tr(psum[:, g % 4, h * P:(h + 1) * P], XT[:, (H2G * g + h) * C:(H2G * g + h + 1) * C], ident[:])
                    last.then_inc(S["p_mm"], 1)
                pe.wait_ge(S["rs_ready"], 1)
                mm(psum[:, 4, 0:H], wright[:], rsum[:], start=True, stop=True).then_inc(S["rs_mm"], 1)
                pe.wait_ge(S["rs_ready"], 3)
                for g in range(GROUPS + 2):
                    if g < GROUPS:
                        o = 4 * (g % 2)
                        p_ = slice(g * CHUNK, (g + 1) * CHUNK)
                        if g >= 2:
                            pe.wait_ge(S["u_ready"], g - 1)
                            pe.wait_ge(S["sg_ready"], g - 1)
                        three(psum[:, o, :], sqh[:, L_, :], sql[:, L_, :], TH[:, p_], TL[:, p_], True, True).then_inc(S["lr_mm"], 1)
                        three(psum[:, o + 1, :], sqh[:, G_, :], sql[:, G_, :], TH[:, p_], TL[:, p_], True, True).then_inc(S["gt_mm"], 1)
                    if 1 <= g <= GROUPS:
                        f = g - 1
                        pe.wait_ge(S["gl_ready"], f + 1)
                        if f >= 2:
                            pe.wait_ge(S["ot_ready"], f - 1)
                        three(psum[:, 4 * (f % 2) + 2, :], sqh[:, O_, :], sql[:, O_, :], Gh[:, f % 2], Gl[:, f % 2], True, True).then_inc(S["o_mm"], 1)
                    if g >= 2:
                        f = g - 2
                        pe.wait_ge(S["ot_ready"], f + 1)
                        if f >= 2:
                            pe.wait_ge(S["z2_ready"], f - 1)
                        for h in range(H2G):
                            last = tr(psum[:, 4 * (f % 2) + 3, h * P:(h + 1) * P], oT[:, f % 2, h * P:(h + 1) * P], ident[:])
                        last.then_inc(S["ot_mm"], 1)
                spatial_layer(1)
                pe.wait_ge(S["zrow_mm"], 8)
                pe.sem_inc(arrived, 1)
                pe.wait_ge(go, b + 1)
                pe.sem_inc(passed, 1)

        @block.scalar
        def _(act):
            a = nc.scalar.activation

            def image(plane, c):
                return plane[:, 1 + c * ROWS:1 + (c + 1) * ROWS, 1:1 + W]

            def rows(t):
                return t.rearrange("p (r w) -> p r w", w=W)

            def elu_exp(c):
                act.wait_ge(S["elu_min"], c + 1)
                a(ebuf[:, c % 2], ebuf[:, c % 2], ACT.Exp).then_inc(S["elu_exp"], 1)
                a(res_chunk(res, c), split_w(psum[:, t_bank.get(c, bA), :]), ACT.Identity, bias=bias[:, B3:B3 + 1]).then_inc(S["res_ready"], 1)

            def elu_high(c):
                act.wait_ge(S["elu_read"], c + 1)
                a(image(xeh, c), rows(ebuf[:, c % 2]), ACT.Copy).then_inc(S["xeh_ready"], 1)

            def c1_high(c):
                act.wait_ge(S["c1_mm"], c + 1)
                a(image(c1h, c), rows(psum[:, c1_bank.get(c, bA), :]), ACT.Identity, bias=bias[:, B1:B1 + 1]).then_inc(S["c1h_ready"], 1)

            def spatial_layer(y):
                for kk in range(8):
                    act.wait_ge(S["qt_mm"], 8 * y + kk + 1)
                    bank = psum[:, 4 + kk % 4, :].rearrange("p (k i) -> p k i", k=2)
                    a(QTh[:, 2 * kk:2 * kk + 2, :], bank, ACT.Copy).then_inc(S["qth_ready"], 1)
                    for k in range(2):
                        if 16 * y + 2 * kk + k >= 1:
                            act.wait_ge(S["sq_ready"], 16 * y + 2 * kk + k)
                        a(square, bank[:, k], ACT.Square, accum_out=d2[:, 2 * kk + k:2 * kk + k + 1]).then_inc(S["sq_ready"], 1)
                for n in range(8):
                    act.wait_ge(S["xn_ready"], 8 * y + n + 1)
                    a(XNH[:, n % 2, (n // 2) * CHUNK:(n // 2 + 1) * CHUNK], ebuf[:, n % 2], ACT.Copy).then_inc(S["xnh_ready"], 1)
                for ih in range(2):
                    for j in range(KT):
                        n = 2 * KT * y + KT * ih + j
                        act.wait_ge(S["e_mm"], n + 1)
                        if n >= 2:
                            act.wait_ge(S["pl_ready"], n - 1)
                        a(pexp[:, j % 2], psum[:, 2 * (j % 2):2 * (j % 2) + 2, :], ACT.Exp,
                          accum_out=zsum[:, ih, j:j + 1]).then_inc(S["p_ready"], 1)
                        act.wait_ge(S["p_ready"], n + 1)
                        if n >= 2:
                            act.wait_ge(S["ap_mm"], n - 1)
                        a(Ph[:, j % 2], pexp[:, j % 2], ACT.Copy).then_inc(S["ph_ready"], 1)
                    if ih == 0:
                        act.wait_ge(S["ap_mm"], 2 * KT * y + KT)
                        for q in range(2):
                            a(stash[:, q], psum[:, 4 + q, :], ACT.Copy).then_inc(S["stash_act"], 1)
                for q in (2, 3):
                    act.wait_ge(S["zrow_mm"], 4 * y + q + 1)
                    a(ebuf[:, q - 2], psum[:, q, :], ACT.Copy).then_inc(S["zrow_copied"], 1)

            act.wait_ge(w_loaded, W_LOADS)
            stage1 = res[:, 0:TAPS * C].rearrange("p (t o) -> p t o", o=C)
            stage2 = prob[:, :, :].rearrange("p a n -> p (a n)")[:, 0:TAPS * 2 * C].rearrange("p (t o) -> p t o", o=2 * C)
            sq = res[:, TAPS * C:TAPS * C + 7 * C].rearrange("p (s o) -> p s o", o=C)
            a(w1h[:], stage1, ACT.Copy).then_inc(act_set, 1)
            a(w2h[:], stage2, ACT.Copy).then_inc(act_set, 1)
            act.wait_ge(dve_set, DVE_FOLDED)
            a(sqh[:], sq[:, 0:6, :], ACT.Copy).then_inc(act_set, 1)
            a(sel_den[:], sel_den32[:], ACT.Copy).then_inc(act_set, 1)
            with act.Fori(0, B) as b:
                for c in range(4):
                    elu_exp(c)
                    if c % 2:
                        elu_high(c - 1)
                        elu_high(c)
                act.wait_ge(S["pads"], PADS)
                for c in range(2):
                    c1_high(c)
                for s in range(CHUNKS + 2):
                    ce = s - 2
                    for u in range(STEPS):
                        if valid(ce):
                            for j in share(4 * (ce + 1), u, STEPS, 3):
                                e = exp_base(ce) + j
                                act.wait_ge(S["t_filled"], e + 1)
                                if e >= 8:
                                    act.wait_ge(S["pv_done"], (e - 8) // 4 + 1)
                                a(prob[:, e % 8], psum[:, bT + j % 2, :], ACT.Exp).then_inc(S["exp_done"], 1)
                        if u == 1 and s + 4 < CHUNKS:
                            elu_exp(s + 4)
                        if u == 2 and valid(ce):
                            act.wait_ge(S["mrep_mm"], ce + 1)
                            for g in (0, 2):
                                a(qop[g * G32:g * G32 + 1, ce % 3, :], psum[g * G32:g * G32 + 1, bT, :], ACT.Copy).then_inc(S["mrow_h"], 1)
                        if u == 5 and s + 4 < CHUNKS:
                            elu_high(s + 4)
                        if s < CHUNKS:
                            if u == 10:
                                act.wait_ge(S["gate_mm"], s + 1)
                                a(th[:], psum[:, bB, :], ACT.Tanh, scale=0.5, bias=bias[:, B2B:B2B + 1]).then_inc(S["th_ready"], 1)
                            if u == 18:
                                act.wait_ge(S["value_mm"], s + 1)
                                a(ah[:], psum[:, bC, :], ACT.Identity, scale=0.5, bias=bias[:, B2A:B2A + 1]).then_inc(S["ah_ready"], 1)
                            if u == 19:
                                act.wait_ge(S["c3_ready"], s + 1)
                                a(c3h[:], c3[:], ACT.Copy).then_inc(S["c3h_ready"], 1)
                            if u == 24:
                                act.wait_ge(S["qk_mm"], s + 1)
                                a(qop[:, s % 3, :], psum[:, bB, :], ACT.Identity, bias=bias[:, QB:QB + 1]).then_inc(S["qh_ready"], 1)
                                a(kop[:, s * CHUNK:(s + 1) * CHUNK], psum[:, bC, :], ACT.Identity, bias=bias[:, KB:KB + 1]).then_inc(S["kh_ready"], 1)
                            if u == 26 and s + 2 < CHUNKS:
                                c1_high(s + 2)
                    if valid(ce):
                        act.wait_ge(S["pv_done"], pv_base(ce + 1))
                        if ce >= 1:
                            act.wait_ge(S["mh_mm"], ce)
                        a(atth[:], psum[:, bP, :], ACT.Copy).then_inc(S["att_h"], 1)
                for g in range(0, GROUPS, 2):
                    act.wait_ge(S["a_mm"], g + 1)
                    a(XT[:, g * CHUNK:(g + 1) * CHUNK], psum[:, g % 4, :], ACT.Copy).then_inc(S["xt_act"], 1)
                spatial_layer(0)
                for g in range(GROUPS):
                    act.wait_ge(S["p_mm"], g + 1)
                    a(TH[:, g * CHUNK:(g + 1) * CHUNK], psum[:, g % 4, :], ACT.Copy).then_inc(S["pth_ready"], 1)
                act.wait_ge(S["rs_mm"], 1)
                for r in range(R):
                    a(rs2[:, :, r], psum[:, 4, 0:H], ACT.Identity, scale=0.5, bias=bias[:, BR:BR + 1]).then_inc(S["rs_ready"], 1)
                for g in range(GROUPS + 2):
                    if g < GROUPS:
                        act.wait_ge(S["gt_mm"], g + 1)
                        if g >= 2:
                            act.wait_ge(S["g_ready"], g - 1)
                        a(sg[:, g % 2], psum[:, 4 * (g % 2) + 1, :], ACT.Tanh, scale=0.5, bias=bias[:, BG:BG + 1]).then_inc(S["sg_ready"], 1)
                        act.wait_ge(S["g_ready"], g + 1)
                        if g >= 2:
                            act.wait_ge(S["o_mm"], g - 1)
                        a(Gh[:, g % 2], gg[:, g % 2], ACT.Copy).then_inc(S["gh_ready"], 1)
                    if 1 <= g <= GROUPS:
                        f = g - 1
                        act.wait_ge(S["o_mm"], f + 1)
                        if f >= 2:
                            act.wait_ge(S["ot_mm"], f - 1)
                        a(oT[:, f % 2], psum[:, 4 * (f % 2) + 2, :], ACT.Identity, bias=bias[:, BO:BO + 1]).then_inc(S["ot_ready"], 1)
                spatial_layer(1)
                act.wait_ge(S["zrow_copied"], 4)
                act.sem_inc(arrived, 1)
                act.wait_ge(go, b + 1)
                act.sem_inc(passed, 1)

        @block.vector
        def _(dve):
            tt, ts, stt = nc.vector.tensor_tensor, nc.vector.tensor_scalar, nc.vector.scalar_tensor_tensor

            def image(plane, c):
                return plane[:, 1 + c * ROWS:1 + (c + 1) * ROWS, 1:1 + W]

            def rows(t):
                return t.rearrange("p (r w) -> p r w", w=W)

            def elu_min(c):
                dve.wait_ge(S["x_transposed"], c + 1)
                if c >= 2:
                    dve.wait_ge(S["xe_ready"], c - 1)
                ts(ebuf[:, c % 2], psum[:, t_bank.get(c, bA), :], 0.0, None, ALU.min).then_inc(S["elu_min"], 1)

            def elu(c):
                dve.wait_ge(S["elu_exp"], c + 1)
                dve.wait_ge(S["res_ready"], c + 1)
                stt(ebuf[:, c % 2], ebuf[:, c % 2], -1.0, psum[:, t_bank.get(c, bA), :], ALU.add, ALU.max).then_inc(S["elu_read"], 1)

            def c1_low(c):
                dve.wait_ge(S["c1h_ready"], c + 1)
                stt(image(c1l, c), rows(psum[:, c1_bank.get(c, bA), :]), bias[:, B1:B1 + 1], image(c1h, c).bitcast(F32),
                    ALU.add, ALU.subtract).then_inc(S["c1_ready"], 1)

            chain = [0]

            def link(ins):
                ins.then_inc(dve_set, 1)
                chain[0] += 1
                dve.wait_ge(dve_set, chain[0])

            dve.wait_ge(w_loaded, W_LOADS)
            dve.wait_ge(pool_set, POOL_SET)
            stage1 = res[:, 0:TAPS * C].rearrange("p (t o) -> p t o", o=C)
            stage2 = prob[:, :, :].rearrange("p a n -> p (a n)")[:, 0:TAPS * 2 * C].rearrange("p (t o) -> p t o", o=2 * C)
            sq = res[:, TAPS * C:TAPS * C + 7 * C].rearrange("p (s o) -> p s o", o=C)
            ts(sq[:, 0, :], sq[:, 0, :], 0.25, None, ALU.mult).then_inc(dve_set, 1)
            nc.vector.tensor_reduce(sq[:, 2, :], planes_w3(res).rearrange("p h o -> p o h"), AX.X, ALU.add).then_inc(dve_set, 1)
            tt(sq[:, 3, :], sq[:, 3, :], sq[:, 6, :], ALU.add).then_inc(dve_set, 1)
            tt(bias[:, BL:BL + 1], bias[:, BL:BL + 1], bias[:, BE:BE + 1], ALU.add).then_inc(dve_set, 1)
            ts(bias[:, QB:QB + 1], bias[:, QB:QB + 1], 0.25, None, ALU.mult).then_inc(dve_set, 1)
            for col, k in ((B2A, 0.5), (B2B, 0.5), (BG, 0.5), (BR, 32.0)):
                ts(bias[:, col:col + 1], bias[:, col:col + 1], k, None, ALU.mult).then_inc(dve_set, 1)
            chain[0] = 9
            nc.vector.memset(bias[0:1, KB:KB + 1], 1.0).then_inc(dve_set, 1)
            nc.vector.memset(bias[64:65, KB:KB + 1], 1.0).then_inc(dve_set, 1)
            chain[0] = DVE_FOLDED
            dve.wait_ge(act_set, 1)
            tt(w1l[:], stage1, w1h[:].bitcast(F32), ALU.subtract).then_inc(dve_set, 1)
            dve.wait_ge(act_set, 2)
            tt(w2l[:], stage2, w2h[:].bitcast(F32), ALU.subtract).then_inc(dve_set, 1)
            dve.wait_ge(act_set, 3)
            tt(sql[:], sq[:, 0:6, :], sqh[:].bitcast(F32), ALU.subtract).then_inc(dve_set, 1)
            dve.wait_ge(dve_set, DVE_SET)

            def spatial_layer(y, gcol):
                for kk in range(8):
                    dve.wait_ge(S["qth_ready"], 8 * y + kk + 1)
                    dve.wait_ge(S["sq_ready"], 16 * y + 2 * kk + 2)
                    tt(QTl[:, 2 * kk:2 * kk + 2, :], psum[:, 4 + kk % 4, :].rearrange("p (k i) -> p k i", k=2),
                       QTh[:, 2 * kk:2 * kk + 2, :].bitcast(F32), ALU.subtract).then_inc(S["qtl_ready"], 1)
                dve.wait_ge(S["rd_ready"], y + 1)
                for k in range(KT):
                    ins = ts(rdiag[:, k, :], ident[:], rd[:, k:k + 1], None, ALU.mult)
                ins.then_inc(S["rdiag_ready"], 1)
                for n in range(8):
                    dve.wait_ge(S["rdrow_mm"], 4 * y + n // 2 + 1)
                    if n >= 2:
                        dve.wait_ge(S["xnl_ready"], 8 * y + n - 1)
                    q = n // 2
                    tt(ebuf[:, n % 2], XTv[:, n % 2, q * CHUNK:(q + 1) * CHUNK], psum[:, q, :], ALU.mult).then_inc(S["xn_ready"], 1)
                for ih in range(2):
                    for j in range(KT):
                        n = 2 * KT * y + KT * ih + j
                        dve.wait_ge(S["ph_ready"], n + 1)
                        tt(Pl[:, j % 2], pexp[:, j % 2], Ph[:, j % 2].bitcast(F32), ALU.subtract).then_inc(S["pl_ready"], 1)
                    if ih == 0:
                        dve.wait_ge(S["ap_mm"], 2 * KT * y + KT)
                        for q in range(2, 4):
                            nc.vector.tensor_copy(stash[:, q], psum[:, 4 + q, :]).then_inc(S["stash_dve"], 1)
                dve.wait_ge(S["p_ready"], 2 * KT * (y + 1))
                tt(gz[:], zsum[:, 0, :], zsum[:, 1, :], ALU.add).then_inc(S["gz_step"], 1)
                dve.wait_ge(S["gz_step"], 3 * y + 1)
                nc.vector.reciprocal(gz[:], gz[:]).then_inc(S["gz_step"], 1)
                dve.wait_ge(S["gz_step"], 3 * y + 2)
                ts(gz[:], gz[:], bias[:, gcol:gcol + 1], None, ALU.mult).then_inc(S["gz_step"], 1)
                dve.wait_ge(S["gz_step"], 3 * y + 3)
                dve.wait_ge(S["pl_ready"], 2 * KT * (y + 1))
                for k in range(KT):
                    ins = ts(zdiag[:, k, :], ident[:], gz[:, k:k + 1], None, ALU.mult)
                ins.then_inc(S["zdiag_ready"], 1)
                dve.wait_ge(S["zrow_mm"], 4 * y + 4)
                for q in range(4):
                    for r2 in range(R):
                        if q < 2:
                            t = stash[:, 2 * r2 + q]
                            ins = tt(t, t, psum[:, q, :], ALU.mult)
                        else:
                            t = scaled[:, 2 * r2 + q - 2]
                            dve.wait_ge(S["zrow_copied"], 2 * y + q - 1)
                            dve.wait_ge(S["ap_mm"], 2 * KT * (y + 1))
                            ins = tt(t, psum[:, 4 + 2 * r2 + q - 2, :], ebuf[:, q - 2], ALU.mult)
                        ins.then_inc(S["scaled_ready"], 1)
                    dve.wait_ge(S["scaled_ready"], 8 * y + 2 * q + 2)
                    xv = XTv[:, 1, q * CHUNK:(q + 1) * CHUNK]
                    tt(xv, t, xv, ALU.add).then_inc(S["x_dve"], 1)

            with dve.Fori(0, B) as b:
                for c in (0, 2):
                    elu_min(c)
                    elu_min(c + 1)
                    elu(c)
                    elu(c + 1)
                dve.wait_ge(S["pads"], PADS)
                for c in range(2):
                    c1_low(c)
                for s in range(CHUNKS + 3):
                    cm, ce, cy = s - 1, s - 2, s - 3
                    for u in range(STEPS):
                        if valid(cm):
                            for i in share(4 * s, u, STEPS):
                                t, kc = divmod(i, cm + 1)
                                n = score_base(s) + i
                                width = (t + 1) * P if kc == cm else CHUNK
                                dve.wait_ge(S["s_filled"], n + 1)
                                if i == 0 and cm >= 1:
                                    dve.wait_ge(S["max_ready"], cm)
                                nc.vector.tensor_reduce(mpart[:, t, kc:kc + 1], psum[:, bS + n % 2, 0:width], AX.X, ALU.max).then_inc(S["s_drained"], 1)
                        if u == 0 and valid(cy):
                            dve.wait_ge(S["den_mm"], cy + 1)
                            if cy >= 1:
                                dve.wait_ge(S["z_ready"], cy)
                            ts(rden[:], psum[:, bT, :], 1e-10, None, ALU.add).then_inc(S["den_added"], 1)
                            dve.wait_ge(S["den_added"], cy + 1)
                            nc.vector.reciprocal(rden[:], rden[:]).then_inc(S["den_inv"], 1)
                            dve.wait_ge(S["den_inv"], cy + 1)
                            dve.wait_ge(S["mh_mm"], cy + 1)
                            if cy >= 1:
                                dve.wait_ge(S["y_ready"], cy)
                            tt(zbuf[:], psum[:, bT + 1, :], rden[:], ALU.mult).then_inc(S["z_ready"], 1)
                        if u == 1 and s + 4 < CHUNKS:
                            elu_min(s + 4)
                        if u == 2 and valid(ce):
                            dve.wait_ge(S["mrow_h"], 2 * ce + 2)
                            tt(qop[64:65, ce % 3, :], psum[64:65, bT, :], qop[64:65, ce % 3, :].bitcast(F32), ALU.subtract).then_inc(S["mrow_ready"], 1)
                        if u == 4 and s + 4 < CHUNKS:
                            elu(s + 4)
                        if s < CHUNKS:
                            if u == 18:
                                dve.wait_ge(S["th_ready"], s + 1)
                                dve.wait_ge(S["ah_ready"], s + 1)
                                if s >= 1:
                                    dve.wait_ge(S["res_added"], s)
                                    dve.wait_ge(S["s_filled"], score_base(s))
                                stt(c3[:], th[:], 1.0, ah[:], ALU.add, ALU.mult).then_inc(S["c3_ready"], 1)
                            if u == 24:
                                dve.wait_ge(S["qh_ready"], s + 1)
                                stt(qop[64:128, s % 3, :], psum[64:128, bB, :], bias[64:128, QB:QB + 1], qop[64:128, s % 3, :].bitcast(F32),
                                    ALU.add, ALU.subtract).then_inc(S["q_ready"], 1)
                                dve.wait_ge(S["kh_ready"], s + 1)
                                for g in (1, 3):
                                    k_ = kop[g * G32:(g + 1) * G32, s * CHUNK:(s + 1) * CHUNK]
                                    ins = stt(k_, psum[g * G32:(g + 1) * G32, bC, :], bias[g * G32:(g + 1) * G32, KB:KB + 1], k_.bitcast(F32),
                                              ALU.add, ALU.subtract)
                                    ins.then_inc(S["k_ready"], 1) if g == 3 else ins
                            if u == 26 and s + 2 < CHUNKS:
                                c1_low(s + 2)
                    if s < CHUNKS:
                        n = score_base(s) + (4 * s if valid(cm) else 0)
                        dve.wait_ge(S["s_filled"], n + 1)
                        src = psum[:, bS + n % 2, 0:TILES * G32].rearrange("p (t d) -> p t d", d=G32)[:, :, 0:DV]
                        tt(vaug[:, s * TILES:(s + 1) * TILES, 0:DV], src, bv_rep[:], ALU.add).then_inc(S["v_ready"], 1)
                        dve.wait_ge(S["v_ready"], s + 1)
                        dve.sem_inc(S["s_drained"], 1)
                    if valid(cm):
                        dve.wait_ge(S["s_drained"], n_drained(s))
                        if cm >= 1:
                            dve.wait_ge(S["mrep_mm"], cm)
                        nc.vector.tensor_reduce(mneg[:, 0, :], mpart[:, :, 0:cm + 1], AX.X, ALU.max).then_inc(S["max_ready"], 1)
                        dve.wait_ge(S["max_ready"], cm + 1)
                        ts(mneg[:, 1, :], mneg[:, 0, :], -1.0, 1e9, ALU.mult, ALU.min).then_inc(S["mfin"], 1)
                        dve.wait_ge(S["mfin"], cm + 1)
                        for t in range(TILES):
                            ins = ts(mdiag[:, t, :], ident[:], mneg[:, 1, t:t + 1], None, ALU.mult)
                        ins.then_inc(S["diag_ready"], 1)
                    if valid(ce):
                        dve.wait_ge(S["att_h"], ce + 1)
                        tt(attl[:], psum[:, bP, :], atth[:].bitcast(F32), ALU.subtract).then_inc(S["att_l"], 1)
                for g in range(1, GROUPS, 2):
                    dve.wait_ge(S["a_mm"], g + 1)
                    nc.vector.tensor_copy(XT[:, g * CHUNK:(g + 1) * CHUNK], psum[:, g % 4, :]).then_inc(S["xt_dve"], 1)
                spatial_layer(0, G1)
                for g in range(GROUPS):
                    dve.wait_ge(S["pth_ready"], g + 1)
                    gs = slice(g * CHUNK, (g + 1) * CHUNK)
                    tt(TL[:, gs], psum[:, g % 4, :], TH[:, gs].bitcast(F32), ALU.subtract).then_inc(S["ptl_ready"], 1)
                    nc.vector.tensor_reduce(rpart[:, g, :], psum[:, g % 4, :].rearrange("p (h c r) -> p c h r", h=H2G, r=R), AX.XY, ALU.add).then_inc(S["p_sum"], 1)
                dve.wait_ge(S["p_sum"], GROUPS)
                nc.vector.tensor_reduce(rsum[:], rpart[:, :, :].rearrange("p g c -> p c g"), AX.X, ALU.add).then_inc(S["rs_ready"], 1)
                rs_row = bcast_mid(rs2, H2G)
                dve.wait_ge(S["rs_ready"], 3)
                for g in range(GROUPS + 2):
                    if g < GROUPS:
                        o = 4 * (g % 2)
                        dve.wait_ge(S["lr_mm"], g + 1)
                        if g >= 2:
                            dve.wait_ge(S["g_ready"], g - 1)
                        stt(ug[:, g % 2].rearrange("p (h i) -> p h i", h=H2G), psum[:, o, :].rearrange("p (h i) -> p h i", h=H2G),
                            bias[:, BL:BL + 1], rs_row, ALU.add, ALU.mult).then_inc(S["u_ready"], 1)
                        dve.wait_ge(S["u_ready"], g + 1)
                        dve.wait_ge(S["sg_ready"], g + 1)
                        if g >= 2:
                            dve.wait_ge(S["gl_ready"], g - 1)
                        stt(gg[:, g % 2], sg[:, g % 2], 1.0, ug[:, g % 2], ALU.add, ALU.mult).then_inc(S["g_ready"], 1)
                    if g >= 2:
                        f = g - 2
                        dve.wait_ge(S["ot_mm"], f + 1)
                        z = XT[:, f * CHUNK:(f + 1) * CHUNK]
                        tt(z, psum[:, 4 * (f % 2) + 3, :], z, ALU.add).then_inc(S["z2_ready"], 1)
                        dve.wait_ge(S["z2_ready"], f + 1)
                        for h in range(H2G):
                            ins = nc.vector.bn_stats(st[:, f % 2, h, :], z[:, h * C:(h + 1) * C])
                        ins.then_inc(S["st_ready"], 1)
                        dve.wait_ge(S["st_ready"], 2 * f + 1)
                        if f >= 2:
                            dve.wait_ge(S["rstd_ready"], f - 1)
                        for h in range(H2G):
                            ins = nc.vector.bn_aggr(mv[:, f % 2, h, :], st[:, f % 2, h, :])
                        ins.then_inc(S["st_ready"], 1)
                        dve.wait_ge(S["rstd_ready"], f + 1)
                        for h in range(H2G):
                            zh = z[:, h * C:(h + 1) * C]
                            ins = ts(zh, zh, mv[:, f % 2, h, 0:1], rstd[:, f % 2, h:h + 1], ALU.subtract, ALU.mult)
                        ins.then_inc(S["centred_ready"], 1)
                spatial_layer(1, G3)
                dve.wait_ge(S["x_dve"], 8)
                dve.sem_inc(arrived, 1)
                dve.wait_ge(go, b + 1)
                dve.sem_inc(passed, 1)

        @block.gpsimd
        def _(gp):
            tt, ts, ms, sel = nc.gpsimd.tensor_tensor, nc.gpsimd.tensor_scalar, nc.gpsimd.memset, nc.gpsimd.affine_select
            count = [0]

            def link(ins):
                ins.then_inc(pool_set, 1)
                count[0] += 1

            def hold():
                gp.wait_ge(pool_set, count[0])
            sq = res[:, TAPS * C:TAPS * C + 7 * C]
            link(ms(sq, 0.0))
            link(ms(planes_w3(res), 0.0))
            link(ms(bias[:], 0.0))
            link(ms(wv32[:], 0.0))
            assert count[0] == POOL_CLEARED
            for t in (ident, identb, sel_den32, sel_max, mask_q, mask_k):
                link(ms(t[:], 0.0))
            link(ms(ones[:], 1.0))
            link(ms(half[:], -0.5))
            link(ms(vaug[:], 0.0))
            hold()
            link(ms(vaug[:, :, DV:DV + 1], 1.0))
            for t in (ident, identb):
                link(sel(out=t[:], in_=t[:], compare_op=ALU.not_equal, fill=1.0, base=0, pattern=[[-1, P]], channel_multiplier=1))
            for g in range(4):
                link(sel(out=sel_den32[:], in_=sel_den32[:], compare_op=ALU.not_equal, fill=1.0, base=-(g * G32 + DV),
                         pattern=[[0, P]], channel_multiplier=1))
                hold()
            for col in (0, 64):
                link(ms(sel_max[:, col:col + 1], 1.0))
            link(sel(out=mask_q[:], in_=mask_q[:], compare_op=ALU.is_gt, fill=NEG, base=0, pattern=[[-1, P]], channel_multiplier=1))
            link(sel(out=mask_k[:], in_=mask_k[:], compare_op=ALU.is_gt, fill=NEG, base=-3 * P, pattern=[[1, CHUNK + 3 * P]], channel_multiplier=-1))
            hold()
            assert count[0] == POOL_SET, count[0]

            def image(plane, c):
                return plane[:, 1 + c * ROWS:1 + (c + 1) * ROWS, 1:1 + W]

            def elu_low(c):
                gp.wait_ge(S["xeh_ready"], c + 1)
                tt(image(xel, c), ebuf[:, c % 2].rearrange("p (r w) -> p r w", w=W), image(xeh, c).bitcast(F32), ALU.subtract).then_inc(S["xe_ready"], 1)

            def spatial_layer(y):
                gp.wait_ge(S["sq_ready"], 16 * (y + 1))
                tt(rd[:], d2[:], half[:], ALU.pow).then_inc(S["rd_ready"], 1)
                for n in range(8):
                    gp.wait_ge(S["xnh_ready"], 8 * y + n + 1)
                    xs = slice((n // 2) * CHUNK, (n // 2 + 1) * CHUNK)
                    tt(XNL[:, n % 2, xs], ebuf[:, n % 2], XNH[:, n % 2, xs].bitcast(F32), ALU.subtract).then_inc(S["xnl_ready"], 1)
                for q in range(4):
                    gp.wait_ge(S["scaled_ready"], 8 * y + 2 * q + 1)
                    t = stash[:, q] if q < 2 else scaled[:, q - 2]
                    xv = XTv[:, 0, q * CHUNK:(q + 1) * CHUNK]
                    tt(xv, t, xv, ALU.add).then_inc(S["x_pool"], 1)

            with gp.Fori(0, B) as b:
                for i in range(4):
                    pl = planes[:, i * IMG:(i + 1) * IMG].bitcast(F32)
                    ms(pl[:, 0:WP + 1], 0.0).then_inc(S["pads"], 1)
                    ms(pl[:, WP + 1 + W:WP + 1 + W + (H - 1) * WP].rearrange("p (r c) -> p r c", c=WP)[:, :, 0:2], 0.0).then_inc(S["pads"], 1)
                    ms(pl[:, (H + 1) * WP - 1:IMG], 0.0).then_inc(S["pads"], 1)
                gp.wait_ge(S["pads"], PADS)
                for c in range(4):
                    elu_low(c)
                for s in range(CHUNKS + 3):
                    cy = s - 3
                    if valid(cy):
                        gp.wait_ge(S["z_ready"], cy + 1)
                        r_ = res_chunk(res, cy)
                        tt(r_, split_w(zbuf[:]), r_, ALU.add).then_inc(S["y_ready"], 1)
                    if s + 4 < CHUNKS:
                        elu_low(s + 4)
                    if s < CHUNKS:
                        gp.wait_ge(S["c3h_ready"], s + 1)
                        if s >= 1:
                            gp.wait_ge(S["qk_mm"], s)
                        tt(c3l[:], c3[:], c3h[:].bitcast(F32), ALU.subtract).then_inc(S["c3l_ready"], 1)
                        r_ = res_chunk(res, s)
                        gp.wait_ge(S["res_ready"], s + 1)
                        tt(r_, r_, split_w(c3[:]), ALU.add).then_inc(S["res_added"], 1)
                spatial_layer(0)
                for g in range(GROUPS + 2):
                    if g < GROUPS:
                        gp.wait_ge(S["gh_ready"], g + 1)
                        if g >= 2:
                            gp.wait_ge(S["o_mm"], g - 1)
                        tt(Gl[:, g % 2], gg[:, g % 2], Gh[:, g % 2].bitcast(F32), ALU.subtract).then_inc(S["gl_ready"], 1)
                    if g >= 2:
                        f = g - 2
                        gp.wait_ge(S["st_ready"], 2 * f + 2)
                        if f >= 2:
                            gp.wait_ge(S["centred_ready"], f - 1)
                        ts(rstd[:, f % 2], mv[:, f % 2, :, 1], EPS_L, None, ALU.add).then_inc(S["eps_ready"], 1)
                        gp.wait_ge(S["eps_ready"], f + 1)
                        tt(rstd[:, f % 2], rstd[:, f % 2], half[:, 0:1].to_broadcast([P, H2G]), ALU.pow).then_inc(S["rstd_ready"], 1)
                        gp.wait_ge(S["centred_ready"], f + 1)
                        z = XT[:, f * CHUNK:(f + 1) * CHUNK].rearrange("p (h k) -> p h k", k=C)
                        tt(z, z, bcast_mid(ln_s, H2G), ALU.mult).then_inc(S["m_step"], 1)
                        gp.wait_ge(S["m_step"], f + 1)
                        tt(z, z, bcast_mid(ln_b, H2G), ALU.add).then_inc(S["ln_ready"], 1)
                spatial_layer(1)
                gp.wait_ge(S["x_pool"], 8)
                gp.wait_ge(arrived, 4 * b + 4)
                gp.sem_inc(passed, 1)
                for s_ in loop_sems:
                    gp.sem_clear(s_)
                gp.sem_inc(go, 1)


POOL_CLEARED = 4
POOL_SET = 4 + 6 + 3 + 1 + 2 + 4 + 2 + 2
ACT_SET = 4
DVE_FOLDED = 11
DVE_SET = 14
PADS = 12
W_LOADS = 16 * (2 + 5 * 4 + 4 + 2 + 7 + 2 + 2 + 4 + 2)


def n_drained(s):
    return score_base(s + 1)


def res_chunk(res, c):
    return res[:, :].rearrange("p (h c r) -> p c h r", c=H, r=R)[:, c * ROWS:(c + 1) * ROWS]


def split_w(t):
    return t.rearrange("p (c h r) -> p c h r", c=ROWS, r=R)


def planes_w3(res):
    o = TAPS * C + 7 * C
    return res[:, o:o + HEADS * C].rearrange("p (h o) -> p h o", o=C)


def bcast(v, p, n):
    return bass.AP(tensor=v.tensor, offset=v.offset, ap=[[0, p], [1, n]])


def bcast_mid(t, k):
    full = t[:, :, :].rearrange("p c r -> p (c r)") if len(t.shape) == 3 else t[:, :]
    return full.unsqueeze(1).to_broadcast([P, k, P])


_INS = ["x", "L0_conv_W1", "L0_conv_b1", "L0_conv_W2", "L0_conv_b2", "L0_conv_Wq", "L0_conv_bq", "L0_conv_Wk", "L0_conv_bk",
        "L0_conv_Wv", "L0_conv_bv", "L0_conv_W3", "L0_conv_b3", "L1_conv_gamma", "L2_conv_W_left", "L2_conv_b_left",
        "L2_conv_W_right", "L2_conv_b_right", "L2_conv_W_gate", "L2_conv_b_gate", "L2_conv_W_eq", "L2_conv_b_eq",
        "L2_conv_W_out", "L2_conv_b_out", "L2_conv_ln_scale", "L2_conv_ln_bias", "L3_conv_gamma"]


def kernel(**inputs):
    import concourse.bacc as bacc
    from concourse.bass_utils import run_bass_kernel_spmd

    nc = bacc.Bacc("TRN2", target_bir_lowering=False, num_devices=1)
    arrays, args = {}, []
    for name in _INS:
        a = np.ascontiguousarray(inputs[name])
        arrays["in_" + name] = a
        args.append(nc.dram_tensor("in_" + name, a.shape, mybir.dt.from_np(a.dtype), kind="ExternalInput").ap())
    args.append(nc.dram_tensor("out_x", (B, H, W, C), F32, kind="ExternalOutput").ap())
    build_program(nc, *args)
    r = run_bass_kernel_spmd(nc, [arrays], core_ids=[0])
    return r.results[0]["out_x"]
```

```python
import numpy as np
import concourse.bass as bass
from concourse import mybir
from contextlib import ExitStack

F32 = mybir.dt.float32
F32R = mybir.dt.float32r
BF16 = mybir.dt.bfloat16
ALU = mybir.AluOpType
ACT = mybir.ActivationFunctionType
AX = mybir.AxisListType

B, H, W, C = 4, 64, 64, 128
N = H * W
P = 128
DQK, DV, HEADS = 4, 16, 8
CHUNK = 512
CHUNKS = N // CHUNK
ROWS = CHUNK // W
TILES = CHUNK // P
TAPS = 9
STEPS = 3 * TAPS
HP, WP = H + 2, W + 2
NEG = -1e10
EPS_L = 1e-5
R = 2
GROUPS = 8
H2G = 4
NPOS = N // 2
KT = NPOS // P
IHALF = NPOS // 2
G32 = 32


def share(n, u, steps, first=0):
    if u < first:
        return range(0)
    return range(n * (u - first) // (steps - first), n * (u - first + 1) // (steps - first))


def valid(c):
    return 0 <= c < CHUNKS


def score_base(s):
    return sum((4 * t if valid(t - 1) else 0) + (1 if valid(t) else 0) for t in range(s))


def exp_base(c):
    return 2 * c * (c + 1)


def pv_base(c):
    return c * (c + 1) // 2


def pair_slots():
    order = [("a", 0, i) for i in range(4)]
    for y in range(2):
        for ih in range(2):
            for j in range(KT):
                order.append(("e", y, KT * ih + j))
                kind, i = EXTRA.get((ih, j), (None, 0))
                if kind and not (kind == "pt" and y == 1):
                    order.append((kind, y, i))
        order.append(("z", y, 1))
        if y == 0:
            order += [("pt", 0, 2), ("pt", 0, 3)] + [("lg", 0, g) for g in range(GROUPS)]
    return order


EXTRA = {(0, 0): ("qt", 2), (0, 2): ("qt", 3), (0, 5): ("rd", 1), (1, 9): ("z", 0), (1, 11): ("pt", 0), (1, 13): ("pt", 1)}
ORDER = pair_slots()
PAIR = {item: 2 * (n % 2) for n, item in enumerate(ORDER)}
BEFORE = {item: ORDER[n - 2] if n >= 2 else None for n, item in enumerate(ORDER)}


def build_program(nc, x, W1, b1, W2, b2, Wq, bq, Wk, bk, Wv, bv, W3, b3, gamma1,
                  Wleft, bleft, Wright, bright, Wgate, bgate, Weq, beq, Wout, bout, ln_scale, ln_bias, gamma3, out):
    ctx = ExitStack()
    with ctx:
        def sb(name, shape, dt=F32):
            return ctx.enter_context(nc.sbuf_tensor(name, shape, dt))

        def sem(name):
            return ctx.enter_context(nc.semaphore(name))

        w1h, w1l = sb("w1h", [P, TAPS, C], F32R), sb("w1l", [P, TAPS, C], F32R)
        w2h, w2l = sb("w2h", [P, TAPS, 2 * C], F32R), sb("w2l", [P, TAPS, 2 * C], F32R)
        sqh, sql = sb("sqh", [P, 6, C], F32R), sb("sql", [P, 6, C], F32R)
        Q_, K_, M_, L_, G_, O_ = range(6)
        wv32 = sb("wv32", [P, G32])
        wright = sb("wright", [P, C])
        ident, ones = sb("ident", [P, P]), sb("ones", [P, P])
        identb = sb("identb", [P, P], BF16)
        sel_den = sb("sel_den", [P, P], F32R)
        sel_den32 = sb("sel_den32", [P, P])
        sel_max = sb("sel_max", [P, P])
        mask_q = sb("mask_q", [P, P], BF16)
        mask_k = sb("mask_k", [P, CHUNK + 3 * P], BF16)
        half = sb("half", [P, KT])
        NB = 13
        bias = sb("bias", [P, NB])
        B1, B2A, B2B, B3, QB, KB, BL, BG, BR, BO, G1, G3, BE = range(NB)
        bv_rep = sb("bv_rep", [P, TILES, DV])
        ln_s, ln_b = sb("ln_s", [P, C]), sb("ln_b", [P, C])

        xin = sb("xin", [P, 4, TILES, C])
        ebuf = sb("ebuf", [P, 2, CHUNK])
        th, ah, c3 = sb("th", [P, CHUNK]), sb("ah", [P, CHUNK]), sb("c3", [P, CHUNK])
        c3h, c3l = sb("c3h", [P, CHUNK], F32R), sb("c3l", [P, CHUNK], F32R)
        qop = sb("qop", [P, 3, CHUNK], F32R)
        atth, attl = sb("atth", [P, CHUNK], F32R), sb("attl", [P, CHUNK], F32R)
        rden = sb("rden", [P, CHUNK])
        zbuf = sb("zbuf", [P, CHUNK])
        mpart = sb("mpart", [P, TILES, CHUNKS])
        mneg = sb("mneg", [P, 2, TILES])
        mdiag = sb("mdiag", [P, TILES, P])
        vaug = sb("vaug", [P, CHUNKS * TILES, G32])
        IMG = HP * WP
        planes = sb("planes", [P, 4 * IMG + 8], F32R)
        kop = sb("kop", [P, N], F32R)
        xeh, xel, c1h, c1l = [planes[:, i * IMG:(i + 1) * IMG].rearrange("p (r c) -> p r c", c=WP) for i in range(4)]
        XH, XL, TH, TL = [planes[:, i * N:(i + 1) * N] for i in range(4)]
        res = sb("res", [P, N])
        prob = sb("prob", [P, 8, CHUNK])
        d2, rd, gz = sb("d2", [P, KT]), sb("rd", [P, KT]), sb("gz", [P, KT])
        zsum = sb("zsum", [P, 2, KT])
        square = [t[:, i * 2 * P:(i + 1) * 2 * P] for t in (c3, th) for i in range(2)]
        rpart = rden[:, :].rearrange("p (g c) -> p g c", c=H)
        xn = [ebuf[:, 0], ebuf[:, 1], ah[:, :], rden[:, :]]
        diag = [mdiag[:, :, :], zbuf[:, :].rearrange("p (k n) -> p k n", n=P)]
        rsum = sb("rsum", [P, H]); rs2 = sb("rs2", [P, H, 2])
        st = sb("st", [P, 2, H2G, 6]); mv = sb("mv", [P, 2, H2G, 2]); rstd = sb("rstd", [P, 2, H2G])
        psum = ctx.enter_context(nc.psum_tensor("psum", [P, 8, CHUNK], F32))
        XT = prob[:, :, :].rearrange("p a n -> p (a n)")
        XTv = XT.rearrange("p (n r) -> p r n", r=R)
        XNH, XNL = [planes[:, i * N:(i + 1) * N].rearrange("p (r n) -> p r n", r=R) for i in range(2)]
        TH, TL = [planes[:, i * N:(i + 1) * N] for i in (2, 3)]
        QTh, QTl = [t.rearrange("p (k i) -> p k i", i=2 * P) for t in (TH, TL)]
        Ph = kop[:, 0:2 * IHALF].rearrange("p (a n) -> p a n", a=2)
        Pl = kop[:, 2 * IHALF:4 * IHALF].rearrange("p (a n) -> p a n", a=2)
        stash = res[:, 0:NPOS].rearrange("p (q n) -> p q n", n=CHUNK)
        pexp = res[:, NPOS:2 * NPOS].rearrange("p (a n) -> p a n", a=2)
        scaled = res[:, NPOS:2 * NPOS].rearrange("p (q n) -> p q n", n=CHUNK)
        Gh = kop[:, 0:2 * CHUNK].rearrange("p (a n) -> p a n", a=2)
        Gl = kop[:, 2 * CHUNK:4 * CHUNK].rearrange("p (a n) -> p a n", a=2)
        sg, ug, gg, oT = [res[:, i * 2 * CHUNK:(i + 1) * 2 * CHUNK].rearrange("p (a n) -> p a n", a=2) for i in range(4)]

        bA, bB, bC, bS, bT, bP = 0, 1, 2, 3, 5, 7
        t_bank = {0: bA, 1: bB, 2: bC}
        c1_bank = {0: bB, 1: bC}

        w_loaded, w_stage1, w_stage2 = sem("w_loaded"), sem("w_stage1"), sem("w_stage2")
        pool_set, dve_set, act_set = sem("pool_set"), sem("dve_set"), sem("act_set")
        arrived, go = sem("arrived"), sem("go")
        passed = sem("passed")
        names = """pads x_transposed elu_min elu_exp res_ready elu_read xeh_ready xe_ready c1_mm c1h_ready c1_ready
            gate_mm value_mm th_ready ah_ready c3_ready c3h_ready c3l_ready res_added qk_mm qh_ready kh_ready q_ready k_ready
            s_filled s_drained v_ready max_ready diag_ready mrep_mm mrow_h mrow_ready t_filled exp_done pv_done att_h att_l
            den_mm mh_mm den_added den_inv z_ready y_ready m_step
            a_mm xt_act xt_dve qt_mm qth_ready sq_ready qtl_ready rd_ready rdiag_ready rdrow_mm xn_ready xnh_ready xnl_pool xnl_dve
            e_mm p_ready ph_ready pl_ready ap_mm stash_act stash_dve gz_step zdiag_ready zrow_mm zrow_copied scaled_ready x_pool x_dve
            p_mm pth_ready p_sum rs_mm rs_ready lr_mm gt_mm sg_ready u_ready g_ready gh_ready gl_ready o_mm ot_ready ot_mm z2_ready
            st_ready eps_ready rstd_ready centred_ready ln_ready mfin""".split()
        S = {n: sem(n) for n in names}
        x_loaded = [sem(f"x_loaded{i}") for i in range(4)]
        out_sent = sem("out_sent")
        loop_sems = list(S.values()) + x_loaded + [out_sent]

        block = ctx.enter_context(nc.Block())

        @block.sync
        def _(sp):
            n = 0
            def load(dst, src):
                nonlocal n
                sp.dma_start(dst, src).then_inc(w_loaded, 16)
                n += 16
            stage1 = res[:, 0:TAPS * C]
            stage2 = prob[:, :, :].rearrange("p a n -> p (a n)")[:, 0:TAPS * 2 * C]
            sp.wait_ge(pool_set, POOL_CLEARED)
            load(stage1.rearrange("p (t o) -> p t o", o=C), W1.rearrange("a b i o -> i (a b) o"))
            load(stage2.rearrange("p (t o) -> p t o", o=2 * C), W2.rearrange("a b i o -> i (a b) o"))
            sq = res[:, TAPS * C:TAPS * C + 7 * C].rearrange("p (s o) -> p s o", o=C)
            for g in range(4):
                load(sq[:, 0, g * G32 + 1:g * G32 + 1 + DQK], Wq)
                load(sq[:, 1, g * G32 + 1:g * G32 + 1 + DQK], Wk)
                load(bias[g * G32 + 1:g * G32 + 1 + DQK, QB:QB + 1], bq.rearrange("(d o) -> d o", o=1))
                load(bias[g * G32 + 1:g * G32 + 1 + DQK, KB:KB + 1], bk.rearrange("(d o) -> d o", o=1))
                load(planes_w3(res)[g * G32:g * G32 + DV], W3.rearrange("(h d) o -> d h o", d=DV))
            load(sq[:, 3, :], Wleft)
            load(sq[:, 4, :], Wgate)
            load(sq[:, 5, :], Wout)
            load(sq[:, 6, :], Weq)
            load(wv32[:, 0:DV], Wv)
            load(wright[:], Wright)
            for col, v in ((B1, b1), (B3, b3), (BL, bleft), (BG, bgate), (BR, bright), (BO, bout), (BE, beq)):
                load(bias[:, col:col + 1], v.rearrange("(c o) -> c o", o=1))
            load(bias[:, B2A:B2A + 1], b2[0:C].rearrange("(c o) -> c o", o=1))
            load(bias[:, B2B:B2B + 1], b2[C:2 * C].rearrange("(c o) -> c o", o=1))
            load(bias[:, G1:G1 + 1], bcast(gamma1, P, 1))
            load(bias[:, G3:G3 + 1], bcast(gamma3, P, 1))
            for t in range(TILES):
                load(bv_rep[:, t, :], bcast(bv, P, DV))
            load(ln_s[:], bcast(ln_scale, P, C))
            load(ln_b[:], bcast(ln_bias, P, C))
            assert n == W_LOADS, n
            with sp.Fori(0, B) as b:
                xb = x[b].rearrange("r w c -> (r w) c").rearrange("(k t p) c -> k p t c", t=TILES, p=P)
                for c in range(CHUNKS):
                    if c >= 4:
                        sp.wait_ge(S["x_transposed"], c - 3)
                    sp.dma_start(xin[:, c % 4], xb[c]).then_inc(x_loaded[c % 4], 16)
                ob = out[b].rearrange("c (g h r) k -> g r c h k", r=R, h=8)
                for g in range(4):
                    sp.wait_ge(S["x_pool"], 4 + g + 1)
                    sp.wait_ge(S["x_dve"], 4 + g + 1)
                    for r1 in range(R):
                        src = XT[r1:P:R, g * 8 * C:(g + 1) * 8 * C].rearrange("p (h k) -> p h k", k=C)
                        sp.dma_start(ob[g, r1], src).then_inc(out_sent, 16)
                sp.wait_ge(out_sent, 4 * R * 16)
                sp.sem_inc(arrived, 1)
                sp.wait_ge(go, b + 1)
                sp.sem_inc(passed, 1)

        @block.tensor
        def _(pe):
            mm, tr = nc.tensor.matmul, nc.tensor.transpose

            def three(o, wh, wl, xh, xl, start, stop):
                mm(o, wh, xh, start=start, stop=False)
                mm(o, wh, xl, start=False, stop=False)
                return mm(o, wl, xh, start=False, stop=stop)

            def transpose_x(c):
                pe.wait_ge(x_loaded[c % 4], 16 * (c // 4 + 1))
                bank = t_bank.get(c, bA)
                if c == 3:
                    pe.wait_ge(S["elu_read"], 1)
                    pe.wait_ge(S["res_ready"], 1)
                elif c == 4:
                    pe.wait_ge(S["elu_read"], 4)
                elif c > 4:
                    pe.wait_ge(S["c1_ready"], c - 2)
                for t in range(TILES):
                    last = tr(psum[:, bank, t * P:(t + 1) * P], xin[:, c % 4, t, :], ident[:])
                last.then_inc(S["x_transposed"], 1)

            def conv1_tap(c, tap):
                bank = c1_bank.get(c, bA)
                if tap == 0:
                    pe.wait_ge(S["xe_ready"], min(c + 2, CHUNKS))
                    if c >= 2:
                        pe.wait_ge(S["elu_read"], min(c + 3, CHUNKS))
                        if c >= 3:
                            pe.wait_ge(S["c1_ready"], c)
                dy, dx = divmod(tap, 3)
                r0 = c * ROWS + dy
                last = three(psum[:, bank, :], w1h[:, tap, :], w1l[:, tap, :],
                             xeh[:, r0:r0 + ROWS, dx:dx + W], xel[:, r0:r0 + ROWS, dx:dx + W], tap == 0, tap == TAPS - 1)
                if tap == TAPS - 1:
                    last.then_inc(S["c1_mm"], 1)

            def conv2_tap(c, tap, gate):
                bank = bB if gate else bC
                if tap == 0 and gate:
                    pe.wait_ge(S["c1_ready"], min(c + 2, CHUNKS))
                    if c >= 1:
                        pe.wait_ge(S["q_ready"], c)
                if tap == 0 and not gate and c >= 1:
                    pe.wait_ge(S["k_ready"], c)
                dy, dx = divmod(tap, 3)
                r0 = c * ROWS + dy
                o = C if gate else 0
                last = three(psum[:, bank, :], w2h[:, tap, o:o + C], w2l[:, tap, o:o + C],
                             c1h[:, r0:r0 + ROWS, dx:dx + W], c1l[:, r0:r0 + ROWS, dx:dx + W], tap == 0, tap == TAPS - 1)
                if tap == TAPS - 1:
                    last.then_inc(S["gate_mm" if gate else "value_mm"], 1)

            def project(c):
                pe.wait_ge(S["c3h_ready"], c + 1)
                pe.wait_ge(S["c3l_ready"], c + 1)
                three(psum[:, bB, :], sqh[:, Q_, :], sql[:, Q_, :], c3h[:], c3l[:], True, True)
                three(psum[:, bC, :], sqh[:, K_, :], sql[:, K_, :], c3h[:], c3l[:], True, True).then_inc(S["qk_mm"], 1)

            def project_values(c):
                i = score_base(c) + (4 * c if valid(c - 1) else 0)
                if i >= 2:
                    pe.wait_ge(S["s_drained"], i - 1)
                for t in range(TILES):
                    last = mm(psum[:, bS + i % 2, t * G32:(t + 1) * G32], c3[:, t * P:(t + 1) * P], wv32[:], start=True, stop=True)
                last.then_inc(S["s_filled"], 1)

            def score_tile(c, i):
                t, kc = divmod(i, c + 1)
                n = score_base(c + 1) + i
                if i == 0:
                    pe.wait_ge(S["q_ready"], c + 1)
                    pe.wait_ge(S["k_ready"], c + 1)
                if n >= 2:
                    pe.wait_ge(S["s_drained"], n - 1)
                bank = bS + n % 2
                diag = kc == c
                width = (t + 1) * P if diag else CHUNK
                if diag:
                    mm(psum[:, bank, t * P:width], identb[:], mask_q[:], start=True, stop=False, skip_group_check=True)
                mm(psum[:, bank, 0:width], qop[:, c % 3, t * P:(t + 1) * P], kop[:, kc * CHUNK:kc * CHUNK + width],
                   start=not diag, stop=True, skip_group_check=diag).then_inc(S["s_filled"], 1)

            def max_rows(c):
                pe.wait_ge(S["diag_ready"], c + 1)
                if c >= 1:
                    pe.wait_ge(S["den_added"], c)
                mm(psum[:, bT, :], sel_max[:], mdiag[:, :, :], start=True, stop=True).then_inc(S["mrep_mm"], 1)

            def exp_tile(c, j):
                e = exp_base(c) + j
                if j == 0:
                    pe.wait_ge(S["mrow_ready"], c + 1)
                elif j == 1:
                    if c >= 1:
                        pe.wait_ge(S["z_ready"], c)
                else:
                    pe.wait_ge(S["exp_done"], e - 1)
                bank = bT + j % 2
                diag = j >= TILES * c
                last = mm(psum[:, bank, :], kop[:, j * P:(j + 1) * P], qop[:, c % 3, :], start=True, stop=not diag)
                if diag:
                    r = j - TILES * c
                    o = (TILES - 1 - r) * P
                    last = mm(psum[:, bank, :], identb[:], mask_k[:, o:o + CHUNK], start=False, stop=True)
                last.then_inc(S["t_filled"], 1)

            def attend(c, g):
                if g == 0:
                    pe.wait_ge(S["v_ready"], c + 1)
                    if c >= 1:
                        pe.wait_ge(S["att_l"], c)
                pe.wait_ge(S["exp_done"], exp_base(c) + 4 * g + 4)
                for q in range(4):
                    j = 4 * g + q
                    last = mm(psum[q * G32:(q + 1) * G32, bP, :], vaug[:, j, :], prob[:, (exp_base(c) + j) % 8, :],
                              start=g == 0, stop=g == c, tile_position=(0, q * G32))
                last.then_inc(S["pv_done"], 1)

            def attention_out(c):
                pe.wait_ge(S["att_l"], c + 1)
                pe.wait_ge(S["exp_done"], exp_base(c + 1))
                mm(psum[:, bT, :], sel_den[:], atth[:], start=True, stop=False)
                mm(psum[:, bT, :], sel_den[:], attl[:], start=False, stop=True).then_inc(S["den_mm"], 1)
                three(psum[:, bT + 1, :], sqh[:, M_, :], sql[:, M_, :], atth[:], attl[:], True, True).then_inc(S["mh_mm"], 1)

            def pair_free(item):
                kind, y, i = BEFORE[item] or (None, 0, 0)
                if kind == "e":
                    pe.wait_ge(S["p_ready"], 2 * KT * y + i + 1)
                elif kind == "a":
                    pe.wait_ge(S["xt_act"], i + 1)
                    pe.wait_ge(S["xt_dve"], i + 1)
                elif kind == "qt":
                    pe.wait_ge(S["qtl_ready"], 8 * y + 2 * i + 2)
                elif kind == "rd":
                    pe.wait_ge(S["xn_ready"], 8 * (y + 1))
                elif kind == "z" and i == 0:
                    pe.wait_ge(S["scaled_ready"], 8 * y + 4)
                elif kind == "z":
                    pe.wait_ge(S["zrow_copied"], 2 * (y + 1))
                elif kind == "pt":
                    pe.wait_ge(S["p_sum"], 2 * i + 2)
                elif kind == "lg":
                    pe.wait_ge(S["u_ready"], i + 1)
                    pe.wait_ge(S["sg_ready"], i + 1)
                return PAIR[item]

            def token_tiles(i):
                pair = pair_free(("a", 0, i))
                for g in (2 * i, 2 * i + 1):
                    for h in range(H2G):
                        src = res[:, (H2G * g + h) * P:(H2G * g + h + 1) * P]
                        last = tr(psum[:, pair + g % 2, h * P:(h + 1) * P], src, ident[:])
                    last.then_inc(S["a_mm"], 1)

            def positions(y, kk, bank):
                if y == 0:
                    pe.wait_ge(S["xt_dve" if kk % 2 else "xt_act"], kk // 2 + 1)
                else:
                    pe.wait_ge(S["ln_ready"], kk + 1)
                for k in range(2):
                    for r2 in range(R):
                        last = tr(psum[:, bank, (2 * k + r2) * P:(2 * k + r2 + 1) * P],
                                  XTv[:, r2, (2 * kk + k) * P:(2 * kk + k + 1) * P], ident[:])
                last.then_inc(S["qt_mm"], 1)

            def inverse_norms(y, q0, bank):
                pe.wait_ge(S["rdiag_ready"], 2 * y + q0 // 2 + 1)
                for q in (q0, q0 + 1):
                    mm(psum[:, bank + q % 2, :], ones[:], diag[q % 2], start=True, stop=True).then_inc(S["rdrow_mm"], 1)

            def scales(y, i):
                pe.wait_ge(S["zdiag_ready"], 2 * y + i + 1)
                pair = pair_free(("z", y, i))
                for q in range(2):
                    mm(psum[:, pair + q, :], ones[:], diag[q], start=True, stop=True).then_inc(S["zrow_mm"], 1)

            def pair_transposed(i):
                pair = pair_free(("pt", 0, i))
                pe.wait_ge(S["x_pool"], i + 1)
                pe.wait_ge(S["x_dve"], i + 1)
                for g in (2 * i, 2 * i + 1):
                    for h in range(H2G):
                        last = tr(psum[:, pair + g % 2, h * P:(h + 1) * P], XT[:, (H2G * g + h) * C:(H2G * g + h + 1) * C], ident[:])
                    last.then_inc(S["p_mm"], 1)

            def spatial_layer(y):
                for ih in range(2):
                    for j in range(KT + 2):
                        if j < KT:
                            energy(y, ih, j)
                            kind, i = EXTRA.get((ih, j), (None, 0))
                            if kind == "qt":
                                pair = pair_free(("qt", y, i))
                                positions(y, 2 * i, pair)
                                positions(y, 2 * i + 1, pair + 1)
                            elif kind == "rd":
                                inverse_norms(y, 2, pair_free(("rd", y, 1)))
                            elif kind == "z":
                                scales(y, 0)
                            elif kind == "pt" and y == 0:
                                pair_transposed(i)
                        elif ih == 1 and j == KT + 1:
                            scales(y, 1)
                        if j >= 2:
                            apply(y, ih, j - 2)

            def energy(y, ih, j):
                pair = pair_free(("e", y, KT * ih + j))
                if ih == 0 and j in (0, KT // 2):
                    pe.wait_ge(S["xnl_pool"], 4 * y + (4 if j else 2))
                    pe.wait_ge(S["xnl_dve"], 4 * y + (4 if j else 2))
                for q in range(2):
                    i0 = ih * IHALF + q * CHUNK
                    for r in range(R):
                        last = three(psum[:, pair + q, :], XNH[:, r, j * P:(j + 1) * P], XNL[:, r, j * P:(j + 1) * P],
                                     XNH[:, r, i0:i0 + CHUNK], XNL[:, r, i0:i0 + CHUNK], r == 0, r == 1)
                last.then_inc(S["e_mm"], 1)

            def apply(y, ih, j):
                n = 2 * KT * y + KT * ih + j
                pe.wait_ge(S["ph_ready"], n + 1)
                pe.wait_ge(S["pl_ready"], n + 1)
                if j == 0 and ih == 0 and y == 1:
                    pe.wait_ge(S["z2_ready"], GROUPS)
                    pe.wait_ge(S["ot_ready"], GROUPS)
                if j == 0 and ih == 1:
                    pe.wait_ge(S["stash_act"], 2 * y + 2)
                    pe.wait_ge(S["stash_dve"], 2 * y + 2)
                for r2 in range(R):
                    for q in range(2):
                        i0 = q * CHUNK
                        last = three(psum[:, 4 + 2 * r2 + q, :], QTh[:, j, r2 * P:(r2 + 1) * P], QTl[:, j, r2 * P:(r2 + 1) * P],
                                     Ph[:, j % 2, i0:i0 + CHUNK], Pl[:, j % 2, i0:i0 + CHUNK], j == 0, j == KT - 1)
                last.then_inc(S["ap_mm"], 1)

            pe.wait_ge(act_set, ACT_SET)
            pe.wait_ge(dve_set, DVE_SET)
            pe.wait_ge(pool_set, POOL_SET)
            with pe.Fori(0, B) as b:
                for c in range(4):
                    transpose_x(c)
                for c in range(2):
                    for tap in range(TAPS):
                        conv1_tap(c, tap)
                for s in range(CHUNKS + 3):
                    cm, ce, cy = s - 1, s - 2, s - 3
                    for u in range(STEPS):
                        if u == 0:
                            if s + 4 < CHUNKS:
                                transpose_x(s + 4)
                            if valid(cy):
                                attention_out(cy)
                        if s < CHUNKS:
                            if u < 2 * TAPS:
                                conv2_tap(s, u % TAPS, u < TAPS)
                            elif s + 2 < CHUNKS:
                                conv1_tap(s + 2, u - 2 * TAPS)
                        if u == 2 and valid(ce):
                            max_rows(ce)
                        if valid(cm):
                            for i in share(4 * s, u, STEPS):
                                score_tile(cm, i)
                        if valid(ce):
                            for j in share(4 * (ce + 1), u, STEPS, 3):
                                if j >= 6 and j % 4 == 2:
                                    attend(ce, (j - 6) // 4)
                                exp_tile(ce, j)
                        if u == 24 and s < CHUNKS:
                            project(s)
                    if s < CHUNKS:
                        project_values(s)
                    if valid(ce):
                        attend(ce, ce)
                pe.wait_ge(S["y_ready"], CHUNKS)
                token_tiles(0)
                token_tiles(1)
                positions(0, 0, 4)
                positions(0, 1, 5)
                token_tiles(2)
                positions(0, 2, 6)
                positions(0, 3, 7)
                token_tiles(3)
                inverse_norms(0, 0, 4)
                spatial_layer(0)
                pair_transposed(2)
                pair_transposed(3)
                for s in range(GROUPS + 3):
                    if s < GROUPS:
                        p_ = slice(s * CHUNK, (s + 1) * CHUNK)
                        pair = pair_free(("lg", 0, s))
                        pe.wait_ge(S["p_sum"], s + 1)
                        three(psum[:, pair, :], sqh[:, L_, :], sql[:, L_, :], TH[:, p_], TL[:, p_], True, True).then_inc(S["lr_mm"], 1)
                        three(psum[:, pair + 1, :], sqh[:, G_, :], sql[:, G_, :], TH[:, p_], TL[:, p_], True, True).then_inc(S["gt_mm"], 1)
                    if s == 0:
                        pe.wait_ge(S["rs_ready"], 1)
                        mm(psum[:, 4, 0:H], wright[:], rsum[:], start=True, stop=True).then_inc(S["rs_mm"], 1)
                    f = s - 2
                    if valid(f):
                        pe.wait_ge(S["gl_ready"], f + 1)
                        if f >= 1:
                            pe.wait_ge(S["ot_ready"], f)
                        else:
                            pe.wait_ge(S["rs_ready"], 3)
                        three(psum[:, 4, :], sqh[:, O_, :], sql[:, O_, :], Gh[:, f % 2], Gl[:, f % 2], True, True).then_inc(S["o_mm"], 1)
                    f = s - 3
                    if valid(f):
                        pe.wait_ge(S["ot_ready"], f + 1)
                        if f >= 1:
                            pe.wait_ge(S["z2_ready"], f)
                        for h in range(H2G):
                            last = tr(psum[:, 5, h * P:(h + 1) * P], oT[:, f % 2, h * P:(h + 1) * P], ident[:])
                        last.then_inc(S["ot_mm"], 1)
                    kk = s - 5
                    if 0 <= kk < 4:
                        if kk >= 2:
                            pe.wait_ge(S["qtl_ready"], 8 + kk - 1)
                        positions(1, kk, 6 + kk % 2)
                inverse_norms(1, 0, 6)
                spatial_layer(1)
                pe.wait_ge(S["zrow_mm"], 8)
                pe.sem_inc(arrived, 1)
                pe.wait_ge(go, b + 1)
                pe.sem_inc(passed, 1)

        @block.scalar
        def _(act):
            a = nc.scalar.activation

            def image(plane, c):
                return plane[:, 1 + c * ROWS:1 + (c + 1) * ROWS, 1:1 + W]

            def rows(t):
                return t.rearrange("p (r w) -> p r w", w=W)

            def elu_exp(c):
                act.wait_ge(S["elu_min"], c + 1)
                a(ebuf[:, c % 2], ebuf[:, c % 2], ACT.Exp).then_inc(S["elu_exp"], 1)
                a(res_chunk(res, c), split_w(psum[:, t_bank.get(c, bA), :]), ACT.Identity, bias=bias[:, B3:B3 + 1]).then_inc(S["res_ready"], 1)

            def elu_high(c):
                act.wait_ge(S["elu_read"], c + 1)
                a(image(xeh, c), rows(ebuf[:, c % 2]), ACT.Copy).then_inc(S["xeh_ready"], 1)

            def c1_high(c):
                act.wait_ge(S["c1_mm"], c + 1)
                a(image(c1h, c), rows(psum[:, c1_bank.get(c, bA), :]), ACT.Identity, bias=bias[:, B1:B1 + 1]).then_inc(S["c1h_ready"], 1)

            def positions_high(y, kk, bank):
                act.wait_ge(S["qt_mm"], 8 * y + kk + 1)
                src = psum[:, bank, :].rearrange("p (k i) -> p k i", k=2)
                a(QTh[:, 2 * kk:2 * kk + 2, :], src, ACT.Copy).then_inc(S["qth_ready"], 1)
                for k in range(2):
                    n = 16 * y + 2 * kk + k
                    if n >= 4:
                        act.wait_ge(S["sq_ready"], n - 3)
                    a(square[n % 4], src[:, k], ACT.Square, accum_out=d2[:, 2 * kk + k:2 * kk + k + 1]).then_inc(S["sq_ready"], 1)

            def normalised_high(y, n0):
                for n in range(n0, n0 + 4):
                    act.wait_ge(S["xn_ready"], 8 * y + n + 1)
                    a(XNH[:, n % 2, (n // 2) * CHUNK:(n // 2 + 1) * CHUNK], xn[n % 4], ACT.Copy).then_inc(S["xnh_ready"], 1)

            def pair_high(i):
                for g in (2 * i, 2 * i + 1):
                    act.wait_ge(S["p_mm"], g + 1)
                    a(TH[:, g * CHUNK:(g + 1) * CHUNK], psum[:, PAIR[("pt", 0, i)] + g % 2, :], ACT.Copy).then_inc(S["pth_ready"], 1)

            def spatial_layer(y):
                for ih in range(2):
                    for j in range(KT):
                        n = 2 * KT * y + KT * ih + j
                        pair = PAIR[("e", y, KT * ih + j)]
                        act.wait_ge(S["e_mm"], n + 1)
                        if n >= 2:
                            act.wait_ge(S["pl_ready"], n - 1)
                        a(pexp[:, j % 2], psum[:, pair:pair + 2, :], ACT.Exp,
                          accum_out=zsum[:, ih, j:j + 1]).then_inc(S["p_ready"], 1)
                        act.wait_ge(S["p_ready"], n + 1)
                        if n >= 2:
                            act.wait_ge(S["ap_mm"], n - 1)
                        a(Ph[:, j % 2], pexp[:, j % 2], ACT.Copy).then_inc(S["ph_ready"], 1)
                        kind, i = EXTRA.get((ih, j), (None, 0))
                        if kind == "qt":
                            for kk in (2 * i, 2 * i + 1):
                                positions_high(y, kk, PAIR[("qt", y, i)] + kk % 2)
                        elif kind == "rd":
                            normalised_high(y, 4)
                        elif kind == "pt" and y == 0:
                            pair_high(i)
                    if ih == 0:
                        act.wait_ge(S["ap_mm"], 2 * KT * y + KT)
                        for q in range(2):
                            a(stash[:, q], psum[:, 4 + q, :], ACT.Copy).then_inc(S["stash_act"], 1)
                for q in range(2):
                    act.wait_ge(S["zrow_mm"], 4 * y + q + 3)
                    a(ebuf[:, q], psum[:, PAIR[("z", y, 1)] + q, :], ACT.Copy).then_inc(S["zrow_copied"], 1)

            act.wait_ge(w_loaded, W_LOADS)
            stage1 = res[:, 0:TAPS * C].rearrange("p (t o) -> p t o", o=C)
            stage2 = prob[:, :, :].rearrange("p a n -> p (a n)")[:, 0:TAPS * 2 * C].rearrange("p (t o) -> p t o", o=2 * C)
            sq = res[:, TAPS * C:TAPS * C + 7 * C].rearrange("p (s o) -> p s o", o=C)
            a(w1h[:], stage1, ACT.Copy).then_inc(act_set, 1)
            a(w2h[:], stage2, ACT.Copy).then_inc(act_set, 1)
            act.wait_ge(dve_set, DVE_FOLDED)
            a(sqh[:], sq[:, 0:6, :], ACT.Copy).then_inc(act_set, 1)
            a(sel_den[:], sel_den32[:], ACT.Copy).then_inc(act_set, 1)
            with act.Fori(0, B) as b:
                for c in range(4):
                    elu_exp(c)
                    if c % 2:
                        elu_high(c - 1)
                        elu_high(c)
                act.wait_ge(S["pads"], PADS)
                for c in range(2):
                    c1_high(c)
                for s in range(CHUNKS + 2):
                    ce = s - 2
                    for u in range(STEPS):
                        if valid(ce):
                            for j in share(4 * (ce + 1), u, STEPS, 3):
                                e = exp_base(ce) + j
                                act.wait_ge(S["t_filled"], e + 1)
                                if e >= 8:
                                    act.wait_ge(S["pv_done"], (e - 8) // 4 + 1)
                                a(prob[:, e % 8], psum[:, bT + j % 2, :], ACT.Exp).then_inc(S["exp_done"], 1)
                        if u == 1 and s + 4 < CHUNKS:
                            elu_exp(s + 4)
                        if u == 2 and valid(ce):
                            act.wait_ge(S["mrep_mm"], ce + 1)
                            for g in (0, 2):
                                a(qop[g * G32:g * G32 + 1, ce % 3, :], psum[g * G32:g * G32 + 1, bT, :], ACT.Copy).then_inc(S["mrow_h"], 1)
                        if u == 5 and s + 4 < CHUNKS:
                            elu_high(s + 4)
                        if s < CHUNKS:
                            if u == 10:
                                act.wait_ge(S["gate_mm"], s + 1)
                                a(th[:], psum[:, bB, :], ACT.Tanh, scale=0.5, bias=bias[:, B2B:B2B + 1]).then_inc(S["th_ready"], 1)
                            if u == 18:
                                act.wait_ge(S["value_mm"], s + 1)
                                a(ah[:], psum[:, bC, :], ACT.Identity, scale=0.5, bias=bias[:, B2A:B2A + 1]).then_inc(S["ah_ready"], 1)
                            if u == 19:
                                act.wait_ge(S["c3_ready"], s + 1)
                                a(c3h[:], c3[:], ACT.Copy).then_inc(S["c3h_ready"], 1)
                            if u == 24:
                                act.wait_ge(S["qk_mm"], s + 1)
                                a(qop[:, s % 3, :], psum[:, bB, :], ACT.Identity, bias=bias[:, QB:QB + 1]).then_inc(S["qh_ready"], 1)
                                a(kop[:, s * CHUNK:(s + 1) * CHUNK], psum[:, bC, :], ACT.Identity, bias=bias[:, KB:KB + 1]).then_inc(S["kh_ready"], 1)
                            if u == 26 and s + 2 < CHUNKS:
                                c1_high(s + 2)
                    if valid(ce):
                        act.wait_ge(S["pv_done"], pv_base(ce + 1))
                        if ce >= 1:
                            act.wait_ge(S["mh_mm"], ce)
                        a(atth[:], psum[:, bP, :], ACT.Copy).then_inc(S["att_h"], 1)
                def token_copy(g):
                    act.wait_ge(S["a_mm"], g + 1)
                    a(XT[:, g * CHUNK:(g + 1) * CHUNK], psum[:, PAIR[("a", 0, g // 2)], :], ACT.Copy).then_inc(S["xt_act"], 1)
                token_copy(0)
                token_copy(2)
                for kk in range(4):
                    positions_high(0, kk, 4 + kk)
                token_copy(4)
                token_copy(6)
                normalised_high(0, 0)
                spatial_layer(0)
                pair_high(2)
                pair_high(3)
                act.wait_ge(S["rs_mm"], 1)
                for r in range(R):
                    a(rs2[:, :, r], psum[:, 4, 0:H], ACT.Identity, scale=0.5, bias=bias[:, BR:BR + 1]).then_inc(S["rs_ready"], 1)
                for s in range(GROUPS + 3):
                    if s < GROUPS:
                        act.wait_ge(S["gt_mm"], s + 1)
                        if s >= 2:
                            act.wait_ge(S["g_ready"], s - 1)
                        a(sg[:, s % 2], psum[:, PAIR[("lg", 0, s)] + 1, :], ACT.Tanh, scale=0.5, bias=bias[:, BG:BG + 1]).then_inc(S["sg_ready"], 1)
                    f = s - 1
                    if valid(f):
                        act.wait_ge(S["g_ready"], f + 1)
                        if f >= 2:
                            act.wait_ge(S["o_mm"], f - 1)
                        a(Gh[:, f % 2], gg[:, f % 2], ACT.Copy).then_inc(S["gh_ready"], 1)
                    f = s - 2
                    if valid(f):
                        act.wait_ge(S["o_mm"], f + 1)
                        if f >= 2:
                            act.wait_ge(S["ot_mm"], f - 1)
                        a(oT[:, f % 2], psum[:, 4, :], ACT.Identity, bias=bias[:, BO:BO + 1]).then_inc(S["ot_ready"], 1)
                    kk = s - 5
                    if 0 <= kk < 4:
                        positions_high(1, kk, 6 + kk % 2)
                normalised_high(1, 0)
                spatial_layer(1)
                act.wait_ge(S["zrow_copied"], 4)
                act.sem_inc(arrived, 1)
                act.wait_ge(go, b + 1)
                act.sem_inc(passed, 1)

        @block.vector
        def _(dve):
            tt, ts, stt = nc.vector.tensor_tensor, nc.vector.tensor_scalar, nc.vector.scalar_tensor_tensor

            def image(plane, c):
                return plane[:, 1 + c * ROWS:1 + (c + 1) * ROWS, 1:1 + W]

            def rows(t):
                return t.rearrange("p (r w) -> p r w", w=W)

            def elu_min(c):
                dve.wait_ge(S["x_transposed"], c + 1)
                if c >= 2:
                    dve.wait_ge(S["xe_ready"], c - 1)
                ts(ebuf[:, c % 2], psum[:, t_bank.get(c, bA), :], 0.0, None, ALU.min).then_inc(S["elu_min"], 1)

            def elu(c):
                dve.wait_ge(S["elu_exp"], c + 1)
                dve.wait_ge(S["res_ready"], c + 1)
                stt(ebuf[:, c % 2], ebuf[:, c % 2], -1.0, psum[:, t_bank.get(c, bA), :], ALU.add, ALU.max).then_inc(S["elu_read"], 1)

            def c1_low(c):
                dve.wait_ge(S["c1h_ready"], c + 1)
                stt(image(c1l, c), rows(psum[:, c1_bank.get(c, bA), :]), bias[:, B1:B1 + 1], image(c1h, c).bitcast(F32),
                    ALU.add, ALU.subtract).then_inc(S["c1_ready"], 1)

            chain = [0]

            def link(ins):
                ins.then_inc(dve_set, 1)
                chain[0] += 1
                dve.wait_ge(dve_set, chain[0])

            dve.wait_ge(w_loaded, W_LOADS)
            dve.wait_ge(pool_set, POOL_SET)
            stage1 = res[:, 0:TAPS * C].rearrange("p (t o) -> p t o", o=C)
            stage2 = prob[:, :, :].rearrange("p a n -> p (a n)")[:, 0:TAPS * 2 * C].rearrange("p (t o) -> p t o", o=2 * C)
            sq = res[:, TAPS * C:TAPS * C + 7 * C].rearrange("p (s o) -> p s o", o=C)
            ts(sq[:, 0, :], sq[:, 0, :], 0.25, None, ALU.mult).then_inc(dve_set, 1)
            nc.vector.tensor_reduce(sq[:, 2, :], planes_w3(res).rearrange("p h o -> p o h"), AX.X, ALU.add).then_inc(dve_set, 1)
            tt(sq[:, 3, :], sq[:, 3, :], sq[:, 6, :], ALU.add).then_inc(dve_set, 1)
            tt(bias[:, BL:BL + 1], bias[:, BL:BL + 1], bias[:, BE:BE + 1], ALU.add).then_inc(dve_set, 1)
            ts(bias[:, QB:QB + 1], bias[:, QB:QB + 1], 0.25, None, ALU.mult).then_inc(dve_set, 1)
            for col, k in ((B2A, 0.5), (B2B, 0.5), (BG, 0.5), (BR, 32.0)):
                ts(bias[:, col:col + 1], bias[:, col:col + 1], k, None, ALU.mult).then_inc(dve_set, 1)
            chain[0] = 9
            nc.vector.memset(bias[0:1, KB:KB + 1], 1.0).then_inc(dve_set, 1)
            nc.vector.memset(bias[64:65, KB:KB + 1], 1.0).then_inc(dve_set, 1)
            chain[0] = DVE_FOLDED
            dve.wait_ge(act_set, 1)
            tt(w1l[:], stage1, w1h[:].bitcast(F32), ALU.subtract).then_inc(dve_set, 1)
            dve.wait_ge(act_set, 2)
            tt(w2l[:], stage2, w2h[:].bitcast(F32), ALU.subtract).then_inc(dve_set, 1)
            dve.wait_ge(act_set, 3)
            tt(sql[:], sq[:, 0:6, :], sqh[:].bitcast(F32), ALU.subtract).then_inc(dve_set, 1)
            dve.wait_ge(dve_set, DVE_SET)

            def positions_low(y, kk, bank):
                dve.wait_ge(S["qth_ready"], 8 * y + kk + 1)
                dve.wait_ge(S["sq_ready"], 16 * y + 2 * kk + 2)
                tt(QTl[:, 2 * kk:2 * kk + 2, :], psum[:, bank, :].rearrange("p (k i) -> p k i", k=2),
                   QTh[:, 2 * kk:2 * kk + 2, :].bitcast(F32), ALU.subtract).then_inc(S["qtl_ready"], 1)

            def norm_diagonals(y, q0):
                dve.wait_ge(S["rd_ready"], 2 * y + q0 // 2 + 1)
                if q0:
                    dve.wait_ge(S["rdrow_mm"], 4 * y + 2)
                for k in range(4 * q0, 4 * q0 + 8):
                    ins = ts(diag[k // 4 % 2][:, k % 4, :], ident[:], rd[:, k:k + 1], None, ALU.mult)
                ins.then_inc(S["rdiag_ready"], 1)

            def normalise(y, q0, bank):
                for n in range(2 * q0, 2 * q0 + 4):
                    q = n // 2
                    dve.wait_ge(S["rdrow_mm"], 4 * y + q + 1)
                    tt(xn[n % 4], XTv[:, n % 2, q * CHUNK:(q + 1) * CHUNK], psum[:, bank + q % 2, :], ALU.mult).then_inc(S["xn_ready"], 1)
                for n in (2 * q0 + 1, 2 * q0 + 3):
                    dve.wait_ge(S["xnh_ready"], 8 * y + n + 1)
                    xs = slice((n // 2) * CHUNK, (n // 2 + 1) * CHUNK)
                    tt(XNL[:, 1, xs], xn[n % 4], XNH[:, 1, xs].bitcast(F32), ALU.subtract).then_inc(S["xnl_dve"], 1)

            def scale_diagonals(y, i, gcol):
                n = 3 * (2 * y + i)
                gz_ = gz[:, 8 * i:8 * i + 8]
                dve.wait_ge(S["p_ready"], 2 * KT * y + KT + 8 * (i + 1))
                tt(gz_, zsum[:, 0, 8 * i:8 * i + 8], zsum[:, 1, 8 * i:8 * i + 8], ALU.add).then_inc(S["gz_step"], 1)
                dve.wait_ge(S["gz_step"], n + 1)
                nc.vector.reciprocal(gz_, gz_).then_inc(S["gz_step"], 1)
                dve.wait_ge(S["gz_step"], n + 2)
                ts(gz_, gz_, bias[:, gcol:gcol + 1], None, ALU.mult).then_inc(S["gz_step"], 1)
                dve.wait_ge(S["gz_step"], n + 3)
                if i:
                    dve.wait_ge(S["zrow_mm"], 4 * y + 2)
                for k in range(8 * i, 8 * i + 8):
                    ins = ts(diag[k // 4 % 2][:, k % 4, :], ident[:], gz[:, k:k + 1], None, ALU.mult)
                ins.then_inc(S["zdiag_ready"], 1)

            def pair_low(i):
                for g in (2 * i, 2 * i + 1):
                    dve.wait_ge(S["pth_ready"], g + 1)
                    gs = slice(g * CHUNK, (g + 1) * CHUNK)
                    src = psum[:, PAIR[("pt", 0, i)] + g % 2, :]
                    tt(TL[:, gs], src, TH[:, gs].bitcast(F32), ALU.subtract)
                    nc.vector.tensor_reduce(rpart[:, g, :], src.rearrange("p (h c r) -> p c h r", h=H2G, r=R), AX.XY, ALU.add).then_inc(S["p_sum"], 1)

            def spatial_layer(y, gcol):
                for ih in range(2):
                    for j in range(KT):
                        n = 2 * KT * y + KT * ih + j
                        dve.wait_ge(S["ph_ready"], n + 1)
                        tt(Pl[:, j % 2], pexp[:, j % 2], Ph[:, j % 2].bitcast(F32), ALU.subtract).then_inc(S["pl_ready"], 1)
                        kind, i = EXTRA.get((ih, j), (None, 0))
                        if kind == "qt":
                            for kk in (2 * i, 2 * i + 1):
                                positions_low(y, kk, PAIR[("qt", y, i)] + kk % 2)
                        elif kind == "rd":
                            normalise(y, 2, PAIR[("rd", y, 1)])
                        elif kind == "z":
                            for q in range(2):
                                dve.wait_ge(S["zrow_mm"], 4 * y + q + 1)
                                for r2 in range(R):
                                    t = stash[:, 2 * r2 + q]
                                    tt(t, t, psum[:, PAIR[("z", y, 0)] + q, :], ALU.mult).then_inc(S["scaled_ready"], 1)
                            for q in range(2):
                                dve.wait_ge(S["scaled_ready"], 8 * y + 2 * q + 2)
                                xv = XTv[:, 1, q * CHUNK:(q + 1) * CHUNK]
                                tt(xv, stash[:, 2 + q], xv, ALU.add).then_inc(S["x_dve"], 1)
                        elif kind == "pt" and y == 0:
                            pair_low(i)
                        if (ih, j) == (0, 3):
                            norm_diagonals(y, 2)
                        if (ih, j) == (1, 7):
                            scale_diagonals(y, 0, gcol)
                    if ih == 0:
                        dve.wait_ge(S["ap_mm"], 2 * KT * y + KT)
                        for q in range(2, 4):
                            nc.vector.tensor_copy(stash[:, q], psum[:, 4 + q, :]).then_inc(S["stash_dve"], 1)
                scale_diagonals(y, 1, gcol)
                dve.wait_ge(S["pl_ready"], 2 * KT * (y + 1))
                dve.wait_ge(S["ap_mm"], 2 * KT * (y + 1))
                for q in range(2, 4):
                    dve.wait_ge(S["zrow_copied"], 2 * y + q - 1)
                    for r2 in range(R):
                        tt(scaled[:, 2 * r2 + q - 2], psum[:, 4 + 2 * r2 + q - 2, :], ebuf[:, q - 2], ALU.mult).then_inc(S["scaled_ready"], 1)
                    dve.wait_ge(S["scaled_ready"], 8 * y + 2 * q + 2)
                    xv = XTv[:, 1, q * CHUNK:(q + 1) * CHUNK]
                    tt(xv, scaled[:, q], xv, ALU.add).then_inc(S["x_dve"], 1)

            with dve.Fori(0, B) as b:
                for c in (0, 2):
                    elu_min(c)
                    elu_min(c + 1)
                    elu(c)
                    elu(c + 1)
                dve.wait_ge(S["pads"], PADS)
                for c in range(2):
                    c1_low(c)
                for s in range(CHUNKS + 3):
                    cm, ce, cy = s - 1, s - 2, s - 3
                    for u in range(STEPS):
                        if valid(cm):
                            for i in share(4 * s, u, STEPS):
                                t, kc = divmod(i, cm + 1)
                                n = score_base(s) + i
                                width = (t + 1) * P if kc == cm else CHUNK
                                dve.wait_ge(S["s_filled"], n + 1)
                                if i == 0 and cm >= 1:
                                    dve.wait_ge(S["max_ready"], cm)
                                nc.vector.tensor_reduce(mpart[:, t, kc:kc + 1], psum[:, bS + n % 2, 0:width], AX.X, ALU.max).then_inc(S["s_drained"], 1)
                        if u == 0 and valid(cy):
                            dve.wait_ge(S["den_mm"], cy + 1)
                            if cy >= 1:
                                dve.wait_ge(S["z_ready"], cy)
                            ts(rden[:], psum[:, bT, :], 1e-10, None, ALU.add).then_inc(S["den_added"], 1)
                            dve.wait_ge(S["den_added"], cy + 1)
                            nc.vector.reciprocal(rden[:], rden[:]).then_inc(S["den_inv"], 1)
                            dve.wait_ge(S["den_inv"], cy + 1)
                            dve.wait_ge(S["mh_mm"], cy + 1)
                            if cy >= 1:
                                dve.wait_ge(S["y_ready"], cy)
                            tt(zbuf[:], psum[:, bT + 1, :], rden[:], ALU.mult).then_inc(S["z_ready"], 1)
                        if u == 1 and s + 4 < CHUNKS:
                            elu_min(s + 4)
                        if u == 2 and valid(ce):
                            dve.wait_ge(S["mrow_h"], 2 * ce + 2)
                            tt(qop[64:65, ce % 3, :], psum[64:65, bT, :], qop[64:65, ce % 3, :].bitcast(F32), ALU.subtract).then_inc(S["mrow_ready"], 1)
                        if u == 4 and s + 4 < CHUNKS:
                            elu(s + 4)
                        if s < CHUNKS:
                            if u == 18:
                                dve.wait_ge(S["th_ready"], s + 1)
                                dve.wait_ge(S["ah_ready"], s + 1)
                                if s >= 1:
                                    dve.wait_ge(S["res_added"], s)
                                    dve.wait_ge(S["s_filled"], score_base(s))
                                stt(c3[:], th[:], 1.0, ah[:], ALU.add, ALU.mult).then_inc(S["c3_ready"], 1)
                            if u == 24:
                                dve.wait_ge(S["qh_ready"], s + 1)
                                stt(qop[64:128, s % 3, :], psum[64:128, bB, :], bias[64:128, QB:QB + 1], qop[64:128, s % 3, :].bitcast(F32),
                                    ALU.add, ALU.subtract).then_inc(S["q_ready"], 1)
                                dve.wait_ge(S["kh_ready"], s + 1)
                                for g in (1, 3):
                                    k_ = kop[g * G32:(g + 1) * G32, s * CHUNK:(s + 1) * CHUNK]
                                    ins = stt(k_, psum[g * G32:(g + 1) * G32, bC, :], bias[g * G32:(g + 1) * G32, KB:KB + 1], k_.bitcast(F32),
                                              ALU.add, ALU.subtract)
                                    ins.then_inc(S["k_ready"], 1) if g == 3 else ins
                            if u == 26 and s + 2 < CHUNKS:
                                c1_low(s + 2)
                    if s < CHUNKS:
                        n = score_base(s) + (4 * s if valid(cm) else 0)
                        dve.wait_ge(S["s_filled"], n + 1)
                        src = psum[:, bS + n % 2, 0:TILES * G32].rearrange("p (t d) -> p t d", d=G32)[:, :, 0:DV]
                        tt(vaug[:, s * TILES:(s + 1) * TILES, 0:DV], src, bv_rep[:], ALU.add).then_inc(S["v_ready"], 1)
                        dve.wait_ge(S["v_ready"], s + 1)
                        dve.sem_inc(S["s_drained"], 1)
                    if valid(cm):
                        dve.wait_ge(S["s_drained"], n_drained(s))
                        if cm >= 1:
                            dve.wait_ge(S["mrep_mm"], cm)
                        nc.vector.tensor_reduce(mneg[:, 0, :], mpart[:, :, 0:cm + 1], AX.X, ALU.max).then_inc(S["max_ready"], 1)
                        dve.wait_ge(S["max_ready"], cm + 1)
                        ts(mneg[:, 1, :], mneg[:, 0, :], -1.0, 1e9, ALU.mult, ALU.min).then_inc(S["mfin"], 1)
                        dve.wait_ge(S["mfin"], cm + 1)
                        for t in range(TILES):
                            ins = ts(mdiag[:, t, :], ident[:], mneg[:, 1, t:t + 1], None, ALU.mult)
                        ins.then_inc(S["diag_ready"], 1)
                    if valid(ce):
                        dve.wait_ge(S["att_h"], ce + 1)
                        tt(attl[:], psum[:, bP, :], atth[:].bitcast(F32), ALU.subtract).then_inc(S["att_l"], 1)
                def token_copy(g):
                    dve.wait_ge(S["a_mm"], g + 1)
                    nc.vector.tensor_copy(XT[:, g * CHUNK:(g + 1) * CHUNK], psum[:, PAIR[("a", 0, g // 2)] + 1, :]).then_inc(S["xt_dve"], 1)
                token_copy(1)
                token_copy(3)
                for kk in range(4):
                    positions_low(0, kk, 4 + kk)
                token_copy(5)
                norm_diagonals(0, 0)
                token_copy(7)
                normalise(0, 0, 4)
                spatial_layer(0, G1)
                pair_low(2)
                pair_low(3)
                dve.wait_ge(S["p_sum"], GROUPS)
                nc.vector.tensor_reduce(rsum[:], rpart[:, :, :].rearrange("p g c -> p c g"), AX.X, ALU.add).then_inc(S["rs_ready"], 1)
                rs_row = bcast_mid(rs2, H2G)
                dve.wait_ge(S["rs_ready"], 3)
                for s in range(GROUPS + 3):
                    if s < GROUPS:
                        dve.wait_ge(S["lr_mm"], s + 1)
                        if s >= 2:
                            dve.wait_ge(S["g_ready"], s - 1)
                        stt(ug[:, s % 2].rearrange("p (h i) -> p h i", h=H2G), psum[:, PAIR[("lg", 0, s)], :].rearrange("p (h i) -> p h i", h=H2G),
                            bias[:, BL:BL + 1], rs_row, ALU.add, ALU.mult).then_inc(S["u_ready"], 1)
                        dve.wait_ge(S["u_ready"], s + 1)
                        dve.wait_ge(S["sg_ready"], s + 1)
                        if s >= 2:
                            dve.wait_ge(S["gl_ready"], s - 1)
                        stt(gg[:, s % 2], sg[:, s % 2], 1.0, ug[:, s % 2], ALU.add, ALU.mult).then_inc(S["g_ready"], 1)
                    kk = s - 5
                    if 0 <= kk < 4:
                        positions_low(1, kk, 6 + kk % 2)
                    if s == GROUPS + 2:
                        norm_diagonals(1, 0)
                        normalise(1, 0, 6)
                    f = s - 3
                    if valid(f):
                        dve.wait_ge(S["ot_mm"], f + 1)
                        z = XT[:, f * CHUNK:(f + 1) * CHUNK]
                        tt(z, psum[:, 5, :], z, ALU.add).then_inc(S["z2_ready"], 1)
                        dve.wait_ge(S["z2_ready"], f + 1)
                        for h in range(H2G):
                            ins = nc.vector.bn_stats(st[:, f % 2, h, :], z[:, h * C:(h + 1) * C])
                        ins.then_inc(S["st_ready"], 1)
                        dve.wait_ge(S["st_ready"], 2 * f + 1)
                        if f >= 2:
                            dve.wait_ge(S["eps_ready"], f - 1)
                        for h in range(H2G):
                            ins = nc.vector.bn_aggr(mv[:, f % 2, h, :], st[:, f % 2, h, :])
                        ins.then_inc(S["st_ready"], 1)
                        dve.wait_ge(S["st_ready"], 2 * f + 2)
                        for h in range(H2G):
                            zh = z[:, h * C:(h + 1) * C]
                            ins = stt(zh, zh, mv[:, f % 2, h, 0:1], ln_s[:], ALU.subtract, ALU.mult)
                        ins.then_inc(S["centred_ready"], 1)
                spatial_layer(1, G3)
                dve.wait_ge(S["x_dve"], 8)
                dve.sem_inc(arrived, 1)
                dve.wait_ge(go, b + 1)
                dve.sem_inc(passed, 1)

        @block.gpsimd
        def _(gp):
            tt, ts, ms, sel = nc.gpsimd.tensor_tensor, nc.gpsimd.tensor_scalar, nc.gpsimd.memset, nc.gpsimd.affine_select
            count = [0]

            def link(ins):
                ins.then_inc(pool_set, 1)
                count[0] += 1

            def hold():
                gp.wait_ge(pool_set, count[0])
            sq = res[:, TAPS * C:TAPS * C + 7 * C]
            link(ms(sq, 0.0))
            link(ms(planes_w3(res), 0.0))
            link(ms(bias[:], 0.0))
            link(ms(wv32[:], 0.0))
            assert count[0] == POOL_CLEARED
            for t in (ident, identb, sel_den32, sel_max, mask_q, mask_k):
                link(ms(t[:], 0.0))
            link(ms(ones[:], 1.0))
            link(ms(half[:], -0.5))
            link(ms(vaug[:], 0.0))
            hold()
            link(ms(vaug[:, :, DV:DV + 1], 1.0))
            for t in (ident, identb):
                link(sel(out=t[:], in_=t[:], compare_op=ALU.not_equal, fill=1.0, base=0, pattern=[[-1, P]], channel_multiplier=1))
            for g in range(4):
                link(sel(out=sel_den32[:], in_=sel_den32[:], compare_op=ALU.not_equal, fill=1.0, base=-(g * G32 + DV),
                         pattern=[[0, P]], channel_multiplier=1))
                hold()
            for col in (0, 64):
                link(ms(sel_max[:, col:col + 1], 1.0))
            link(sel(out=mask_q[:], in_=mask_q[:], compare_op=ALU.is_gt, fill=NEG, base=0, pattern=[[-1, P]], channel_multiplier=1))
            link(sel(out=mask_k[:], in_=mask_k[:], compare_op=ALU.is_gt, fill=NEG, base=-3 * P, pattern=[[1, CHUNK + 3 * P]], channel_multiplier=-1))
            hold()
            assert count[0] == POOL_SET, count[0]

            def image(plane, c):
                return plane[:, 1 + c * ROWS:1 + (c + 1) * ROWS, 1:1 + W]

            def elu_low(c):
                gp.wait_ge(S["xeh_ready"], c + 1)
                tt(image(xel, c), ebuf[:, c % 2].rearrange("p (r w) -> p r w", w=W), image(xeh, c).bitcast(F32), ALU.subtract).then_inc(S["xe_ready"], 1)

            def inverse_norm(y, i):
                gp.wait_ge(S["sq_ready"], 16 * y + 8 * (i + 1))
                tt(rd[:, 8 * i:8 * i + 8], d2[:, 8 * i:8 * i + 8], half[:, 0:8], ALU.pow).then_inc(S["rd_ready"], 1)

            def normalised_low(y, q0):
                for q in (q0, q0 + 1):
                    gp.wait_ge(S["xnh_ready"], 8 * y + 2 * q + 1)
                    xs = slice(q * CHUNK, (q + 1) * CHUNK)
                    tt(XNL[:, 0, xs], xn[2 * q % 4], XNH[:, 0, xs].bitcast(F32), ALU.subtract).then_inc(S["xnl_pool"], 1)

            def spatial_layer(y):
                inverse_norm(y, 1)
                normalised_low(y, 2)
                for q in range(4):
                    gp.wait_ge(S["scaled_ready"], 8 * y + 2 * q + 1)
                    t = stash[:, q] if q < 2 else scaled[:, q - 2]
                    xv = XTv[:, 0, q * CHUNK:(q + 1) * CHUNK]
                    tt(xv, t, xv, ALU.add).then_inc(S["x_pool"], 1)

            with gp.Fori(0, B) as b:
                for i in range(4):
                    pl = planes[:, i * IMG:(i + 1) * IMG].bitcast(F32)
                    ms(pl[:, 0:WP + 1], 0.0).then_inc(S["pads"], 1)
                    ms(pl[:, WP + 1 + W:WP + 1 + W + (H - 1) * WP].rearrange("p (r c) -> p r c", c=WP)[:, :, 0:2], 0.0).then_inc(S["pads"], 1)
                    ms(pl[:, (H + 1) * WP - 1:IMG], 0.0).then_inc(S["pads"], 1)
                gp.wait_ge(S["pads"], PADS)
                for c in range(4):
                    elu_low(c)
                for s in range(CHUNKS + 3):
                    cy = s - 3
                    if valid(cy):
                        gp.wait_ge(S["z_ready"], cy + 1)
                        r_ = res_chunk(res, cy)
                        tt(r_, split_w(zbuf[:]), r_, ALU.add).then_inc(S["y_ready"], 1)
                    if s + 4 < CHUNKS:
                        elu_low(s + 4)
                    if s < CHUNKS:
                        gp.wait_ge(S["c3h_ready"], s + 1)
                        if s >= 1:
                            gp.wait_ge(S["qk_mm"], s)
                        tt(c3l[:], c3[:], c3h[:].bitcast(F32), ALU.subtract).then_inc(S["c3l_ready"], 1)
                        r_ = res_chunk(res, s)
                        gp.wait_ge(S["res_ready"], s + 1)
                        tt(r_, r_, split_w(c3[:]), ALU.add).then_inc(S["res_added"], 1)
                inverse_norm(0, 0)
                normalised_low(0, 0)
                spatial_layer(0)
                for s in range(GROUPS + 4):
                    f = s - 1
                    if valid(f):
                        gp.wait_ge(S["gh_ready"], f + 1)
                        if f >= 2:
                            gp.wait_ge(S["o_mm"], f - 1)
                        tt(Gl[:, f % 2], gg[:, f % 2], Gh[:, f % 2].bitcast(F32), ALU.subtract).then_inc(S["gl_ready"], 1)
                    if s == GROUPS + 1:
                        inverse_norm(1, 0)
                    if s == GROUPS + 3:
                        normalised_low(1, 0)
                    f = s - 4
                    if valid(f):
                        gp.wait_ge(S["st_ready"], 2 * f + 2)
                        ts(rstd[:, f % 2], mv[:, f % 2, :, 1], EPS_L, None, ALU.add).then_inc(S["eps_ready"], 1)
                        gp.wait_ge(S["eps_ready"], f + 1)
                        tt(rstd[:, f % 2], rstd[:, f % 2], half[:, 0:1].to_broadcast([P, H2G]), ALU.pow).then_inc(S["rstd_ready"], 1)
                        gp.wait_ge(S["rstd_ready"], f + 1)
                        gp.wait_ge(S["centred_ready"], f + 1)
                        z = XT[:, f * CHUNK:(f + 1) * CHUNK].rearrange("p (h k) -> p h k", k=C)
                        tt(z, z, rstd[:, f % 2].unsqueeze(2).to_broadcast([P, H2G, C]), ALU.mult).then_inc(S["m_step"], 1)
                        gp.wait_ge(S["m_step"], f + 1)
                        tt(z, z, bcast_mid(ln_b, H2G), ALU.add).then_inc(S["ln_ready"], 1)
                spatial_layer(1)
                gp.wait_ge(S["x_pool"], 8)
                gp.wait_ge(arrived, 4 * b + 4)
                gp.sem_inc(passed, 1)
                for s_ in loop_sems:
                    gp.sem_clear(s_)
                gp.sem_inc(go, 1)


POOL_CLEARED = 4
POOL_SET = 4 + 6 + 3 + 1 + 2 + 4 + 2 + 2
ACT_SET = 4
DVE_FOLDED = 11
DVE_SET = 14
PADS = 12
W_LOADS = 16 * (2 + 5 * 4 + 4 + 2 + 7 + 2 + 2 + 4 + 2)


def n_drained(s):
    return score_base(s + 1)


def res_chunk(res, c):
    return res[:, :].rearrange("p (h c r) -> p c h r", c=H, r=R)[:, c * ROWS:(c + 1) * ROWS]


def split_w(t):
    return t.rearrange("p (c h r) -> p c h r", c=ROWS, r=R)


def planes_w3(res):
    o = TAPS * C + 7 * C
    return res[:, o:o + HEADS * C].rearrange("p (h o) -> p h o", o=C)


def bcast(v, p, n):
    return bass.AP(tensor=v.tensor, offset=v.offset, ap=[[0, p], [1, n]])


def bcast_mid(t, k):
    full = t[:, :, :].rearrange("p c r -> p (c r)") if len(t.shape) == 3 else t[:, :]
    return full.unsqueeze(1).to_broadcast([P, k, P])


_INS = ["x", "L0_conv_W1", "L0_conv_b1", "L0_conv_W2", "L0_conv_b2", "L0_conv_Wq", "L0_conv_bq", "L0_conv_Wk", "L0_conv_bk",
        "L0_conv_Wv", "L0_conv_bv", "L0_conv_W3", "L0_conv_b3", "L1_conv_gamma", "L2_conv_W_left", "L2_conv_b_left",
        "L2_conv_W_right", "L2_conv_b_right", "L2_conv_W_gate", "L2_conv_b_gate", "L2_conv_W_eq", "L2_conv_b_eq",
        "L2_conv_W_out", "L2_conv_b_out", "L2_conv_ln_scale", "L2_conv_ln_bias", "L3_conv_gamma"]


def kernel(**inputs):
    import concourse.bacc as bacc
    from concourse.bass_utils import run_bass_kernel_spmd

    nc = bacc.Bacc("TRN2", target_bir_lowering=False, num_devices=1)
    arrays, args = {}, []
    for name in _INS:
        a = np.ascontiguousarray(inputs[name])
        arrays["in_" + name] = a
        args.append(nc.dram_tensor("in_" + name, a.shape, mybir.dt.from_np(a.dtype), kind="ExternalInput").ap())
    args.append(nc.dram_tensor("out_x", (B, H, W, C), F32, kind="ExternalOutput").ap())
    build_program(nc, *args)
    r = run_bass_kernel_spmd(nc, [arrays], core_ids=[0])
    return r.results[0]["out_x"]
```

```python
import numpy as np
import concourse.bass as bass
from concourse import mybir
from contextlib import ExitStack

F32 = mybir.dt.float32
F32R = mybir.dt.float32r
BF16 = mybir.dt.bfloat16
ALU = mybir.AluOpType
ACT = mybir.ActivationFunctionType
AX = mybir.AxisListType

B, H, W, C = 4, 64, 64, 128
N = H * W
P = 128
DQK, DV, HEADS = 4, 16, 8
CHUNK = 512
CHUNKS = N // CHUNK
ROWS = CHUNK // W
TILES = CHUNK // P
TAPS = 9
STEPS = 3 * TAPS
HP, WP = H + 2, W + 2
NEG = -1e10
EPS_L = 1e-5
R = 2
GROUPS = 8
H2G = 4
NPOS = N // 2
KT = NPOS // P
IHALF = NPOS // 2
G32 = 32


def share(n, u, steps, first=0):
    if u < first:
        return range(0)
    return range(n * (u - first) // (steps - first), n * (u - first + 1) // (steps - first))


def valid(c):
    return 0 <= c < CHUNKS


def score_base(s):
    return sum((1 if valid(t - 2) else 0) + (4 * t if valid(t - 1) else 0) + (1 if valid(t) else 0) for t in range(s))


def tiles_base(s):
    return score_base(s) + (1 if valid(s - 2) else 0)


def exp_base(c):
    return 2 * c * (c + 1)


def pv_base(c):
    return c * (c + 1) // 2


MIRRORED = {(1, 0), (0, 2), (1, 2), (0, 3), (1, 3), (3, 2)}
KEPT = {(0, 1): 0, (2, 0): 1, (2, 1): 2, (3, 0): 3, (3, 1): 0, (2, 3): 0}


def tile_of(n):
    return n // (2 * KT), n // KT % 2, n % KT


def kept_before(y, ih, j):
    def in_half(h, n):
        return sum((t // 4, 2 * h + q) in KEPT for t in range(n) for q in range(2))
    return y * (in_half(0, KT) + in_half(1, KT)) + ih * in_half(0, KT) + in_half(ih, j)


def pair_slots():
    order = [("a", 0, i) for i in range(4)]
    for y in range(2):
        for ih in range(2):
            for j in range(KT):
                order.append(("e", y, KT * ih + j))
                kind, i = EXTRA.get((ih, j), (None, 0))
                if kind and not (kind == "pt" and y == 1):
                    order.append((kind, y, i))
        order.append(("z", y, 1))
        if y == 0:
            order += [("pt", 0, 2), ("pt", 0, 3)] + [("lg", 0, g) for g in range(GROUPS)]
    return order


EXTRA = {(0, 0): ("qt", 2), (0, 2): ("qt", 3), (0, 5): ("rd", 1), (1, 9): ("z", 0), (1, 11): ("pt", 0), (1, 13): ("pt", 1)}
ORDER = pair_slots()
PAIR = {item: 2 * (n % 2) for n, item in enumerate(ORDER)}
BEFORE = {item: ORDER[n - 2] if n >= 2 else None for n, item in enumerate(ORDER)}


def build_program(nc, x, W1, b1, W2, b2, Wq, bq, Wk, bk, Wv, bv, W3, b3, gamma1,
                  Wleft, bleft, Wright, bright, Wgate, bgate, Weq, beq, Wout, bout, ln_scale, ln_bias, gamma3, out):
    ctx = ExitStack()
    with ctx:
        def sb(name, shape, dt=F32):
            return ctx.enter_context(nc.sbuf_tensor(name, shape, dt))

        def sem(name):
            return ctx.enter_context(nc.semaphore(name))

        w1h, w1l = sb("w1h", [P, TAPS, C], F32R), sb("w1l", [P, TAPS, C], F32R)
        w2h, w2l = sb("w2h", [P, TAPS, 2 * C], F32R), sb("w2l", [P, TAPS, 2 * C], F32R)
        sqh, sql = sb("sqh", [P, 6, C], F32R), sb("sql", [P, 6, C], F32R)
        Q_, K_, M_, L_, G_, O_ = range(6)
        wv32 = sb("wv32", [P, G32])
        wright = sb("wright", [P, C])
        ident = sb("ident", [P, P])
        identb = sb("identb", [P, P], BF16)
        sel_den = sb("sel_den", [P, P], F32R)
        sel_den32 = sb("sel_den32", [P, P])
        mask_q = sb("mask_q", [P, P], BF16)
        mask_k = sb("mask_k", [P, CHUNK + 3 * P], BF16)
        half = sb("half", [P, KT])
        NB = 13
        bias = sb("bias", [P, NB])
        B1, B2A, B2B, B3, QB, KB, BL, BG, BR, BO, G1, G3, BE = range(NB)
        bv_rep = sb("bv_rep", [P, TILES, DV])
        ln_s, ln_b = sb("ln_s", [P, C]), sb("ln_b", [P, C])

        xin = sb("xin", [P, 4, TILES, C])
        ebuf = sb("ebuf", [P, 2, CHUNK])
        th, ah, c3 = sb("th", [P, CHUNK]), sb("ah", [P, CHUNK]), sb("c3", [P, CHUNK])
        rden = sb("rden", [P, CHUNK])
        with nc.sbuf_tensor("kept_exps", [P, 8, CHUNK], F32) as kept_exps:
            pass
        c3h, c3l = sb("c3h", [P, CHUNK], F32R), sb("c3l", [P, CHUNK], F32R)
        qop = sb("qop", [P, 3, CHUNK], F32R)
        atth, attl = sb("atth", [P, CHUNK], F32R), sb("attl", [P, CHUNK], F32R)
        zbuf = sb("zbuf", [P, CHUNK])
        mpart = sb("mpart", [P, TILES, CHUNKS])
        mneg = sb("mneg", [P, 2, TILES])
        vaug = sb("vaug", [P, CHUNKS * TILES, G32])
        IMG = HP * WP
        planes = sb("planes", [P, 4 * IMG + 8], F32R)
        kop = sb("kop", [P, N], F32R)
        xeh, xel, c1h, c1l = [planes[:, i * IMG:(i + 1) * IMG].rearrange("p (r c) -> p r c", c=WP) for i in range(4)]
        res = sb("res", [P, N])
        prob = sb("prob", [P, 8, CHUNK])
        d2, rd, gz = sb("d2", [P, KT]), sb("rd", [P, KT]), sb("gz", [P, KT])
        zsum = sb("zsum", [P, 3, KT])
        square = [t[:, i * 2 * P:(i + 1) * 2 * P] for t in (c3, th) for i in range(2)]
        rpart = rden[:, :].rearrange("p (g c) -> p g c", c=H)
        xn = [ebuf[:, 0], ebuf[:, 1], ah[:, :], rden[:, :]]
        rsum = sb("rsum", [P, H]); rs2 = sb("rs2", [P, H, 2])
        st = sb("st", [P, 2, H2G, 6]); mv = sb("mv", [P, 2, H2G, 2]); rstd = sb("rstd", [P, 2, H2G])
        psum = ctx.enter_context(nc.psum_tensor("psum", [P, 8, CHUNK], F32))
        XT = prob[:, :, :].rearrange("p a n -> p (a n)")
        XTv = XT.rearrange("p (n r) -> p r n", r=R)
        XNH, XNL = [planes[:, i * N:(i + 1) * N].rearrange("p (r n) -> p r n", r=R) for i in range(2)]
        TH, TL = [planes[:, i * N:(i + 1) * N] for i in (2, 3)]
        QTh, QTl = [t.rearrange("p (k i) -> p k i", i=2 * P) for t in (TH, TL)]
        Ph = kop[:, 0:2 * IHALF].rearrange("p (a n) -> p a n", a=2)
        Pl = kop[:, 2 * IHALF:4 * IHALF].rearrange("p (a n) -> p a n", a=2)
        stash = res[:, 0:NPOS].rearrange("p (q n) -> p q n", n=CHUNK)
        pexp = res[:, NPOS:2 * NPOS].rearrange("p (a n) -> p a n", a=2)
        scaled = res[:, NPOS:2 * NPOS].rearrange("p (q n) -> p q n", n=CHUNK)
        Gh = kop[:, 0:2 * CHUNK].rearrange("p (a n) -> p a n", a=2)
        Gl = kop[:, 2 * CHUNK:4 * CHUNK].rearrange("p (a n) -> p a n", a=2)
        sg, ug, gg, oT = [res[:, i * 2 * CHUNK:(i + 1) * 2 * CHUNK].rearrange("p (a n) -> p a n", a=2) for i in range(4)]

        bA, bB, bC, bS, bT, bP = 0, 1, 2, 3, 5, 7
        store = [[kept_exps[:, i] for i in range(4)],
                 [kept_exps[:, i] for i in range(4, 8)],
                 [xin[:, i, :, :].rearrange("p t c -> p (t c)") for i in range(4)],
                 [c3[:, :], th[:, :], ah[:, :], rden[:, :]]]
        first_bank = [PAIR["e", 1, 2 * KT - 1], PAIR["e", 1, 2 * KT - 1] + 1, PAIR["z", 1, 1], PAIR["z", 1, 1] + 1]
        first_elu = [ah[:, :], rden[:, :], kept_exps[:, 0], kept_exps[:, 1]]
        c1_bank = {0: bT, 1: bT + 1}

        conv_loaded, w_loaded = sem("conv_loaded"), sem("w_loaded")
        pool_set, dve_set, act_set = sem("pool_set"), sem("dve_set"), sem("act_set")
        out_sent = sem("out_sent")
        arrived, go = sem("arrived"), sem("go")
        passed = sem("passed")
        names = """out_left first_transposed first_min first_exp first_elu first_high first_low first_res pads x_transposed elu_min elu_exp res_ready elu_read xeh_ready xe_ready c1_mm c1h_ready c1_ready
            gate_mm value_mm th_ready ah_ready c3_ready c3h_ready c3l_ready res_added qk_mm qh_ready kh_ready q_ready k_ready
            s_filled s_drained v_ready max_ready mrow_h mrow_ready t_filled exp_done pv_done att_h att_l
            den_mm mh_mm den_added den_inv z_copied z_ready y_ready m_step
            a_mm xt_act xt_dve qt_mm qth_ready sq_ready qtl_ready rd_ready rdrow_mm xn_ready xnh_ready xnl_pool xnl_dve
            e_mm kept p_ready ph_ready pl_ready ap_mm stash_act stash_dve gz_step zrow_mm zrow_copied scaled_ready x_pool x_dve
            p_mm pth_ready p_sum rs_mm rs_ready lr_mm gt_mm sg_ready u_ready g_ready gh_ready gl_ready o_mm ot_ready ot_mm z2_ready
            st_ready eps_ready rstd_ready centred_ready ln_ready neg_max_ready""".split()
        S = {n: sem(n) for n in names}
        x_loaded = [sem(f"x_loaded{i}") for i in range(4)]
        first_loaded = [sem(f"first_loaded{i}") for i in range(4)]
        loop_sems = list(S.values()) + x_loaded + first_loaded
        assert [s_.num for s_ in loop_sems] == list(range(loop_sems[0].num, loop_sems[0].num + len(loop_sems)))

        block = ctx.enter_context(nc.Block())

        @block.sync
        def _(sp):
            n = 0
            def load(dst, src):
                nonlocal n
                sp.dma_start(dst, src).then_inc(w_loaded, 16)
                n += 16
            stage1 = res[:, 0:TAPS * C]
            stage2 = prob[:, :, :].rearrange("p a n -> p (a n)")[:, 0:TAPS * 2 * C]

            def chunks(b):
                return x[b].rearrange("r w c -> (r w) c").rearrange("(k t p) c -> k p t c", t=TILES, p=P)
            sp.dma_start(stage1.rearrange("p (t o) -> p t o", o=C), W1.rearrange("a b i o -> i (a b) o")).then_inc(conv_loaded, 16)
            sp.dma_start(stage2.rearrange("p (t o) -> p t o", o=2 * C), W2.rearrange("a b i o -> i (a b) o")).then_inc(conv_loaded, 16)
            for c in range(4):
                sp.dma_start(xin[:, c], chunks(0)[c]).then_inc(first_loaded[c], 16)
            sp.wait_ge(pool_set, POOL_CLEARED)
            sq = res[:, TAPS * C:TAPS * C + 7 * C].rearrange("p (s o) -> p s o", o=C)
            for g in range(4):
                load(sq[:, 0, g * G32 + 1:g * G32 + 1 + DQK], Wq)
                load(sq[:, 1, g * G32 + 1:g * G32 + 1 + DQK], Wk)
                load(bias[g * G32 + 1:g * G32 + 1 + DQK, QB:QB + 1], bq.rearrange("(d o) -> d o", o=1))
                load(bias[g * G32 + 1:g * G32 + 1 + DQK, KB:KB + 1], bk.rearrange("(d o) -> d o", o=1))
                load(planes_w3(res)[g * G32:g * G32 + DV], W3.rearrange("(h d) o -> d h o", d=DV))
            load(sq[:, 3, :], Wleft)
            load(sq[:, 4, :], Wgate)
            load(sq[:, 5, :], Wout)
            load(sq[:, 6, :], Weq)
            load(wv32[:, 0:DV], Wv)
            load(wright[:], Wright)
            for col, v in ((B1, b1), (B3, b3), (BL, bleft), (BG, bgate), (BR, bright), (BO, bout), (BE, beq)):
                load(bias[:, col:col + 1], v.rearrange("(c o) -> c o", o=1))
            load(bias[:, B2A:B2A + 1], b2[0:C].rearrange("(c o) -> c o", o=1))
            load(bias[:, B2B:B2B + 1], b2[C:2 * C].rearrange("(c o) -> c o", o=1))
            load(bias[:, G1:G1 + 1], bcast(gamma1, P, 1))
            load(bias[:, G3:G3 + 1], bcast(gamma3, P, 1))
            load(bv_rep[:], bass.AP(tensor=bv.tensor, offset=bv.offset, ap=[[0, P], [0, TILES], [1, DV]]))
            load(ln_s[:], bcast(ln_scale, P, C))
            load(ln_b[:], bcast(ln_bias, P, C))
            assert n == W_LOADS, n
            sp.sem_inc(out_sent, OUT_SENT)
            sp.sem_inc(arrived, 1)
            sp.wait_ge(go, 1)
            with sp.Fori(0, B) as b:
                for c in range(4, CHUNKS):
                    sp.dma_start(xin[:, c - 4], chunks(b)[c]).then_inc(x_loaded[c - 4], 16)
                sp.wait_ge(out_sent, OUT_SENT * b + OUT_SENT)
                sp.sem_inc(S["out_left"], 1)
                for c in range(4):
                    if c == 0:
                        sp.wait_ge(S["e_mm"], 3 * KT + KT // 2)
                    sp.dma_start(xin[:, c], chunks((b + 1) % B)[c]).then_inc(first_loaded[c], 16)
                ob = out[b].rearrange("c (g h r) k -> g r c h k", r=R, h=8)
                for g in range(4):
                    sp.wait_ge(S["x_pool"], 4 + g + 1)
                    sp.wait_ge(S["x_dve"], 4 + g + 1)
                    for r1 in range(R):
                        src = XT[r1:P:R, g * 8 * C:(g + 1) * 8 * C].rearrange("p (h k) -> p h k", k=C)
                        sp.dma_start(ob[g, r1], src).then_inc(out_sent, 16)
                sp.sem_inc(arrived, 1)
                sp.wait_ge(go, b + 2)
                sp.sem_inc(passed, 1)
            sp.wait_ge(out_sent, OUT_SENT * (B + 1))

        @block.tensor
        def _(pe):
            mm, tr = nc.tensor.matmul, nc.tensor.transpose

            def three(o, wh, wl, xh, xl, start, stop):
                mm(o, wh, xh, start=start, stop=False)
                mm(o, wh, xl, start=False, stop=False)
                return mm(o, wl, xh, start=False, stop=stop)

            def spread(o, v):
                for k in range(TILES):
                    last = tr(o[:, k * P:(k + 1) * P], v[:, k:k + 1].to_broadcast([P, P]), ident[:])
                return last

            def first_transpose(c, ahead):
                pe.wait_ge(first_loaded[c], 16)
                if ahead and c == 0:
                    pe.wait_ge(S["p_ready"], 4 * KT)
                elif ahead and c == 2:
                    pe.wait_ge(S["zrow_copied"], 4)
                for t in range(TILES):
                    last = tr(psum[:, first_bank[c], t * P:(t + 1) * P], xin[:, c, t, :], ident[:])
                last.then_inc(S["first_transposed"], 1)

            def transpose_x(c):
                pe.wait_ge(x_loaded[c - 4], 16)
                if c == 4:
                    pe.wait_ge(S["first_res"], 4)
                if c > 4:
                    pe.wait_ge(S["c1_ready"], c - 2)
                for t in range(TILES):
                    last = tr(psum[:, bA, t * P:(t + 1) * P], xin[:, c - 4, t, :], ident[:])
                last.then_inc(S["x_transposed"], 1)

            def conv1_tap(c, tap):
                bank = c1_bank.get(c, bA)
                if tap == 0:
                    below = min(c + 1, CHUNKS - 1)
                    if below >= 4:
                        pe.wait_ge(S["xe_ready"], below - 3)
                    if c >= 2:
                        pe.wait_ge(S["elu_read"], min(c + 3, CHUNKS) - 4)
                        if c >= 3:
                            pe.wait_ge(S["c1_ready"], c)
                dy, dx = divmod(tap, 3)
                r0 = c * ROWS + dy
                last = three(psum[:, bank, :], w1h[:, tap, :], w1l[:, tap, :],
                             xeh[:, r0:r0 + ROWS, dx:dx + W], xel[:, r0:r0 + ROWS, dx:dx + W], tap == 0, tap == TAPS - 1)
                if tap == TAPS - 1:
                    last.then_inc(S["c1_mm"], 1)

            def conv2_tap(c, tap, gate):
                bank = bB if gate else bC
                if tap == 0 and gate:
                    pe.wait_ge(S["c1_ready"], min(c + 2, CHUNKS))
                    if c >= 1:
                        pe.wait_ge(S["q_ready"], c)
                if tap == 0 and not gate and c >= 1:
                    pe.wait_ge(S["k_ready"], c)
                dy, dx = divmod(tap, 3)
                r0 = c * ROWS + dy
                o = C if gate else 0
                last = three(psum[:, bank, :], w2h[:, tap, o:o + C], w2l[:, tap, o:o + C],
                             c1h[:, r0:r0 + ROWS, dx:dx + W], c1l[:, r0:r0 + ROWS, dx:dx + W], tap == 0, tap == TAPS - 1)
                if tap == TAPS - 1:
                    last.then_inc(S["gate_mm" if gate else "value_mm"], 1)

            def project(c):
                pe.wait_ge(S["c3h_ready"], c + 1)
                pe.wait_ge(S["c3l_ready"], c + 1)
                three(psum[:, bB, :], sqh[:, Q_, :], sql[:, Q_, :], c3h[:], c3l[:], True, True)
                three(psum[:, bC, :], sqh[:, K_, :], sql[:, K_, :], c3h[:], c3l[:], True, True).then_inc(S["qk_mm"], 1)

            def project_values(c):
                i = tiles_base(c) + (4 * c if valid(c - 1) else 0)
                if i >= 2:
                    pe.wait_ge(S["s_drained"], i - 1)
                for t in range(TILES):
                    last = mm(psum[:, bS + i % 2, t * G32:(t + 1) * G32], c3[:, t * P:(t + 1) * P], wv32[:], start=True, stop=True)
                last.then_inc(S["s_filled"], 1)

            def score_tile(c, i):
                t, kc = divmod(i, c + 1)
                n = tiles_base(c + 1) + i
                if i == 0:
                    pe.wait_ge(S["q_ready"], c + 1)
                    pe.wait_ge(S["k_ready"], c + 1)
                if n >= 2:
                    pe.wait_ge(S["s_drained"], n - 1)
                bank = bS + n % 2
                diag = kc == c
                width = (t + 1) * P if diag else CHUNK
                if diag:
                    mm(psum[:, bank, t * P:width], identb[:], mask_q[:], start=True, stop=False, skip_group_check=True)
                mm(psum[:, bank, 0:width], qop[:, c % 3, t * P:(t + 1) * P], kop[:, kc * CHUNK:kc * CHUNK + width],
                   start=not diag, stop=True, skip_group_check=diag).then_inc(S["s_filled"], 1)

            def max_rows(c):
                n = score_base(c + 2)
                pe.wait_ge(S["neg_max_ready"], c + 1)
                pe.wait_ge(S["s_drained"], n - 1)
                spread(psum[:, bS + n % 2, :], mneg[:, 1, :]).then_inc(S["s_filled"], 1)

            def exp_tile(c, j):
                e = exp_base(c) + j
                if j == 0:
                    pe.wait_ge(S["mrow_ready"], c + 1)
                    if c >= 1:
                        pe.wait_ge(S["den_added"], c)
                elif j == 1:
                    if c >= 1:
                        pe.wait_ge(S["z_copied"], c)
                else:
                    pe.wait_ge(S["exp_done"], e - 1)
                bank = bT + j % 2
                diag = j >= TILES * c
                last = mm(psum[:, bank, :], kop[:, j * P:(j + 1) * P], qop[:, c % 3, :], start=True, stop=not diag)
                if diag:
                    r = j - TILES * c
                    o = (TILES - 1 - r) * P
                    last = mm(psum[:, bank, :], identb[:], mask_k[:, o:o + CHUNK], start=False, stop=True)
                last.then_inc(S["t_filled"], 1)

            def attend(c, g):
                if g == 0:
                    pe.wait_ge(S["v_ready"], c + 1)
                    if c >= 1:
                        pe.wait_ge(S["att_l"], c)
                pe.wait_ge(S["exp_done"], exp_base(c) + 4 * g + 4)
                for q in range(4):
                    j = 4 * g + q
                    last = mm(psum[q * G32:(q + 1) * G32, bP, :], vaug[:, j, :], prob[:, (exp_base(c) + j) % 8, :],
                              start=g == 0, stop=g == c, tile_position=(0, q * G32))
                last.then_inc(S["pv_done"], 1)

            def attention_out(c):
                pe.wait_ge(S["att_l"], c + 1)
                pe.wait_ge(S["exp_done"], exp_base(c + 1))
                mm(psum[:, bT, :], sel_den[:], atth[:], start=True, stop=False)
                mm(psum[:, bT, :], sel_den[:], attl[:], start=False, stop=True).then_inc(S["den_mm"], 1)
                three(psum[:, bT + 1, :], sqh[:, M_, :], sql[:, M_, :], atth[:], attl[:], True, True).then_inc(S["mh_mm"], 1)

            def pair_free(item):
                kind, y, i = BEFORE[item] or (None, 0, 0)
                if kind == "e":
                    pe.wait_ge(S["p_ready"], 2 * KT * y + i + 1)
                elif kind == "a":
                    pe.wait_ge(S["xt_act"], i + 1)
                    pe.wait_ge(S["xt_dve"], i + 1)
                elif kind == "qt":
                    pe.wait_ge(S["qtl_ready"], 8 * y + 2 * i + 2)
                elif kind == "rd":
                    pe.wait_ge(S["xn_ready"], 8 * (y + 1))
                elif kind == "z" and i == 0:
                    pe.wait_ge(S["scaled_ready"], 8 * y + 4)
                elif kind == "z":
                    pe.wait_ge(S["zrow_copied"], 2 * (y + 1))
                elif kind == "pt":
                    pe.wait_ge(S["p_sum"], 2 * i + 2)
                elif kind == "lg":
                    pe.wait_ge(S["u_ready"], i + 1)
                    pe.wait_ge(S["sg_ready"], i + 1)
                return PAIR[item]

            def token_tiles(i):
                pair = pair_free(("a", 0, i))
                for g in (2 * i, 2 * i + 1):
                    for h in range(H2G):
                        src = res[:, (H2G * g + h) * P:(H2G * g + h + 1) * P]
                        last = tr(psum[:, pair + g % 2, h * P:(h + 1) * P], src, ident[:])
                    last.then_inc(S["a_mm"], 1)

            def positions(y, kk, bank):
                if y == 0:
                    pe.wait_ge(S["xt_dve" if kk % 2 else "xt_act"], kk // 2 + 1)
                else:
                    pe.wait_ge(S["ln_ready"], kk + 1)
                for k in range(2):
                    for r2 in range(R):
                        last = tr(psum[:, bank, (2 * k + r2) * P:(2 * k + r2 + 1) * P],
                                  XTv[:, r2, (2 * kk + k) * P:(2 * kk + k + 1) * P], ident[:])
                last.then_inc(S["qt_mm"], 1)

            def inverse_norms(y, q0, bank):
                pe.wait_ge(S["rd_ready"], 2 * y + q0 // 2 + 1)
                if q0 == 0:
                    pe.wait_ge(S["qtl_ready"], 8 * y + 4)
                for q in (q0, q0 + 1):
                    spread(psum[:, bank + q % 2, :], rd[:, 4 * q:4 * q + 4]).then_inc(S["rdrow_mm"], 1)

            def scales(y, i):
                pe.wait_ge(S["gz_step"], 4 * (2 * y + i) + 4)
                pair = pair_free(("z", y, i))
                for q in range(2):
                    spread(psum[:, pair + q, :], gz[:, 8 * i + 4 * q:8 * i + 4 * q + 4]).then_inc(S["zrow_mm"], 1)

            def pair_transposed(i):
                pair = pair_free(("pt", 0, i))
                pe.wait_ge(S["x_pool"], i + 1)
                pe.wait_ge(S["x_dve"], i + 1)
                for g in (2 * i, 2 * i + 1):
                    for h in range(H2G):
                        last = tr(psum[:, pair + g % 2, h * P:(h + 1) * P], XT[:, (H2G * g + h) * C:(H2G * g + h + 1) * C], ident[:])
                    last.then_inc(S["p_mm"], 1)

            def spatial_layer(y):
                for ih in range(2):
                    for j in range(KT + 2):
                        if j < KT:
                            energy(y, ih, j)
                            kind, i = EXTRA.get((ih, j), (None, 0))
                            if kind == "qt":
                                pair = pair_free(("qt", y, i))
                                positions(y, 2 * i, pair)
                                positions(y, 2 * i + 1, pair + 1)
                            elif kind == "rd":
                                inverse_norms(y, 2, pair_free(("rd", y, 1)))
                            elif kind == "z":
                                scales(y, 0)
                            elif kind == "pt" and y == 0:
                                pair_transposed(i)
                        elif ih == 1 and j == KT + 1:
                            scales(y, 1)
                            if y == 1:
                                first_transpose(0, True)
                                first_transpose(1, True)
                        if j >= 2:
                            apply(y, ih, j - 2)

            def energy(y, ih, j):
                pair = pair_free(("e", y, KT * ih + j))
                if ih == 0 and j in (0, KT // 2):
                    pe.wait_ge(S["xnl_pool"], 4 * y + (4 if j else 2))
                    pe.wait_ge(S["xnl_dve"], 4 * y + (4 if j else 2))
                for q in range(2):
                    J, Q = j // TILES, 2 * ih + q
                    if (J, Q) in MIRRORED:
                        src_half, src_last = J // 2, TILES * Q + TILES - 1
                        pe.wait_ge(S["kept"], kept_before(y, src_half, src_last + 1))
                        for t in range(TILES):
                            last = tr(psum[:, pair + q, t * P:(t + 1) * P], store[KEPT[Q, J]][t][:, (j % TILES) * P:(j % TILES + 1) * P], ident[:])
                        continue
                    i0 = ih * IHALF + q * CHUNK
                    for r in range(R):
                        last = three(psum[:, pair + q, :], XNH[:, r, j * P:(j + 1) * P], XNL[:, r, j * P:(j + 1) * P],
                                     XNH[:, r, i0:i0 + CHUNK], XNL[:, r, i0:i0 + CHUNK], r == 0, r == 1)
                last.then_inc(S["e_mm"], 1)

            def apply(y, ih, j):
                n = 2 * KT * y + KT * ih + j
                pe.wait_ge(S["ph_ready"], n + 1)
                pe.wait_ge(S["pl_ready"], n + 1)
                if j == 0 and ih == 0 and y == 1:
                    pe.wait_ge(S["z2_ready"], GROUPS)
                    pe.wait_ge(S["ot_ready"], GROUPS)
                if j == 0 and ih == 1:
                    pe.wait_ge(S["stash_act"], 2 * y + 2)
                    pe.wait_ge(S["stash_dve"], 2 * y + 2)
                for r2 in range(R):
                    for q in range(2):
                        i0 = q * CHUNK
                        last = three(psum[:, 4 + 2 * r2 + q, :], QTh[:, j, r2 * P:(r2 + 1) * P], QTl[:, j, r2 * P:(r2 + 1) * P],
                                     Ph[:, j % 2, i0:i0 + CHUNK], Pl[:, j % 2, i0:i0 + CHUNK], j == 0, j == KT - 1)
                    if (y, ih, j, r2) == (1, 1, KT - 1, 0):
                        first_transpose(2, True)
                        first_transpose(3, True)
                last.then_inc(S["ap_mm"], 1)

            pe.wait_ge(pool_set, POOL_SET)
            for c in range(4):
                first_transpose(c, False)
            pe.wait_ge(act_set, ACT_SET)
            pe.wait_ge(dve_set, DVE_SET)
            pe.sem_inc(arrived, 1)
            pe.wait_ge(go, 1)
            with pe.Fori(0, B) as b:
                for c in range(2):
                    for tap in range(TAPS):
                        conv1_tap(c, tap)
                for s in range(CHUNKS + 3):
                    cm, ce, cy = s - 1, s - 2, s - 3
                    for u in range(STEPS):
                        if u == 0:
                            if s + 4 < CHUNKS:
                                transpose_x(s + 4)
                            if valid(ce):
                                max_rows(ce)
                        if u == 1 and valid(cy):
                            attention_out(cy)
                        if s < CHUNKS:
                            if u < 2 * TAPS:
                                conv2_tap(s, u % TAPS, u < TAPS)
                            elif s + 2 < CHUNKS:
                                conv1_tap(s + 2, u - 2 * TAPS)
                        if valid(cm):
                            for i in share(4 * s, u, STEPS, 2):
                                score_tile(cm, i)
                        if valid(ce):
                            for j in share(4 * (ce + 1), u, STEPS, 3):
                                if j >= 6 and j % 4 == 2:
                                    attend(ce, (j - 6) // 4)
                                exp_tile(ce, j)
                        if u == 23 and s < CHUNKS:
                            project(s)
                    if s < CHUNKS:
                        project_values(s)
                    if valid(ce):
                        attend(ce, ce)
                pe.wait_ge(S["y_ready"], CHUNKS - 1 + TILES)
                token_tiles(0)
                token_tiles(1)
                positions(0, 0, 4)
                positions(0, 1, 5)
                token_tiles(2)
                positions(0, 2, 6)
                positions(0, 3, 7)
                token_tiles(3)
                inverse_norms(0, 0, 4)
                spatial_layer(0)
                pair_transposed(2)
                pair_transposed(3)
                for s in range(GROUPS + 3):
                    if s < GROUPS:
                        p_ = slice(s * CHUNK, (s + 1) * CHUNK)
                        pair = pair_free(("lg", 0, s))
                        pe.wait_ge(S["p_sum"], s + 1)
                        three(psum[:, pair, :], sqh[:, L_, :], sql[:, L_, :], TH[:, p_], TL[:, p_], True, True).then_inc(S["lr_mm"], 1)
                        three(psum[:, pair + 1, :], sqh[:, G_, :], sql[:, G_, :], TH[:, p_], TL[:, p_], True, True).then_inc(S["gt_mm"], 1)
                    if s == 0:
                        pe.wait_ge(S["rs_ready"], 1)
                        mm(psum[:, 4, 0:H], wright[:], rsum[:], start=True, stop=True).then_inc(S["rs_mm"], 1)
                    f = s - 2
                    if valid(f):
                        pe.wait_ge(S["gl_ready"], f + 1)
                        if f >= 1:
                            pe.wait_ge(S["ot_ready"], f)
                        else:
                            pe.wait_ge(S["rs_ready"], 3)
                        three(psum[:, 4, :], sqh[:, O_, :], sql[:, O_, :], Gh[:, f % 2], Gl[:, f % 2], True, True).then_inc(S["o_mm"], 1)
                    f = s - 3
                    if valid(f):
                        pe.wait_ge(S["ot_ready"], f + 1)
                        if f >= 1:
                            pe.wait_ge(S["z2_ready"], f)
                        for h in range(H2G):
                            last = tr(psum[:, 5, h * P:(h + 1) * P], oT[:, f % 2, h * P:(h + 1) * P], ident[:])
                        last.then_inc(S["ot_mm"], 1)
                    kk = s - 5
                    if 0 <= kk < 4:
                        if kk >= 2:
                            pe.wait_ge(S["qtl_ready"], 8 + kk - 1)
                        positions(1, kk, 6 + kk % 2)
                inverse_norms(1, 0, 6)
                spatial_layer(1)
                pe.wait_ge(S["first_transposed"], 4)
                pe.sem_inc(arrived, 1)
                pe.wait_ge(go, b + 2)
                pe.sem_inc(passed, 1)

        @block.scalar
        def _(act):
            a = nc.scalar.activation

            def image(plane, c):
                return plane[:, 1 + c * ROWS:1 + (c + 1) * ROWS, 1:1 + W]

            def rows(t):
                return t.rearrange("p (r w) -> p r w", w=W)

            def first_exps_highs():
                for c in (0, 2):
                    for k in (c, c + 1):
                        act.wait_ge(S["first_min"], k + 1)
                        a(first_elu[k], first_elu[k], ACT.Exp).then_inc(S["first_exp"], 1)
                    for k in (c, c + 1):
                        act.wait_ge(S["first_elu"], k + 1)
                        a(image(xeh, k), rows(first_elu[k]), ACT.Copy).then_inc(S["first_high"], 1)

            def elu_exp(c):
                act.wait_ge(S["elu_min"], c - 3)
                a(ebuf[:, c % 2], ebuf[:, c % 2], ACT.Exp).then_inc(S["elu_exp"], 1)
                a(res_chunk(res, c), split_w(psum[:, bA, :]), ACT.Identity, bias=bias[:, B3:B3 + 1]).then_inc(S["res_ready"], 1)

            def elu_high(c):
                act.wait_ge(S["elu_read"], c - 3)
                a(image(xeh, c), rows(ebuf[:, c % 2]), ACT.Copy).then_inc(S["xeh_ready"], 1)

            def c1_high(c):
                act.wait_ge(S["c1_mm"], c + 1)
                a(image(c1h, c), rows(psum[:, c1_bank.get(c, bA), :]), ACT.Identity, bias=bias[:, B1:B1 + 1]).then_inc(S["c1h_ready"], 1)

            def positions_high(y, kk, bank):
                act.wait_ge(S["qt_mm"], 8 * y + kk + 1)
                src = psum[:, bank, :].rearrange("p (k i) -> p k i", k=2)
                a(QTh[:, 2 * kk:2 * kk + 2, :], src, ACT.Copy).then_inc(S["qth_ready"], 1)
                for k in range(2):
                    n = 16 * y + 2 * kk + k
                    if n >= 4:
                        act.wait_ge(S["sq_ready"], n - 3)
                    a(square[n % 4], src[:, k], ACT.Square, accum_out=d2[:, 2 * kk + k:2 * kk + k + 1]).then_inc(S["sq_ready"], 1)

            def normalised_high(y, n0):
                for n in range(n0, n0 + 4):
                    act.wait_ge(S["xn_ready"], 8 * y + n + 1)
                    a(XNH[:, n % 2, (n // 2) * CHUNK:(n // 2 + 1) * CHUNK], xn[n % 4], ACT.Copy).then_inc(S["xnh_ready"], 1)

            def pair_high(i):
                for g in (2 * i, 2 * i + 1):
                    act.wait_ge(S["p_mm"], g + 1)
                    a(TH[:, g * CHUNK:(g + 1) * CHUNK], psum[:, PAIR[("pt", 0, i)] + g % 2, :], ACT.Copy).then_inc(S["pth_ready"], 1)

            def spatial_layer(y):
                for ih in range(2):
                    for j in range(KT):
                        n = 2 * KT * y + KT * ih + j
                        pair = PAIR[("e", y, KT * ih + j)]
                        act.wait_ge(S["e_mm"], n + 1)
                        if n >= 2:
                            act.wait_ge(S["pl_ready"], n - 1)
                            act.wait_ge(S["kept"], kept_before(*tile_of(n - 1)))
                        mirrored = [(j // TILES, 2 * ih + q) in MIRRORED for q in range(2)]
                        if mirrored[0] == mirrored[1]:
                            a(pexp[:, j % 2], psum[:, pair:pair + 2, :], ACT.Copy if mirrored[0] else ACT.Exp,
                              accum_out=zsum[:, ih, j:j + 1]).then_inc(S["p_ready"], 1)
                        else:
                            a(pexp[:, j % 2, 0:CHUNK], psum[:, pair, :], ACT.Copy, accum_out=zsum[:, 2, j:j + 1])
                            a(pexp[:, j % 2, CHUNK:2 * CHUNK], psum[:, pair + 1, :], ACT.Exp,
                              accum_out=zsum[:, ih, j:j + 1]).then_inc(S["p_ready"], 1)
                        act.wait_ge(S["p_ready"], n + 1)
                        if n >= 2:
                            act.wait_ge(S["ap_mm"], n - 1)
                        a(Ph[:, j % 2], pexp[:, j % 2], ACT.Copy).then_inc(S["ph_ready"], 1)
                        kind, i = EXTRA.get((ih, j), (None, 0))
                        if kind == "qt":
                            for kk in (2 * i, 2 * i + 1):
                                positions_high(y, kk, PAIR[("qt", y, i)] + kk % 2)
                        elif kind == "rd":
                            normalised_high(y, 4)
                        elif kind == "pt" and y == 0:
                            pair_high(i)
                    if ih == 0:
                        act.wait_ge(S["ap_mm"], 2 * KT * y + KT)
                        for q in range(2):
                            a(stash[:, q], psum[:, 4 + q, :], ACT.Copy).then_inc(S["stash_act"], 1)
                for q in range(2):
                    act.wait_ge(S["zrow_mm"], 4 * y + q + 3)
                    a(ebuf[:, q], psum[:, PAIR[("z", y, 1)] + q, :], ACT.Copy).then_inc(S["zrow_copied"], 1)

            act.wait_ge(conv_loaded, 32)
            stage1 = res[:, 0:TAPS * C].rearrange("p (t o) -> p t o", o=C)
            stage2 = prob[:, :, :].rearrange("p a n -> p (a n)")[:, 0:TAPS * 2 * C].rearrange("p (t o) -> p t o", o=2 * C)
            sq = res[:, TAPS * C:TAPS * C + 7 * C].rearrange("p (s o) -> p s o", o=C)
            a(w1h[:], stage1, ACT.Copy).then_inc(act_set, 1)
            a(w2h[:], stage2, ACT.Copy).then_inc(act_set, 1)
            first_exps_highs()
            act.wait_ge(dve_set, DVE_FOLDED)
            a(sqh[:], sq[:, 0:6, :], ACT.Copy).then_inc(act_set, 1)
            a(sel_den[:], sel_den32[:], ACT.Copy).then_inc(act_set, 1)
            act.wait_ge(dve_set, DVE_SET)
            act.sem_inc(arrived, 1)
            act.wait_ge(go, 1)
            with act.Fori(0, B) as b:
                for c in range(4):
                    a(res_chunk(res, c), split_w(psum[:, first_bank[c], :]), ACT.Identity, bias=bias[:, B3:B3 + 1]).then_inc(S["first_res"], 1)
                for c in range(2):
                    c1_high(c)
                for s in range(CHUNKS + 3):
                    ce = s - 2
                    for u in range(STEPS):
                        if valid(ce):
                            for j in share(4 * (ce + 1), u, STEPS, 3):
                                e = exp_base(ce) + j
                                if e == 0:
                                    act.wait_ge(S["out_left"], 1)
                                act.wait_ge(S["t_filled"], e + 1)
                                if e >= 8:
                                    act.wait_ge(S["pv_done"], (e - 8) // 4 + 1)
                                a(prob[:, e % 8], psum[:, bT + j % 2, :], ACT.Exp).then_inc(S["exp_done"], 1)
                        if u == 1 and valid(s - 3):
                            cy = s - 3
                            act.wait_ge(S["mh_mm"], cy + 1)
                            if cy >= 1:
                                act.wait_ge(S["y_ready"], cy)
                            a(zbuf[:], psum[:, bT + 1, :], ACT.Copy).then_inc(S["z_copied"], 1)
                        if u == 1 and s + 4 < CHUNKS:
                            elu_exp(s + 4)
                        if u == 0 and valid(ce):
                            act.wait_ge(S["s_filled"], score_base(s) + 1)
                            bank = bS + score_base(s) % 2
                            for g in (0, 2):
                                a(qop[g * G32:g * G32 + 1, ce % 3, :], psum[g * G32:g * G32 + 1, bank, :], ACT.Copy).then_inc(S["mrow_h"], 1)
                        if u == 5 and s + 4 < CHUNKS:
                            elu_high(s + 4)
                        if s < CHUNKS:
                            if u == 10:
                                act.wait_ge(S["gate_mm"], s + 1)
                                a(th[:], psum[:, bB, :], ACT.Tanh, scale=0.5, bias=bias[:, B2B:B2B + 1]).then_inc(S["th_ready"], 1)
                            if u == 18:
                                act.wait_ge(S["value_mm"], s + 1)
                                a(ah[:], psum[:, bC, :], ACT.Identity, scale=0.5, bias=bias[:, B2A:B2A + 1]).then_inc(S["ah_ready"], 1)
                            if u == 20:
                                act.wait_ge(S["c3_ready"], s + 1)
                                a(c3h[:], c3[:], ACT.Copy).then_inc(S["c3h_ready"], 1)
                            if u == 24:
                                act.wait_ge(S["qk_mm"], s + 1)
                                a(qop[:, s % 3, :], psum[:, bB, :], ACT.Identity, bias=bias[:, QB:QB + 1]).then_inc(S["qh_ready"], 1)
                                a(kop[:, s * CHUNK:(s + 1) * CHUNK], psum[:, bC, :], ACT.Identity, bias=bias[:, KB:KB + 1]).then_inc(S["kh_ready"], 1)
                            if u == 26 and s + 2 < CHUNKS:
                                c1_high(s + 2)
                    if valid(ce):
                        act.wait_ge(S["pv_done"], pv_base(ce + 1))
                        if ce >= 1:
                            act.wait_ge(S["mh_mm"], ce)
                        a(atth[:], psum[:, bP, :], ACT.Copy).then_inc(S["att_h"], 1)
                def token_copy(g):
                    act.wait_ge(S["a_mm"], g + 1)
                    a(XT[:, g * CHUNK:(g + 1) * CHUNK], psum[:, PAIR[("a", 0, g // 2)], :], ACT.Copy).then_inc(S["xt_act"], 1)
                token_copy(0)
                token_copy(2)
                for kk in range(4):
                    positions_high(0, kk, 4 + kk)
                token_copy(4)
                token_copy(6)
                normalised_high(0, 0)
                spatial_layer(0)
                pair_high(2)
                pair_high(3)
                act.wait_ge(S["rs_mm"], 1)
                for r in range(R):
                    a(rs2[:, :, r], psum[:, 4, 0:H], ACT.Identity, scale=0.5, bias=bias[:, BR:BR + 1]).then_inc(S["rs_ready"], 1)
                for s in range(GROUPS + 3):
                    if s < GROUPS:
                        act.wait_ge(S["gt_mm"], s + 1)
                        if s >= 2:
                            act.wait_ge(S["g_ready"], s - 1)
                        a(sg[:, s % 2], psum[:, PAIR[("lg", 0, s)] + 1, :], ACT.Tanh, scale=0.5, bias=bias[:, BG:BG + 1]).then_inc(S["sg_ready"], 1)
                    f = s - 1
                    if valid(f):
                        act.wait_ge(S["g_ready"], f + 1)
                        if f >= 2:
                            act.wait_ge(S["o_mm"], f - 1)
                        a(Gh[:, f % 2], gg[:, f % 2], ACT.Copy).then_inc(S["gh_ready"], 1)
                    f = s - 2
                    if valid(f):
                        act.wait_ge(S["o_mm"], f + 1)
                        if f >= 2:
                            act.wait_ge(S["ot_mm"], f - 1)
                        a(oT[:, f % 2], psum[:, 4, :], ACT.Identity, bias=bias[:, BO:BO + 1]).then_inc(S["ot_ready"], 1)
                    kk = s - 5
                    if 0 <= kk < 4:
                        positions_high(1, kk, 6 + kk % 2)
                normalised_high(1, 0)
                spatial_layer(1)
                first_exps_highs()
                act.wait_ge(S["first_high"], 4)
                act.sem_inc(arrived, 1)
                act.wait_ge(go, b + 2)
                act.sem_inc(passed, 1)

        @block.vector
        def _(dve):
            tt, ts, stt = nc.vector.tensor_tensor, nc.vector.tensor_scalar, nc.vector.scalar_tensor_tensor

            def image(plane, c):
                return plane[:, 1 + c * ROWS:1 + (c + 1) * ROWS, 1:1 + W]

            def rows(t):
                return t.rearrange("p (r w) -> p r w", w=W)

            def first_min(c):
                dve.wait_ge(S["first_transposed"], c + 1)
                ts(first_elu[c], psum[:, first_bank[c], :], 0.0, None, ALU.min).then_inc(S["first_min"], 1)

            def first_elus(*chunks):
                for c in chunks:
                    dve.wait_ge(S["first_exp"], c + 1)
                    stt(first_elu[c], first_elu[c], -1.0, psum[:, first_bank[c], :], ALU.add, ALU.max).then_inc(S["first_elu"], 1)

            def first_low(c):
                dve.wait_ge(S["first_high"], c + 1)
                tt(image(xel, c), rows(first_elu[c]), image(xeh, c).bitcast(F32), ALU.subtract).then_inc(S["first_low"], 1)

            def elu_min(c):
                dve.wait_ge(S["x_transposed"], c - 3)
                if c >= 6:
                    dve.wait_ge(S["xe_ready"], c - 5)
                ts(ebuf[:, c % 2], psum[:, bA, :], 0.0, None, ALU.min).then_inc(S["elu_min"], 1)

            def elu(c):
                dve.wait_ge(S["elu_exp"], c - 3)
                dve.wait_ge(S["res_ready"], c - 3)
                stt(ebuf[:, c % 2], ebuf[:, c % 2], -1.0, psum[:, bA, :], ALU.add, ALU.max).then_inc(S["elu_read"], 1)

            def c1_low(c):
                dve.wait_ge(S["c1h_ready"], c + 1)
                stt(image(c1l, c), rows(psum[:, c1_bank.get(c, bA), :]), bias[:, B1:B1 + 1], image(c1h, c).bitcast(F32),
                    ALU.add, ALU.subtract).then_inc(S["c1_ready"], 1)

            stage1 = res[:, 0:TAPS * C].rearrange("p (t o) -> p t o", o=C)
            stage2 = prob[:, :, :].rearrange("p a n -> p (a n)")[:, 0:TAPS * 2 * C].rearrange("p (t o) -> p t o", o=2 * C)
            sq = res[:, TAPS * C:TAPS * C + 7 * C].rearrange("p (s o) -> p s o", o=C)
            dve.wait_ge(act_set, 1)
            tt(w1l[:], stage1, w1h[:].bitcast(F32), ALU.subtract).then_inc(dve_set, 1)
            for c in range(4):
                first_min(c)
            dve.wait_ge(act_set, 2)
            tt(w2l[:], stage2, w2h[:].bitcast(F32), ALU.subtract).then_inc(dve_set, 1)
            first_elus(0, 1, 2, 3)
            first_low(1)
            first_low(3)
            dve.wait_ge(w_loaded, W_LOADS)
            dve.wait_ge(pool_set, POOL_SET)
            ts(sq[:, 0, :], sq[:, 0, :], 0.25, None, ALU.mult).then_inc(dve_set, 1)
            nc.vector.tensor_reduce(sq[:, 2, :], planes_w3(res).rearrange("p h o -> p o h"), AX.X, ALU.add).then_inc(dve_set, 1)
            tt(sq[:, 3, :], sq[:, 3, :], sq[:, 6, :], ALU.add).then_inc(dve_set, 1)
            tt(bias[:, BL:BL + 1], bias[:, BL:BL + 1], bias[:, BE:BE + 1], ALU.add).then_inc(dve_set, 1)
            ts(bias[:, QB:QB + 1], bias[:, QB:QB + 1], 0.25, None, ALU.mult).then_inc(dve_set, 1)
            for col, k in ((B2A, 0.5), (B2B, 0.5), (BG, 0.5), (BR, 32.0)):
                ts(bias[:, col:col + 1], bias[:, col:col + 1], k, None, ALU.mult).then_inc(dve_set, 1)
            dve.wait_ge(dve_set, 11)
            nc.vector.memset(bias[0:1, KB:KB + 1], 1.0).then_inc(dve_set, 1)
            nc.vector.memset(bias[64:65, KB:KB + 1], 1.0).then_inc(dve_set, 1)
            dve.wait_ge(act_set, 3)
            tt(sql[:], sq[:, 0:6, :], sqh[:].bitcast(F32), ALU.subtract).then_inc(dve_set, 1)
            dve.wait_ge(dve_set, DVE_SET)

            def positions_low(y, kk, bank):
                dve.wait_ge(S["qth_ready"], 8 * y + kk + 1)
                dve.wait_ge(S["sq_ready"], 16 * y + 2 * kk + 2)
                tt(QTl[:, 2 * kk:2 * kk + 2, :], psum[:, bank, :].rearrange("p (k i) -> p k i", k=2),
                   QTh[:, 2 * kk:2 * kk + 2, :].bitcast(F32), ALU.subtract).then_inc(S["qtl_ready"], 1)

            def normalise(y, q0, bank):
                for n in range(2 * q0, 2 * q0 + 4):
                    q = n // 2
                    dve.wait_ge(S["rdrow_mm"], 4 * y + q + 1)
                    tt(xn[n % 4], XTv[:, n % 2, q * CHUNK:(q + 1) * CHUNK], psum[:, bank + q % 2, :], ALU.mult).then_inc(S["xn_ready"], 1)
                for n in (2 * q0 + 1, 2 * q0 + 3):
                    dve.wait_ge(S["xnh_ready"], 8 * y + n + 1)
                    xs = slice((n // 2) * CHUNK, (n // 2 + 1) * CHUNK)
                    tt(XNL[:, 1, xs], xn[n % 4], XNH[:, 1, xs].bitcast(F32), ALU.subtract).then_inc(S["xnl_dve"], 1)

            def scale_factors(y, i, gcol):
                n = 4 * (2 * y + i)
                gz_ = gz[:, 8 * i:8 * i + 8]
                dve.wait_ge(S["p_ready"], 2 * KT * y + KT + 8 * (i + 1))
                tt(gz_, zsum[:, 0, 8 * i:8 * i + 8], zsum[:, 1, 8 * i:8 * i + 8], ALU.add).then_inc(S["gz_step"], 1)
                dve.wait_ge(S["gz_step"], n + 1)
                tt(gz_, gz_, zsum[:, 2, 8 * i:8 * i + 8], ALU.add).then_inc(S["gz_step"], 1)
                dve.wait_ge(S["gz_step"], n + 2)
                nc.vector.reciprocal(gz_, gz_).then_inc(S["gz_step"], 1)
                dve.wait_ge(S["gz_step"], n + 3)
                ts(gz_, gz_, bias[:, gcol:gcol + 1], None, ALU.mult).then_inc(S["gz_step"], 1)

            def pair_low(i):
                for g in (2 * i, 2 * i + 1):
                    dve.wait_ge(S["pth_ready"], g + 1)
                    gs = slice(g * CHUNK, (g + 1) * CHUNK)
                    src = psum[:, PAIR[("pt", 0, i)] + g % 2, :]
                    tt(TL[:, gs], src, TH[:, gs].bitcast(F32), ALU.subtract)
                    nc.vector.tensor_reduce(rpart[:, g, :], src.rearrange("p (h c r) -> p c h r", h=H2G, r=R), AX.XY, ALU.add).then_inc(S["p_sum"], 1)

            def spatial_layer(y, gcol):
                for ih in range(2):
                    for j in range(KT):
                        n = 2 * KT * y + KT * ih + j
                        dve.wait_ge(S["ph_ready"], n + 1)
                        tt(Pl[:, j % 2], pexp[:, j % 2], Ph[:, j % 2].bitcast(F32), ALU.subtract).then_inc(S["pl_ready"], 1)
                        kind, i = EXTRA.get((ih, j), (None, 0))
                        if kind == "qt":
                            for kk in (2 * i, 2 * i + 1):
                                positions_low(y, kk, PAIR[("qt", y, i)] + kk % 2)
                        elif kind == "rd":
                            normalise(y, 2, PAIR[("rd", y, 1)])
                        elif kind == "z":
                            for q in range(2):
                                dve.wait_ge(S["zrow_mm"], 4 * y + q + 1)
                                for r2 in range(R):
                                    t = stash[:, 2 * r2 + q]
                                    tt(t, t, psum[:, PAIR[("z", y, 0)] + q, :], ALU.mult).then_inc(S["scaled_ready"], 1)
                            for q in range(2):
                                dve.wait_ge(S["scaled_ready"], 8 * y + 2 * q + 2)
                                xv = XTv[:, 1, q * CHUNK:(q + 1) * CHUNK]
                                tt(xv, stash[:, 2 + q], xv, ALU.add).then_inc(S["x_dve"], 1)
                        elif kind == "pt" and y == 0:
                            pair_low(i)
                        if (ih, j) == (1, 7):
                            scale_factors(y, 0, gcol)
                    if ih == 0:
                        dve.wait_ge(S["ap_mm"], 2 * KT * y + KT)
                        for q in range(2, 4):
                            nc.vector.tensor_copy(stash[:, q], psum[:, 4 + q, :]).then_inc(S["stash_dve"], 1)
                scale_factors(y, 1, gcol)
                if y == 1:
                    first_min(0)
                    first_min(1)
                    first_elus(0, 1)
                    first_min(2)
                    first_min(3)
                    first_low(1)
                    first_elus(2, 3)
                dve.wait_ge(S["pl_ready"], 2 * KT * (y + 1))
                dve.wait_ge(S["ap_mm"], 2 * KT * (y + 1))
                for q in range(2, 4):
                    dve.wait_ge(S["zrow_copied"], 2 * y + q - 1)
                    for r2 in range(R):
                        tt(scaled[:, 2 * r2 + q - 2], psum[:, 4 + 2 * r2 + q - 2, :], ebuf[:, q - 2], ALU.mult).then_inc(S["scaled_ready"], 1)
                    dve.wait_ge(S["scaled_ready"], 8 * y + 2 * q + 2)
                    xv = XTv[:, 1, q * CHUNK:(q + 1) * CHUNK]
                    tt(xv, scaled[:, q], xv, ALU.add).then_inc(S["x_dve"], 1)

            dve.wait_ge(S["first_low"], 2)
            dve.sem_inc(arrived, 1)
            dve.wait_ge(go, 1)
            with dve.Fori(0, B) as b:
                for c in range(2):
                    c1_low(c)
                for s in range(CHUNKS + 3):
                    cm, ce, cy = s - 1, s - 2, s - 3
                    for u in range(STEPS):
                        if u == 0 and valid(ce):
                            dve.wait_ge(S["mrow_h"], 2 * ce + 2)
                            bank = bS + score_base(s) % 2
                            tt(qop[64:65, ce % 3, :], psum[64:65, bank, :], qop[64:65, ce % 3, :].bitcast(F32), ALU.subtract).then_inc(S["mrow_ready"], 1)
                            dve.wait_ge(S["mrow_ready"], ce + 1)
                            dve.sem_inc(S["s_drained"], 1)
                        if valid(cm):
                            for i in share(4 * s, u, STEPS, 2):
                                t, kc = divmod(i, cm + 1)
                                n = tiles_base(s) + i
                                width = (t + 1) * P if kc == cm else CHUNK
                                dve.wait_ge(S["s_filled"], n + 1)
                                if i == 0 and cm >= 1:
                                    dve.wait_ge(S["max_ready"], cm)
                                nc.vector.tensor_reduce(mpart[:, t, kc:kc + 1], psum[:, bS + n % 2, 0:width], AX.X, ALU.max).then_inc(S["s_drained"], 1)
                        if valid(cy):
                            if u == 1:
                                dve.wait_ge(S["den_mm"], cy + 1)
                                if cy >= 1:
                                    dve.wait_ge(S["z_ready"], cy)
                                ts(rden[:], psum[:, bT, :], 1e-10, None, ALU.add).then_inc(S["den_added"], 1)
                            if 2 <= u < 2 + TILES:
                                if u == 2:
                                    dve.wait_ge(S["den_added"], cy + 1)
                                piece = rden[:, (u - 2) * P:(u - 1) * P]
                                nc.vector.reciprocal(piece, piece).then_inc(S["den_inv"], 1)
                                if cy == CHUNKS - 1:
                                    if u == 2:
                                        dve.wait_ge(S["z_copied"], CHUNKS)
                                    dve.wait_ge(S["den_inv"], TILES * cy + u - 1)
                                    zp = zbuf[:, (u - 2) * P:(u - 1) * P]
                                    tt(zp, zp, piece, ALU.mult).then_inc(S["z_ready"], 1)
                            if u == 2 + TILES and cy < CHUNKS - 1:
                                dve.wait_ge(S["den_inv"], TILES * (cy + 1))
                                dve.wait_ge(S["z_copied"], cy + 1)
                                tt(zbuf[:], zbuf[:], rden[:], ALU.mult).then_inc(S["z_ready"], 1)
                        if u == 0 and s + 4 < CHUNKS:
                            elu_min(s + 4)
                        if u == 4 and s + 4 < CHUNKS:
                            elu(s + 4)
                        if s < CHUNKS:
                            if u == 19:
                                dve.wait_ge(S["th_ready"], s + 1)
                                dve.wait_ge(S["ah_ready"], s + 1)
                                if s >= 1:
                                    dve.wait_ge(S["res_added"], s)
                                    dve.wait_ge(S["s_filled"], score_base(s))
                                stt(c3[:], th[:], 1.0, ah[:], ALU.add, ALU.mult).then_inc(S["c3_ready"], 1)
                            if u == 25:
                                dve.wait_ge(S["qh_ready"], s + 1)
                                stt(qop[64:128, s % 3, :], psum[64:128, bB, :], bias[64:128, QB:QB + 1], qop[64:128, s % 3, :].bitcast(F32),
                                    ALU.add, ALU.subtract).then_inc(S["q_ready"], 1)
                                dve.wait_ge(S["kh_ready"], s + 1)
                                for g in (1, 3):
                                    k_ = kop[g * G32:(g + 1) * G32, s * CHUNK:(s + 1) * CHUNK]
                                    ins = stt(k_, psum[g * G32:(g + 1) * G32, bC, :], bias[g * G32:(g + 1) * G32, KB:KB + 1], k_.bitcast(F32),
                                              ALU.add, ALU.subtract)
                                    ins.then_inc(S["k_ready"], 1) if g == 3 else ins
                            if u == 26 and s + 2 < CHUNKS:
                                c1_low(s + 2)
                    if s < CHUNKS:
                        n = tiles_base(s) + (4 * s if valid(cm) else 0)
                        dve.wait_ge(S["s_filled"], n + 1)
                        src = psum[:, bS + n % 2, 0:TILES * G32].rearrange("p (t d) -> p t d", d=G32)[:, :, 0:DV]
                        tt(vaug[:, s * TILES:(s + 1) * TILES, 0:DV], src, bv_rep[:], ALU.add).then_inc(S["v_ready"], 1)
                        dve.wait_ge(S["v_ready"], s + 1)
                        dve.sem_inc(S["s_drained"], 1)
                    if valid(cm):
                        dve.wait_ge(S["s_drained"], n_drained(s))
                        if cm >= 1:
                            dve.wait_ge(S["s_filled"], score_base(s) + 1)
                        nc.vector.tensor_reduce(mneg[:, 0, :], mpart[:, :, 0:cm + 1], AX.X, ALU.max).then_inc(S["max_ready"], 1)
                        dve.wait_ge(S["max_ready"], cm + 1)
                        ts(mneg[:, 1, :], mneg[:, 0, :], -1.0, 1e9, ALU.mult, ALU.min).then_inc(S["neg_max_ready"], 1)
                    if valid(ce):
                        dve.wait_ge(S["att_h"], ce + 1)
                        tt(attl[:], psum[:, bP, :], atth[:].bitcast(F32), ALU.subtract).then_inc(S["att_l"], 1)
                def token_copy(g):
                    dve.wait_ge(S["a_mm"], g + 1)
                    nc.vector.tensor_copy(XT[:, g * CHUNK:(g + 1) * CHUNK], psum[:, PAIR[("a", 0, g // 2)] + 1, :]).then_inc(S["xt_dve"], 1)
                token_copy(1)
                token_copy(3)
                for kk in range(4):
                    positions_low(0, kk, 4 + kk)
                token_copy(5)
                token_copy(7)
                normalise(0, 0, 4)
                spatial_layer(0, G1)
                pair_low(2)
                pair_low(3)
                dve.wait_ge(S["p_sum"], GROUPS)
                nc.vector.tensor_reduce(rsum[:], rpart[:, :, :].rearrange("p g c -> p c g"), AX.X, ALU.add).then_inc(S["rs_ready"], 1)
                rs_row = bcast_mid(rs2, H2G)
                dve.wait_ge(S["rs_ready"], 3)
                for s in range(GROUPS + 3):
                    if s < GROUPS:
                        dve.wait_ge(S["lr_mm"], s + 1)
                        if s >= 2:
                            dve.wait_ge(S["g_ready"], s - 1)
                        stt(ug[:, s % 2].rearrange("p (h i) -> p h i", h=H2G), psum[:, PAIR[("lg", 0, s)], :].rearrange("p (h i) -> p h i", h=H2G),
                            bias[:, BL:BL + 1], rs_row, ALU.add, ALU.mult).then_inc(S["u_ready"], 1)
                        dve.wait_ge(S["u_ready"], s + 1)
                        dve.wait_ge(S["sg_ready"], s + 1)
                        if s >= 2:
                            dve.wait_ge(S["gl_ready"], s - 1)
                        stt(gg[:, s % 2], sg[:, s % 2], 1.0, ug[:, s % 2], ALU.add, ALU.mult).then_inc(S["g_ready"], 1)
                    kk = s - 5
                    if 0 <= kk < 4:
                        positions_low(1, kk, 6 + kk % 2)
                    if s == GROUPS + 2:
                        normalise(1, 0, 6)
                    f = s - 3
                    if valid(f):
                        dve.wait_ge(S["ot_mm"], f + 1)
                        z = XT[:, f * CHUNK:(f + 1) * CHUNK]
                        tt(z, psum[:, 5, :], z, ALU.add).then_inc(S["z2_ready"], 1)
                        dve.wait_ge(S["z2_ready"], f + 1)
                        for h in range(H2G):
                            ins = nc.vector.bn_stats(st[:, f % 2, h, :], z[:, h * C:(h + 1) * C])
                        ins.then_inc(S["st_ready"], 1)
                        dve.wait_ge(S["st_ready"], 2 * f + 1)
                        if f >= 2:
                            dve.wait_ge(S["eps_ready"], f - 1)
                        for h in range(H2G):
                            ins = nc.vector.bn_aggr(mv[:, f % 2, h, :], st[:, f % 2, h, :])
                        ins.then_inc(S["st_ready"], 1)
                        dve.wait_ge(S["st_ready"], 2 * f + 2)
                        for h in range(H2G):
                            zh = z[:, h * C:(h + 1) * C]
                            ins = stt(zh, zh, mv[:, f % 2, h, 0:1], ln_s[:], ALU.subtract, ALU.mult)
                        ins.then_inc(S["centred_ready"], 1)
                spatial_layer(1, G3)
                first_low(3)
                dve.wait_ge(S["first_low"], 2)
                dve.sem_inc(arrived, 1)
                dve.wait_ge(go, b + 2)
                dve.sem_inc(passed, 1)

        @block.gpsimd
        def _(gp):
            tt, ts, ms, sel = nc.gpsimd.tensor_tensor, nc.gpsimd.tensor_scalar, nc.gpsimd.memset, nc.gpsimd.affine_select
            count = [0]

            def link(ins):
                ins.then_inc(pool_set, 1)
                count[0] += 1

            def hold():
                gp.wait_ge(pool_set, count[0])
            sq = res[:, TAPS * C:TAPS * C + 7 * C]
            link(ms(sq, 0.0))
            link(ms(planes_w3(res), 0.0))
            link(ms(bias[:], 0.0))
            link(ms(wv32[:], 0.0))
            assert count[0] == POOL_CLEARED
            for t in (ident, identb, sel_den32, mask_q, mask_k):
                link(ms(t[:], 0.0))
            link(ms(half[:], -0.5))
            link(ms(zsum[:, 2, :], 0.0))
            link(ms(vaug[:], 0.0))
            hold()
            link(ms(vaug[:, :, DV:DV + 1], 1.0))
            for t in (ident, identb):
                link(sel(out=t[:], in_=t[:], compare_op=ALU.not_equal, fill=1.0, base=0, pattern=[[-1, P]], channel_multiplier=1))
            for g in range(4):
                link(sel(out=sel_den32[:], in_=sel_den32[:], compare_op=ALU.not_equal, fill=1.0, base=-(g * G32 + DV),
                         pattern=[[0, P]], channel_multiplier=1))
                hold()
            link(sel(out=mask_q[:], in_=mask_q[:], compare_op=ALU.is_gt, fill=NEG, base=0, pattern=[[-1, P]], channel_multiplier=1))
            link(sel(out=mask_k[:], in_=mask_k[:], compare_op=ALU.is_gt, fill=NEG, base=-3 * P, pattern=[[1, CHUNK + 3 * P]], channel_multiplier=-1))
            hold()
            assert count[0] == POOL_SET, count[0]

            def image(plane, c):
                return plane[:, 1 + c * ROWS:1 + (c + 1) * ROWS, 1:1 + W]

            def pads(i):
                pl = planes[:, i * IMG:(i + 1) * IMG].bitcast(F32)
                ms(pl[:, 0:WP + 1], 0.0).then_inc(S["pads"], 1)
                ms(pl[:, WP + 1 + W:WP + 1 + W + (H - 1) * WP].rearrange("p (r c) -> p r c", c=WP)[:, :, 0:2], 0.0).then_inc(S["pads"], 1)
                ms(pl[:, (H + 1) * WP - 1:IMG], 0.0).then_inc(S["pads"], 1)

            def first_low(c):
                gp.wait_ge(S["first_high"], c + 1)
                tt(image(xel, c), first_elu[c].rearrange("p (r w) -> p r w", w=W), image(xeh, c).bitcast(F32), ALU.subtract).then_inc(S["pads"], 1)

            def next_batch(k):
                gp.wait_ge(arrived, k)
                gp.sem_inc(passed, 1)
                gp.sem_clear(range(loop_sems[0].num, loop_sems[-1].num + 1))
                gp.sem_inc(go, 1)

            def elu_low(c):
                gp.wait_ge(S["xeh_ready"], c - 3)
                tt(image(xel, c), ebuf[:, c % 2].rearrange("p (r w) -> p r w", w=W), image(xeh, c).bitcast(F32), ALU.subtract).then_inc(S["xe_ready"], 1)

            def inverse_norm(y, i):
                gp.wait_ge(S["sq_ready"], 16 * y + 8 * (i + 1))
                tt(rd[:, 8 * i:8 * i + 8], d2[:, 8 * i:8 * i + 8], half[:, 0:8], ALU.pow).then_inc(S["rd_ready"], 1)

            def normalised_low(y, q0):
                for q in (q0, q0 + 1):
                    gp.wait_ge(S["xnh_ready"], 8 * y + 2 * q + 1)
                    xs = slice(q * CHUNK, (q + 1) * CHUNK)
                    tt(XNL[:, 0, xs], xn[2 * q % 4], XNH[:, 0, xs].bitcast(F32), ALU.subtract).then_inc(S["xnl_pool"], 1)

            def spatial_layer(y):
                for ih in range(2):
                    for j in range(KT):
                        n = 2 * KT * y + KT * ih + j
                        for q in range(2):
                            if (j // TILES, 2 * ih + q) in KEPT:
                                gp.wait_ge(S["p_ready"], n + 1)
                                nc.gpsimd.tensor_copy(store[KEPT[j // TILES, 2 * ih + q]][j % TILES],
                                                      pexp[:, j % 2, q * CHUNK:(q + 1) * CHUNK]).then_inc(S["kept"], 1)
                        if (ih, j) == (0, 3):
                            inverse_norm(y, 1)
                        if (ih, j) == (0, 5):
                            normalised_low(y, 2)
                        if (ih, j) == (1, 9):
                            add_rows(y, 0)
                            add_rows(y, 1)
                if y == 1:
                    gp.wait_ge(S["e_mm"], 4 * KT)
                    pads(0)
                    pads(1)
                    first_low(0)
                    gp.wait_ge(S["ap_mm"], 4 * KT)
                    pads(2)
                    pads(3)
                add_rows(y, 2)
                add_rows(y, 3)

            def add_rows(y, q):
                gp.wait_ge(S["scaled_ready"], 8 * y + 2 * q + 1)
                t = stash[:, q] if q < 2 else scaled[:, q - 2]
                xv = XTv[:, 0, q * CHUNK:(q + 1) * CHUNK]
                tt(xv, t, xv, ALU.add).then_inc(S["x_pool"], 1)

            for i in range(4):
                pads(i)
            first_low(0)
            first_low(2)
            gp.wait_ge(S["pads"], PADS + 2)
            next_batch(4)
            with gp.Fori(0, B) as b:
                for s in range(CHUNKS + 3):
                    cy = s - 3
                    if valid(cy):
                        r_ = res_chunk(res, cy)
                        if cy < CHUNKS - 1:
                            gp.wait_ge(S["z_ready"], cy + 1)
                            tt(r_, split_w(zbuf[:]), r_, ALU.add).then_inc(S["y_ready"], 1)
                        else:
                            for t in range(TILES):
                                gp.wait_ge(S["z_ready"], cy + 1 + t)
                                rows_ = r_[:, 2 * t:2 * t + 2]
                                tt(rows_, split_w(zbuf[:])[:, 2 * t:2 * t + 2], rows_, ALU.add).then_inc(S["y_ready"], 1)
                    if s + 4 < CHUNKS:
                        elu_low(s + 4)
                    if s < CHUNKS:
                        gp.wait_ge(S["c3h_ready"], s + 1)
                        if s >= 1:
                            gp.wait_ge(S["qk_mm"], s)
                        tt(c3l[:], c3[:], c3h[:].bitcast(F32), ALU.subtract).then_inc(S["c3l_ready"], 1)
                        r_ = res_chunk(res, s)
                        gp.wait_ge(S["res_ready" if s >= 4 else "first_res"], s - 3 if s >= 4 else s + 1)
                        tt(r_, r_, split_w(c3[:]), ALU.add).then_inc(S["res_added"], 1)
                inverse_norm(0, 0)
                normalised_low(0, 0)
                spatial_layer(0)
                for s in range(GROUPS + 4):
                    f = s - 1
                    if valid(f):
                        gp.wait_ge(S["gh_ready"], f + 1)
                        if f >= 2:
                            gp.wait_ge(S["o_mm"], f - 1)
                        tt(Gl[:, f % 2], gg[:, f % 2], Gh[:, f % 2].bitcast(F32), ALU.subtract).then_inc(S["gl_ready"], 1)
                    if s == GROUPS + 1:
                        inverse_norm(1, 0)
                    if s == GROUPS + 3:
                        normalised_low(1, 0)
                    f = s - 4
                    if valid(f):
                        gp.wait_ge(S["st_ready"], 2 * f + 2)
                        ts(rstd[:, f % 2], mv[:, f % 2, :, 1], EPS_L, None, ALU.add).then_inc(S["eps_ready"], 1)
                        gp.wait_ge(S["eps_ready"], f + 1)
                        tt(rstd[:, f % 2], rstd[:, f % 2], half[:, 0:1].to_broadcast([P, H2G]), ALU.pow).then_inc(S["rstd_ready"], 1)
                        gp.wait_ge(S["rstd_ready"], f + 1)
                        gp.wait_ge(S["centred_ready"], f + 1)
                        z = XT[:, f * CHUNK:(f + 1) * CHUNK].rearrange("p (h k) -> p h k", k=C)
                        tt(z, z, rstd[:, f % 2].unsqueeze(2).to_broadcast([P, H2G, C]), ALU.mult).then_inc(S["m_step"], 1)
                        gp.wait_ge(S["m_step"], f + 1)
                        tt(z, z, bcast_mid(ln_b, H2G), ALU.add).then_inc(S["ln_ready"], 1)
                spatial_layer(1)
                first_low(2)
                gp.wait_ge(S["pads"], PADS + 2)
                gp.wait_ge(S["x_pool"], 8)
                next_batch(4 * b + 8)


POOL_CLEARED = 4
POOL_SET = 4 + 5 + 3 + 1 + 2 + 4 + 2
ACT_SET = 4
DVE_FOLDED = 13
DVE_SET = 14
PADS = 12
OUT_SENT = 4 * R * 16
W_LOADS = 16 * (5 * 4 + 4 + 2 + 7 + 2 + 2 + 1 + 2)


def n_drained(s):
    return score_base(s + 1)


def res_chunk(res, c):
    return res[:, :].rearrange("p (h c r) -> p c h r", c=H, r=R)[:, c * ROWS:(c + 1) * ROWS]


def split_w(t):
    return t.rearrange("p (c h r) -> p c h r", c=ROWS, r=R)


def planes_w3(res):
    o = TAPS * C + 7 * C
    return res[:, o:o + HEADS * C].rearrange("p (h o) -> p h o", o=C)


def bcast(v, p, n):
    return bass.AP(tensor=v.tensor, offset=v.offset, ap=[[0, p], [1, n]])


def bcast_mid(t, k):
    full = t[:, :, :].rearrange("p c r -> p (c r)") if len(t.shape) == 3 else t[:, :]
    return full.unsqueeze(1).to_broadcast([P, k, P])


_INS = ["x", "L0_conv_W1", "L0_conv_b1", "L0_conv_W2", "L0_conv_b2", "L0_conv_Wq", "L0_conv_bq", "L0_conv_Wk", "L0_conv_bk",
        "L0_conv_Wv", "L0_conv_bv", "L0_conv_W3", "L0_conv_b3", "L1_conv_gamma", "L2_conv_W_left", "L2_conv_b_left",
        "L2_conv_W_right", "L2_conv_b_right", "L2_conv_W_gate", "L2_conv_b_gate", "L2_conv_W_eq", "L2_conv_b_eq",
        "L2_conv_W_out", "L2_conv_b_out", "L2_conv_ln_scale", "L2_conv_ln_bias", "L3_conv_gamma"]


def kernel(**inputs):
    import concourse.bacc as bacc
    from concourse.bass_utils import run_bass_kernel_spmd

    nc = bacc.Bacc("TRN2", target_bir_lowering=False, num_devices=1)
    arrays, args = {}, []
    for name in _INS:
        a = np.ascontiguousarray(inputs[name])
        arrays["in_" + name] = a
        args.append(nc.dram_tensor("in_" + name, a.shape, mybir.dt.from_np(a.dtype), kind="ExternalInput").ap())
    args.append(nc.dram_tensor("out_x", (B, H, W, C), F32, kind="ExternalOutput").ap())
    build_program(nc, *args)
    r = run_bass_kernel_spmd(nc, [arrays], core_ids=[0])
    return r.results[0]["out_x"]
```
